# Optimizing a Trainium2 kernel written in Bass

```python
import numpy as np
import jax
import jax.numpy as jnp

def _softmax(x, axis=-1):
    return jax.nn.softmax(x, axis=axis)

def _gelu(x):
    return jax.nn.gelu(x, approximate=True)

def _silu(x):
    return jax.nn.silu(x)

def _sigmoid(x):
    return jax.nn.sigmoid(x)

def _layernorm(x, axis=-1, eps=1e-05):
    m = jnp.mean(x, axis=axis, keepdims=True)
    v = jnp.var(x, axis=axis, keepdims=True)
    return (x - m) / jnp.sqrt(v + eps)

def _scatter_add(tgt, idx, src, axis=0):
    return tgt.at[idx].add(src)

def _segment_sum(src, seg, n):
    return jax.ops.segment_sum(src, seg, n)
kernel_name = 'mk_conv_attn_hybrid_d2_conv_nhwc768_r4_fec9df'

def setup_inputs(seed: int=0):
    np.random.seed(seed)
    _w = jnp.asarray

    def _rec_inputs():
        import jax
        import jax.numpy as jnp
        _gk = jax.random.key(seed)
        x = -0.0004039 + 1 * jax.random.normal(jax.random.fold_in(_gk, 1), (4, 16, 16, 192), jnp.float32)
        return x
    x = _rec_inputs()

    def _L0_conv_setup():
        import jax, jax.numpy as jnp
        import numpy as np
        N_EXPERTS = 8
        TOP_K = 2
        HIDDEN = 192
        INTER = 512

        def _gelu(h):
            return jax.nn.gelu(h, approximate=False)
        key = jax.random.key(seed)
        ks = jax.random.split(key, 12)
        s_in = 1.0 / np.sqrt(HIDDEN)
        s_mid = 1.0 / np.sqrt(INTER)
        return {'x': jax.random.normal(ks[0], (4, 16, 16, HIDDEN), dtype=jnp.float32), 'gate_w': jax.random.normal(ks[1], (N_EXPERTS, HIDDEN), dtype=jnp.float32), 'fc1_w': jax.random.uniform(ks[2], (N_EXPERTS, INTER, HIDDEN), jnp.float32, -s_in, s_in), 'fc1_b': jax.random.uniform(ks[3], (N_EXPERTS, INTER), jnp.float32, -s_in, s_in), 'fc2_w': jax.random.uniform(ks[4], (N_EXPERTS, HIDDEN, INTER), jnp.float32, -s_mid, s_mid), 'fc2_b': jax.random.uniform(ks[5], (N_EXPERTS, HIDDEN), jnp.float32, -s_mid, s_mid), 'w1_w': jax.random.uniform(ks[6], (INTER, HIDDEN), jnp.float32, -s_in, s_in), 'w1_b': jax.random.uniform(ks[7], (INTER,), jnp.float32, -s_in, s_in), 'w3_w': jax.random.uniform(ks[8], (INTER, HIDDEN), jnp.float32, -s_in, s_in), 'w3_b': jax.random.uniform(ks[9], (INTER,), jnp.float32, -s_in, s_in), 'w2_w': jax.random.uniform(ks[10], (HIDDEN, INTER), jnp.float32, -s_mid, s_mid), 'w2_b': jax.random.uniform(ks[11], (HIDDEN,), jnp.float32, -s_mid, s_mid)}
    _L0_conv_all = _L0_conv_setup()
    _L0_conv_in = {k: v for k, v in _L0_conv_all.items() if k in ('gate_w', 'fc1_w', 'fc1_b', 'fc2_w', 'fc2_b', 'w1_w', 'w1_b', 'w3_w', 'w3_b', 'w2_w', 'w2_b')}
    del _L0_conv_all

    def _L1_attn_setup():
        import jax, jax.numpy as jnp
        import numpy as np
        HIDDEN = 192
        HEADS = 12
        HEAD_DIM = HIDDEN // HEADS
        SCALE = HEAD_DIM ** (-0.5)
        GAMMA = 0.5

        def _spa_mask(N: int, dtype) -> jnp.ndarray:
            NUM = N // 4
            rows = jnp.arange(N) % NUM
            cols = jnp.arange(N) % NUM
            return jnp.where(rows[:, None] == cols[None, :], jnp.asarray(GAMMA, dtype), jnp.asarray(1.0, dtype))
        key = jax.random.key(seed)
        k1, k2, k3, k4 = jax.random.split(key, 4)
        B, N, C = (2, 512, HIDDEN)
        x = jax.random.normal(k1, (B, N, C), dtype=jnp.float32)
        w_qkv = jax.random.normal(k2, (3 * C, C), dtype=jnp.float32) * 0.02
        w_out = jax.random.normal(k3, (C, C), dtype=jnp.float32) * 0.02
        b_out = jax.random.normal(k4, (C,), dtype=jnp.float32) * 0.02
        return {'x': x, 'w_qkv': w_qkv, 'w_out': w_out, 'b_out': b_out}
    _L1_attn_all = _L1_attn_setup()
    _L1_attn_in = {k: v for k, v in _L1_attn_all.items() if k in ('w_qkv', 'w_out', 'b_out')}
    del _L1_attn_all

    def _L1_ffn_setup():
        import jax, jax.numpy as jnp
        import numpy as np
        E = 16
        TOP_K = 2
        C = 192
        I = 384
        B, T = (8, 512)

        def _expert(x, wg_e, wu_e, wd_e):
            return jax.nn.silu(x @ wg_e) * (x @ wu_e) @ wd_e
        key = jax.random.key(seed)
        ks = jax.random.split(key, 9)
        s = 0.02
        return {'x': jax.random.normal(ks[0], (B, T, C), jnp.float32), 'w_gate': jax.random.normal(ks[1], (C, E), jnp.float32) * s, 'expert_bias': jnp.zeros((E,), jnp.float32), 'wg': jax.random.normal(ks[2], (E, C, I), jnp.float32) * s, 'wu': jax.random.normal(ks[3], (E, C, I), jnp.float32) * s, 'wd': jax.random.normal(ks[4], (E, I, C), jnp.float32) * s, 'swg': jax.random.normal(ks[5], (C, I), jnp.float32) * s, 'swu': jax.random.normal(ks[6], (C, I), jnp.float32) * s, 'swd': jax.random.normal(ks[7], (I, C), jnp.float32) * s}
    _L1_ffn_all = _L1_ffn_setup()
    _L1_ffn_in = {k: v for k, v in _L1_ffn_all.items() if k in ('w_gate', 'expert_bias', 'wg', 'wu', 'wd', 'swg', 'swu', 'swd')}
    del _L1_ffn_all
    return {'x': x, 'L0_conv_gate_w': _L0_conv_in['gate_w'], 'L0_conv_fc1_w': _L0_conv_in['fc1_w'], 'L0_conv_fc1_b': _L0_conv_in['fc1_b'], 'L0_conv_fc2_w': _L0_conv_in['fc2_w'], 'L0_conv_fc2_b': _L0_conv_in['fc2_b'], 'L0_conv_w1_w': _L0_conv_in['w1_w'], 'L0_conv_w1_b': _L0_conv_in['w1_b'], 'L0_conv_w3_w': _L0_conv_in['w3_w'], 'L0_conv_w3_b': _L0_conv_in['w3_b'], 'L0_conv_w2_w': _L0_conv_in['w2_w'], 'L0_conv_w2_b': _L0_conv_in['w2_b'], 'L1_attn_w_qkv': _L1_attn_in['w_qkv'], 'L1_attn_w_out': _L1_attn_in['w_out'], 'L1_attn_b_out': _L1_attn_in['b_out'], 'L1_ffn_w_gate': _L1_ffn_in['w_gate'], 'L1_ffn_expert_bias': _L1_ffn_in['expert_bias'], 'L1_ffn_wg': _L1_ffn_in['wg'], 'L1_ffn_wu': _L1_ffn_in['wu'], 'L1_ffn_wd': _L1_ffn_in['wd'], 'L1_ffn_swg': _L1_ffn_in['swg'], 'L1_ffn_swu': _L1_ffn_in['swu'], 'L1_ffn_swd': _L1_ffn_in['swd']}

def reference(x, L0_conv_gate_w, L0_conv_fc1_w, L0_conv_fc1_b, L0_conv_fc2_w, L0_conv_fc2_b, L0_conv_w1_w, L0_conv_w1_b, L0_conv_w3_w, L0_conv_w3_b, L0_conv_w2_w, L0_conv_w2_b, L1_attn_w_qkv, L1_attn_w_out, L1_attn_b_out, L1_ffn_w_gate, L1_ffn_expert_bias, L1_ffn_wg, L1_ffn_wu, L1_ffn_wd, L1_ffn_swg, L1_ffn_swu, L1_ffn_swd):
    import jax
    import jax.numpy as jnp

    def _L0_conv_ref(x, gate_w, fc1_w, fc1_b, fc2_w, fc2_b, w1_w, w1_b, w3_w, w3_b, w2_w, w2_b):
        import jax, jax.numpy as jnp
        import numpy as np
        N_EXPERTS = 8
        TOP_K = 2
        HIDDEN = 192
        INTER = 512

        def _gelu(h):
            return jax.nn.gelu(h, approximate=False)
        B, H, W, C = x.shape
        xf = x.reshape(-1, C)
        scores = jax.nn.softmax(xf @ gate_w.T, axis=-1)
        top_v, top_i = jax.lax.top_k(scores, TOP_K)
        top_v = top_v / jnp.sum(top_v, axis=-1, keepdims=True)
        out = jnp.zeros_like(xf)
        for e in range(N_EXPERTS):
            w_e = jnp.sum(jnp.where(top_i == e, top_v, 0.0), axis=-1)
            h = _gelu(xf @ fc1_w[e].T + fc1_b[e])
            y = h @ fc2_w[e].T + fc2_b[e]
            out = out + w_e[:, None] * y
        shared = _gelu(xf @ w1_w.T + w1_b) * (xf @ w3_w.T + w3_b) @ w2_w.T + w2_b
        return (out + shared).reshape(B, H, W, C)

    def _L1_attn_ref(x, w_qkv, w_out, b_out):
        import jax, jax.numpy as jnp
        import numpy as np
        HIDDEN = 192
        HEADS = 12
        HEAD_DIM = HIDDEN // HEADS
        SCALE = HEAD_DIM ** (-0.5)
        GAMMA = 0.5

        def _spa_mask(N: int, dtype) -> jnp.ndarray:
            NUM = N // 4
            rows = jnp.arange(N) % NUM
            cols = jnp.arange(N) % NUM
            return jnp.where(rows[:, None] == cols[None, :], jnp.asarray(GAMMA, dtype), jnp.asarray(1.0, dtype))
        B, N, C = x.shape
        H, D = (HEADS, HEAD_DIM)
        qkv = jnp.einsum('bnc,fc->bnf', x, w_qkv).reshape(B, N, 3, H, D)
        qkv = jnp.transpose(qkv, (2, 0, 3, 1, 4))
        q, k, v = (qkv[0], qkv[1], qkv[2])
        att = jax.nn.softmax(jnp.einsum('bhxd,bhyd->bhxy', q, k) * SCALE, axis=-1)
        mask = _spa_mask(N, att.dtype)
        att = jax.nn.softmax(att * mask, axis=-1)
        out = jnp.einsum('bhxy,bhyd->bhxd', att, v)
        out = jnp.transpose(out, (0, 2, 1, 3)).reshape(B, N, C)
        return jnp.einsum('bnc,oc->bno', out, w_out) + b_out

    def _L1_ffn_ref(x, w_gate, expert_bias, wg, wu, wd, swg, swu, swd):
        import jax, jax.numpy as jnp
        import numpy as np
        E = 16
        TOP_K = 2
        C = 192
        I = 384
        B, T = (8, 512)

        def _expert(x, wg_e, wu_e, wd_e):
            return jax.nn.silu(x @ wg_e) * (x @ wu_e) @ wd_e
        Bq, Tq, Cq = x.shape
        xf = x.reshape(-1, Cq)
        n_tok = xf.shape[0]
        shared = _expert(xf, swg, swu, swd)
        logits = xf @ w_gate + expert_bias
        probs = jax.nn.softmax(logits, axis=-1)
        topk_p, topk_i = jax.lax.top_k(probs, TOP_K)
        topk_p = topk_p / jnp.sum(topk_p, axis=-1, keepdims=True)
        comb = jnp.zeros((n_tok, E), xf.dtype).at[jnp.arange(n_tok)[:, None], topk_i].add(topk_p)
        routed = jnp.zeros_like(xf)
        for e in range(E):
            routed = routed + comb[:, e:e + 1] * _expert(xf, wg[e], wu[e], wd[e])
        return (shared + routed).reshape(Bq, Tq, Cq)

    def _gn(v, G=32, eps=1e-05):
        B_, H_, W_, C_ = v.shape
        g = v.reshape(B_, H_, W_, G, C_ // G)
        m = jnp.mean(g, axis=(1, 2, 4), keepdims=True)
        s = jnp.var(g, axis=(1, 2, 4), keepdims=True)
        return ((g - m) / jnp.sqrt(s + eps)).reshape(v.shape)

    def _ln_c(v, eps=1e-06):
        m = jnp.mean(v, axis=-1, keepdims=True)
        s = jnp.var(v, axis=-1, keepdims=True)
        return (v - m) / jnp.sqrt(s + eps)

    def _ln_t(v, eps=1e-05):
        m = jnp.mean(v, axis=-1, keepdims=True)
        s = jnp.var(v, axis=-1, keepdims=True)
        return (v - m) / jnp.sqrt(s + eps)

    def _to_tokens(v):
        B_, H_, W_, C_ = v.shape
        return v.reshape(B_, H_ * W_, C_)

    def _from_tokens(t, like):
        return t.reshape(like.shape)
    x = x + _L0_conv_ref(_gn(x), L0_conv_gate_w, L0_conv_fc1_w, L0_conv_fc1_b, L0_conv_fc2_w, L0_conv_fc2_b, L0_conv_w1_w, L0_conv_w1_b, L0_conv_w3_w, L0_conv_w3_b, L0_conv_w2_w, L0_conv_w2_b)
    t = _to_tokens(x)
    t = t + _L1_attn_ref(_ln_t(t), L1_attn_w_qkv, L1_attn_w_out, L1_attn_b_out)
    t = t + _L1_ffn_ref(_ln_t(t), L1_ffn_w_gate, L1_ffn_expert_bias, L1_ffn_wg, L1_ffn_wu, L1_ffn_wd, L1_ffn_swg, L1_ffn_swu, L1_ffn_swd)
    x = _from_tokens(t, x)
    return x

_drawn_inputs = setup_inputs


def setup_inputs(seed=0):
    import zlib

    import numpy as np

    out = dict(_drawn_inputs(seed))
    spreads = {'L1_ffn_expert_bias': (0.0, 0.8)}
    factors = {'L0_conv_fc1_b': 4.116,
     'L0_conv_w1_b': 6.713,
     'L0_conv_w3_b': 7.079,
     'L1_attn_w_qkv': 8.0,
     'L1_attn_w_out': 8.0,
     'L1_attn_b_out': 3.058,
     'L1_ffn_w_gate': 5.79,
     'L1_ffn_wg': 5.342,
     'L1_ffn_wu': 5.277,
     'L1_ffn_wd': 5.288,
     'L1_ffn_swg': 3.77,
     'L1_ffn_swu': 3.752,
     'L1_ffn_swd': 3.759}
    for name, (base, spread) in spreads.items():
        noise = np.random.default_rng([zlib.crc32(name.encode()), seed]).standard_normal(out[name].shape)
        drawn = base * np.exp(spread * noise) if base else spread * noise
        out[name] = jnp.asarray(drawn.astype(out[name].dtype))
    for name, factor in factors.items():
        out[name] = (out[name] * factor).astype(out[name].dtype)
    return out
```

```python
from contextlib import ExitStack

import numpy as np

import concourse.bass as bass
from concourse import mybir

ALU = mybir.AluOpType
ACT = mybir.ActivationFunctionType
AXX = mybir.AxisListType.X
F32 = mybir.dt.float32
I32 = mybir.dt.int32
U32 = mybir.dt.uint32

P = 128
IMAGES, TOKENS_IMG = 4, 256
T = IMAGES * TOKENS_IMG
NT = T // P
C = 192
CH = 96
NCH = C // CH
GROUP = C // 32
HEADS, D = 12, 16
DV = D + 1
ROWG = 32
QKC = 2 * HEADS * ROWG // P
TOPK = 2
E0, I0 = 8, 512
E1, I1 = 16, 384
NB0 = TOPK * T // P + E0 - 1
NB1 = TOPK * T // P + E1 - 1
OUT_OF_BOUNDS = 4096

C_IDENT = 0
C_TRI = C_IDENT + P
C_IOTA = C_TRI + P
C_GAVG = C_IOTA + P
C_MASK = C_GAVG + CH
C_TOK1 = C_MASK + TOKENS_IMG
C_BLK = C_TOK1 + NT
C_SUBT = C_BLK + NB1 + 1
C_ALL = C_SUBT + NT * E1


def constants():
    c = np.zeros((P, C_ALL), np.float32)
    n = np.arange(P)
    c[:, C_IDENT:C_IDENT + P] = np.eye(P)
    c[:, C_TRI:C_TRI + P] = n[:, None] < n[None, :]
    c[:, C_IOTA:C_IOTA + P] = n[None, :]
    g = np.arange(CH) // GROUP
    c[:CH, C_GAVG:C_GAVG + CH] = (g[:, None] == g[None, :]) / GROUP
    k = np.arange(TOKENS_IMG)
    c[:, C_MASK:C_MASK + TOKENS_IMG] = np.where(n[:, None] % 64 == k[None, :] % 64, 0.5, 1.0)
    c[:, C_TOK1:C_TOK1 + NT] = P * np.arange(NT)[None, :] + n[:, None] + 1
    c[:, C_BLK:C_BLK + NB1 + 1] = P * np.arange(NB1 + 1)[None, :]
    e = np.arange(E1)
    c[:E1, C_SUBT:C_SUBT + NT * E1] = np.tile(e[:, None] < e[None, :], (1, NT))
    return c


class Layer:

    def __init__(self, n, experts, blocks, inner, hid, sem):
        self.l, self.E, self.NB, self.I, self.IC, self.hid = n, experts, blocks, inner, inner // P, hid
        self.sh_stored = [sem(f"L{n}_sh_stored{i}") for i in range(2)]
        self.rows_in = [sem(f"L{n}_rows_in{i}") for i in range(2)]
        self.logits_ps = sem(f"L{n}_logits_ps")
        self.gap_ready = sem(f"L{n}_gap_ready")
        self.gap_exp = sem(f"L{n}_gap_exp")
        self.prefix_ready = sem(f"L{n}_prefix_ready")
        self.count_ps = sem(f"L{n}_count_ps")
        self.pads_ready = sem(f"L{n}_pads_ready")
        self.rank_ps = sem(f"L{n}_rank_ps")
        self.ended_ready = sem(f"L{n}_ended_ready")
        self.expert_ps = sem(f"L{n}_expert_ps")
        self.expert_ready = sem(f"L{n}_expert_ready")
        self.in_blk_ready = sem(f"L{n}_in_blk_ready")
        self.at_place_ready = sem(f"L{n}_at_place_ready")
        self.slots_ps = sem(f"L{n}_slots_ps")
        self.slots_ready = sem(f"L{n}_slots_ready")
        self.comb_ready = sem(f"L{n}_comb_ready")
        self.comb_ps = sem(f"L{n}_comb_ps")
        self.comb_out = sem(f"L{n}_comb_out")
        self.sh_a_ps = sem(f"L{n}_sh_a_ps")
        self.sh_c_ps = sem(f"L{n}_sh_c_ps")
        self.sh_g_ready = sem(f"L{n}_sh_g_ready")
        self.sh_h_ready = sem(f"L{n}_sh_h_ready")
        self.sh_y_ps = sem(f"L{n}_sh_y_ps")
        self.sh_y_ready = sem(f"L{n}_sh_y_ready")
        self.rows_t_ps = sem(f"L{n}_rows_t_ps")
        self.rows_t_ready = sem(f"L{n}_rows_t_ready")
        self.first_ps = sem(f"L{n}_first_ps")
        self.up_ps = sem(f"L{n}_up_ps")
        self.gate_act = sem(f"L{n}_gate_act")
        self.hid_ready = sem(f"L{n}_hid_ready")
        self.hid_t_ps = sem(f"L{n}_hid_t_ps")
        self.hid_t_ready = sem(f"L{n}_hid_t_ready")
        self.y_ps = sem(f"L{n}_y_ps")
        self.y_ready = sem(f"L{n}_y_ready")
        self.added = sem(f"L{n}_added")


def build(nc, d, out):
    with ExitStack() as ctx:
        def sb(name, shape, dt=F32):
            return ctx.enter_context(nc.sbuf_tensor(name, shape, dt))

        def sem(name):
            return ctx.enter_context(nc.semaphore(name))

        bank = ctx.enter_context(nc.psum_tensor("bank", [P, 8, 512], F32))

        xn_rows = [nc.dram_tensor(f"xn_rows{l}", [T, C], F32).ap() for l in range(2)]
        sum0 = nc.dram_tensor("sum0", [T, C], F32).ap()

        def by_tile(ap):
            return ap.rearrange("(j p) c -> p j c", p=P)

        const = sb("const", [P, C_ALL])
        ident = const[:, C_IDENT:C_IDENT + P]
        tri = const[:, C_TRI:C_TRI + P]
        iota = const[:, C_IOTA:C_IOTA + P]
        gavg = const[0:CH, C_GAVG:C_GAVG + CH]
        mask = const[:, C_MASK:C_MASK + TOKENS_IMG]
        tok1 = const[:, C_TOK1:C_TOK1 + NT]
        blk_start = const[:, C_BLK:C_BLK + NB1 + 1]

        ones = sb("ones", [P, P])
        w_first = sb("w_first", [P, E1 * NCH * 2 * I1])
        w_second = sb("w_second", [P, E1 * (I1 // P) * C])
        wg_up = w_first[0:CH, :].rearrange("p (e k g i) -> p e k g i", e=E1, k=NCH, g=2)
        fc1 = w_first[0:CH + 1, 0:E0 * NCH * I0].rearrange("p (e k i) -> p e k i", e=E0, k=NCH)
        fc2 = w_second[:, 0:E0 * (I0 // P) * C]
        o = E0 * NCH * I0
        w13 = w_first[0:CH, o:o + NCH * 2 * I0].rearrange("p (k g i) -> p k g i", k=NCH, g=2)
        o += NCH * 2 * I0
        w2 = w_first[:, o:o + (I0 // P) * C].rearrange("p (i c) -> p i c", c=C)
        o += (I0 // P) * C
        hid0 = w_first[:, o:o + (I0 // P) * T].rearrange("p (i t) -> p i t", t=T)
        o += (I0 // P) * T
        x_t = w_first[0:CH, o:o + NCH * T].rearrange("p (k t) -> p k t", t=T)
        o += NCH * T
        a_end = E1 * NCH * 2 * I1
        a = a_end - (NCH * QKC * P + NCH * C)
        wqk = w_first[0:CH, a:a + NCH * QKC * P].rearrange("p (k c m) -> p k c m", k=NCH, c=QKC)
        wv = w_first[0:CH, a + NCH * QKC * P:a_end].rearrange("p (k c) -> p k c", k=NCH)
        a -= NCH * TOKENS_IMG
        o_t = w_first[0:CH + 1, a:a + NCH * TOKENS_IMG].rearrange("p (k t) -> p k t", k=NCH)
        a -= 2 * C
        o_tok = w_first[:, a:a + 2 * C].rearrange("p (q c) -> p q c", q=2)
        a -= NT * HEADS * DV
        v_tok = w_first[:, a:a + NT * HEADS * DV].rearrange("p (j h d) -> p j h d", j=NT, h=HEADS)
        assert o <= a
        a -= QKC * T
        qk_t = w_first[:, a:a + QKC * T].rearrange("p (c t) -> p c t", c=QKC)
        per_expert = NCH * 2 * I1
        EARLY = a // per_expert
        LATE = E1 - 2
        hid1 = w_first[:, LATE * per_expert:].rearrange("p (i t) -> p i t", t=T)
        comb_t = w_second[0:E0 + 1, E0 * (I0 // P) * C:E0 * (I0 // P) * C + T]
        scratch = sb("scratch", [P, 4096])

        def scratch_at(o, *dims):
            n = int(np.prod(dims))
            ap = scratch[:, o:o + n]
            return ap.rearrange("p (a b) -> p a b", a=dims[0]) if len(dims) == 2 else ap.rearrange(
                "p (a b c) -> p a b c", a=dims[0], b=dims[1])

        x_tok = sb("x_tok", [P, NT, C])
        xn_tok = sb("xn_tok", [P, NT, C])
        xn_t = sb("xn_t", [CH + 1, NCH, T])
        chan_stats = sb("chan_stats", [CH, NCH * IMAGES, 6])
        chan_mv = sb("chan_mv", [CH, NCH * IMAGES, 2])
        grp_mean = sb("grp_mean", [CH, NCH * IMAGES])
        chan_dev = sb("chan_dev", [CH, NCH * IMAGES])
        grp_rstd = sb("grp_rstd", [CH, NCH * IMAGES])
        tok_stats = sb("tok_stats", [P, NT, 6])
        tok_mv = sb("tok_mv", [P, NT, 2])
        tok_rstd = sb("tok_rstd", [P, NT])

        gate_w = [sb("gate0", [CH, NCH, E0]), sb("gate1", [CH + 1, NCH, E1])]
        b13 = sb("b13", [P, 2, I0 // P])
        b2 = sb("b2", [E0 + 1, C])
        wo = sb("wo", [CH + 1, NCH, C])
        sh1 = sb("sh1", [CH, NCH, 2, I1])
        sh1d = sb("sh1d", [P, I1 // P, C])

        logit = sb("logit", [P, NT, E1])
        top8 = sb("top8", [P, NT, 8])
        top8i = sb("top8i", [P, NT, 8], U32)
        choice = sb("choice", [P, NT, TOPK])
        gap = sb("gap", [P, NT])
        gap_e = sb("gap_e", [P, NT])
        gap_1 = sb("gap_1", [P, NT])
        weight = sb("weight", [P, TOPK, NT])
        picked = sb("picked", [P, TOPK, NT, E1])
        comb = sb("comb", [P, NT, E0 + 1])
        comb_a = sb("comb_a", [P, NT, E0])
        before = sb("before", [P, NT + 1, E1])
        count_i = sb("count_i", [E1, 1], I32)
        count_i2 = sb("count_i2", [E1, 1], I32)
        padded = sb("padded", [E1, 1])
        padded_b = sb("padded_b", [E1, P])
        ended = sb("ended", [E1, NB1 + 1])
        blk_expert = sb("blk_expert", [1, NB1 + 1], I32)
        at_pick = sb("at_pick", [P, NT, E1])
        slot = sb("slot", [P, TOPK, NT])
        slot_i = sb("slot_i", [P, TOPK * NT], I32)
        slot_j = sb("slot_j", [P, 2, TOPK * NT], I32)
        slot_f = sb("slot_f", [P, 2, TOPK * NT])
        at_place = scratch_at(0, TOPK * NT, P)
        in_blk = scratch_at(TOPK * NT * P, TOPK * NT, 2, NB1 + 1)
        eq_blk = scratch_at(TOPK * NT * (P + 2 * NB1 + 2), TOPK * NT, NB1 + 1)
        empty = sb("empty", [P, NB1 + 1])
        slot_tok = sb("slot_tok", [P, NB1 + 1], I32)
        slot_w = sb("slot_w", [P, NB1 + 1])

        rows = [sb(f"rows{i}", [P, C]) for i in range(2)]
        rows_t = sb("rows_t", [CH + 1, NCH, P])
        act_h = sb("act_h", [P, I0])
        act_g = sb("act_g", [P, I1])
        hid_t = sb("hid_t", [P, I0])
        y = [sb(f"y{i}", [P, C]) for i in range(2)]
        g_sh = [sb(f"g_sh{i}", [P, 512]) for i in range(2)]
        y_sh = [sb(f"y_sh{i}", [P, C]) for i in range(2)]

        neg_max = sb("neg_max", [P, 4, 2])
        exp_sum = sb("exp_sum", [P, 4, 2])
        exp_inv = sb("exp_inv", [P, 2, 2])
        e1 = [scratch_at(512 * i, 2, TOKENS_IMG) for i in range(3)]
        att = [scratch_at(512 * (3 + i), 2, TOKENS_IMG) for i in range(2)]
        p2_t = [scratch_at(512 * (5 + i), 2, TOKENS_IMG) for i in range(3)]
        o_inv = sb("o_inv", [P, 2, HEADS])

        s_const, s_x, s_gate0, s_sh0, s_fc1, s_fc2 = (sem(n) for n in (
            "const_loaded", "x_loaded", "gate0_loaded", "shared0_loaded", "fc1_loaded", "fc2_loaded"))
        s_attw, s_gate1, s_sh1, s_w1a, s_w1b = (sem(n) for n in (
            "attn_w_loaded", "gate1_loaded", "shared1_loaded", "gate_up_loaded", "down_loaded"))
        filled = sem("fills_done")
        x_tok_in = sem("x_tok_loaded")
        act_c, dve_c, pool_c = sem("act_own"), sem("dve_own"), sem("pool_own")
        chan_ready, dev_ready = sem("chan_stats_ready"), sem("chan_dev_ready")
        gmean_ps, gvar_ps = sem("group_mean_in_psum"), sem("group_var_in_psum")
        var_ready, std_ready = sem("var_ready"), sem("std_ready")
        xn_t_ready = sem("xn_t_ready")
        tp_ps = sem("norm_transposed_in_psum")
        tp_out = sem("norm_transposes_copied")
        xn_stored = sem("xn_rows_stored")
        xn_tok_ready = sem("xn_tok_ready")
        sum_ready = sem("sum0_loaded")

        layers = []
        for l, (E, NB, I) in enumerate(((E0, NB0, I0), (E1, NB1, I1))):
            layers.append(Layer(l, E, NB, I, (hid0, hid1)[l], sem))
        L0, L1 = layers

        qk_ps, qk_out, v_ps, v_out = sem("qk_in_psum"), sem("qk_copied"), sem("v_in_psum"), sem("v_copied")
        qk_out_v = sem("qk_copied_by_vector")
        sc_ps, nmax_ready, e1_ready, att_ready = (
            sem("scores_in_psum"), sem("neg_max_ready"), sem("exp_ready"), sem("att_ready"))
        att_t_ps, p2_ready, av_ps = sem("att_t_in_psum"), sem("p2_ready"), sem("av_in_psum")
        o_ready, o_t_ps, o_t_ready, proj_ps, x_new = (
            sem("o_ready"), sem("o_t_in_psum"), sem("o_t_ready"), sem("proj_in_psum"), sem("x_updated"))
        out_done = sem("out_stored")

        def chained(eng, s):
            n = [0]

            def step(ins):
                n[0] += 1
                ins.then_inc(s, 1)

            def join():
                eng.wait_ge(s, n[0])

            def go(ins):
                step(ins)
                join()
            return step, join, go

        N_HEADS = IMAGES * HEADS
        ATT_STEPS = N_HEADS + 8
        OUT_T_LAG = 5

        HALF = T // 2
        plan = {
            0: (["logits", 0, 1, "count", 2, "rank", 3, "expert", 4, 5, "slots", 6, 7],
                ["top2", 0, 1, "pads", 2, "ended", 3, "expert", "place", 4, 5, "slots", 6, 7]),
            1: (["logits", 0, 1, "count", 2, "rank", 3, "expert", 4, "slots", 5],
                ["top2", 0, 1, "pads", 2, "ended", 3, "expert", "place", 4, "slots", 5]),
        }

        def bc(ap, axis, shape):
            return ap.unsqueeze(axis).to_broadcast(shape)

        block = ctx.enter_context(nc.Block())

        @block.sync
        def _(sp):
            sp.dma_start(x_t, d["x_t"]).then_inc(s_x, 16)
            sp.dma_start(const[:], d["const"]).then_inc(s_const, 16)
            sp.dma_start(gate_w[0][:], d["gate0"]).then_inc(s_gate0, 16)
            sp.dma_start(w13, d["w13"]).then_inc(s_sh0, 16)
            sp.dma_start(b13[:], d["b13"]).then_inc(s_sh0, 16)
            sp.dma_start(w2, d["w2"]).then_inc(s_sh0, 16)
            sp.dma_start(b2[0:E0, :], d["fc2_b"]).then_inc(s_sh0, 16)
            sp.dma_start(b2[E0:E0 + 1, :], d["w2_b"]).then_inc(s_sh0, 16)
            sp.dma_start(x_tok[:], by_tile(d["x"])).then_inc(x_tok_in, 16)
            sp.dma_start(fc1[0:CH], d["fc1"]).then_inc(s_fc1, 16)
            sp.dma_start(fc1[CH:CH + 1, :, 1, :], d["fc1_b"]).then_inc(s_fc1, 16)
            sp.dma_start(fc2, d["fc2"]).then_inc(s_fc2, 16)
            sp.wait_ge(tp_out, NT // 2)
            sp.dma_start(by_tile(xn_rows[0]), xn_tok[:]).then_inc(xn_stored, 16)
            sp.dma_start(wqk, d["wqk"]).then_inc(s_attw, 16)
            sp.dma_start(wv, d["wv"]).then_inc(s_attw, 16)
            sp.dma_start(wo[0:CH], d["wo"]).then_inc(s_attw, 16)
            sp.dma_start(wo[CH:CH + 1, 1, :], d["b_out"]).then_inc(s_attw, 16)
            sp.dma_start(gate_w[1][0:CH], d["gate1"]).then_inc(s_gate1, 16)
            sp.dma_start(gate_w[1][CH:CH + 1, 1, :], d["bias1"]).then_inc(s_gate1, 16)
            sp.dma_start(sh1[:], d["sh1"]).then_inc(s_sh1, 16)
            sp.dma_start(sh1d[:], d["sh1d"]).then_inc(s_sh1, 16)
            for j in range(NT):
                sp.wait_ge(L0.sh_y_ready, j + 1)
                sp.dma_start(sum0[j * P:(j + 1) * P], y_sh[j % 2][:]).then_inc(L0.sh_stored[j % 2], 16)
            sp.wait_ge(L0.added, 16 * NB0)
            sp.dma_start(x_tok[:], by_tile(sum0)).then_inc(sum_ready, 16)
            sp.wait_ge(L0.y_ps, NB0)
            for e in range(EARLY):
                sp.dma_start(wg_up[:, e], d["gate_up"][:, e]).then_inc(s_w1a, 16)
            sp.dma_start(w_second[:], d["down"]).then_inc(s_w1b, 16)
            sp.wait_ge(xn_tok_ready, 2 * NT)
            sp.dma_start(by_tile(xn_rows[1]), xn_tok[:]).then_inc(xn_stored, 16)
            for e in range(EARLY, LATE):
                sp.dma_start(wg_up[:, e], d["gate_up"][:, e]).then_inc(s_w1a, 16)
            for j in range(NT):
                sp.wait_ge(L1.sh_y_ready, j + 1)
                sp.dma_start(out[j * P:(j + 1) * P], y_sh[j % 2][:]).then_inc(L1.sh_stored[j % 2], 16)
            for e in range(LATE, E1):
                sp.dma_start(wg_up[:, e], d["gate_up"][:, e]).then_inc(s_w1a, 16)
            sp.wait_ge(L1.added, 16 * NB1)

        def pool_blocks(pool, L, target):
            pool.wait_ge(L.slots_ready, 1)
            pool.wait_ge(xn_stored, 16 * (L.l + 1))

            def gather(b):
                pool.indirect_dma_start(
                    rows[b % 2][:], None, xn_rows[L.l],
                    bass.IndirectOffsetOnAxis(slot_tok[:, b:b + 1].bitcast(U32), 0),
                    bounds_check=T - 1, oob_is_err=False).then_inc(L.rows_in[b % 2], 16)

            def add(b):
                pool.wait_ge(L.y_ready, b + 1)
                if b:
                    pool.wait_ge(L.added, b * 16)
                pool.indirect_dma_start(
                    target, bass.IndirectOffsetOnAxis(slot_tok[:, b:b + 1].bitcast(U32), 0), y[b % 2][:], None,
                    bounds_check=T - 1, oob_is_err=False, compute_op=ALU.add).then_inc(L.added, 16)

            AHEAD = 4
            for b in range(AHEAD):
                if b >= 2:
                    pool.wait_ge(L.rows_t_ps, b - 1)
                gather(b)
            for s in L.sh_stored:
                pool.wait_ge(s, 16 * NT // 2)
            for b in range(L.NB):
                add(b)
                if b + AHEAD <= L.NB:
                    pool.wait_ge(L.rows_t_ps, b + AHEAD - 1)
                    gather(b + AHEAD)

        @block.gpsimd
        def _(pool):
            fills = [(ones[:], 1.0), (rows[0][:], 0.0), (rows[1][:], 0.0), (comb[:, :, E0:E0 + 1], 1.0),
                     (xn_t[CH:CH + 1, 1, :], 1.0), (rows_t[CH:CH + 1, 1, :], 1.0),
                     (o_t[CH:CH + 1, 1, :], 1.0), (v_tok[:, :, :, D:DV], 1.0),
                     (before[:, 0, :], 0.0)]
            for n, (ap, v) in enumerate(fills):
                nc.gpsimd.memset(ap, v).then_inc(pool_c, 1)
                pool.wait_ge(pool_c, n + 1)
            pool.sem_inc(filled, 1)
            pool_blocks(pool, L0, sum0)
            pool_blocks(pool, L1, out)

        def act_norm_transposes(act, which):
            for n in range(NT // 2):
                act.wait_ge(tp_ps, which * (NT // 2) + n + 1)
                src = bank[:, 1 + n % 2, :]
                if which == 0:
                    ins = nc.scalar.copy(xn_tok[:, 2 * n:2 * n + 2, :],
                                         src[:, 0:2 * C].rearrange("p (j c) -> p j c", c=C))
                else:
                    ins = nc.scalar.copy(xn_t[0:CH, :, 2 * n * P:(2 * n + 2) * P],
                                         src[0:CH].rearrange("p (k t) -> p k t", k=NCH))
                ins.then_inc(tp_out, 1)

        def act_shared(act, L, s):
            ic = s % L.IC
            act.wait_ge(L.sh_a_ps, s + 1)
            if s >= 2:
                act.wait_ge(L.sh_h_ready, s - 1)
            if L.l == 0:
                ins = nc.scalar.activation(g_sh[s % 2][:], bank[:, 4 + s % 2, :], ACT.Gelu,
                                           bias=b13[:, 0, ic:ic + 1])
            else:
                ins = nc.scalar.activation(g_sh[s % 2][:], bank[:, 4 + s % 2, :], ACT.Silu)
            ins.then_inc(L.sh_g_ready, 1)

        def act_rows(act, L, b):
            act.wait_ge(L.rows_t_ps, b + 1)
            nc.scalar.copy(rows_t[0:CH], bank[0:CH, 0, 0:NCH * P].rearrange("p (k t) -> p k t", k=NCH)
                           ).then_inc(L.rows_t_ready, 1)

        def act_block(act, L, b):
            act.wait_ge(L.first_ps, b + 1)
            if L.l == 0:
                nc.scalar.activation(act_h[:], bank[:, 5, :], ACT.Gelu).then_inc(L.hid_ready, 1)
            else:
                if not isinstance(b, int) or b > 0:
                    act.wait_ge(L.hid_ready, b)
                nc.scalar.activation(act_g[:], bank[:, 5, 0:I1], ACT.Silu).then_inc(L.gate_act, 1)

        def act_blocks(act, L):
            act_rows(act, L, 0)
            act_block(act, L, 0)
            act_rows(act, L, 1)
            with act.Fori(0, (L.NB - 1) // 2) as i:
                for u in range(2):
                    b = i * 2 + (u + 1)
                    act_block(act, L, b)
                    act_rows(act, L, b + 1)

        @block.scalar
        def _(act):
            act.wait_ge(var_ready, 1)
            nc.scalar.sqrt(grp_rstd[:], grp_rstd[:]).then_inc(std_ready, 1)
            act_norm_transposes(act, 0)
            act.wait_ge(L0.gap_ready, 1)
            nc.scalar.activation(gap_e[:], gap[:], ACT.Exp).then_inc(L0.gap_exp, 1)
            for s in range(2 * L0.IC):
                act_shared(act, L0, s)
            act_blocks(act, L0)

            act.wait_ge(var_ready, 2)
            nc.scalar.sqrt(tok_rstd[:], tok_rstd[:]).then_inc(std_ready, 1)
            act_norm_transposes(act, 1)
            for n in range(0, 2 * QKC, 2):
                c, half = n // 2, 0
                act.wait_ge(qk_ps, n + 1)
                nc.scalar.mul(qk_t[:, c, 0:HALF], bank[:, n % 6, :],
                              D ** -0.5 if c < QKC // 2 else 1.0).then_inc(qk_out, 1)

            def exp_scores(n):
                act.wait_ge(nmax_ready, n + 1)
                if n >= 3:
                    act.wait_ge(att_ready, n - 2)
                for qt in range(2):
                    nc.scalar.activation(e1[n % 3][:, qt, :], bank[:, n % 3, qt * 256:(qt + 1) * 256], ACT.Exp,
                                         bias=neg_max[:, n % 4, qt:qt + 1],
                                         accum_out=exp_sum[:, n % 4, qt:qt + 1]).then_inc(e1_ready, 1)

            def exp_att(n):
                act.wait_ge(att_t_ps, n + 1)
                if n >= 3:
                    act.wait_ge(av_ps, n - 2)
                nc.scalar.activation(p2_t[n % 3][:].rearrange("p a b -> p (a b)"), bank[:, 3 + n % 2, :],
                                     ACT.Exp).then_inc(p2_ready, 1)

            def out_t(img):
                act.wait_ge(o_t_ps, img + 1)
                nc.scalar.copy(o_t[0:CH], bank[0:CH, 7, :].rearrange("p (k t) -> p k t", k=NCH)
                               ).then_inc(o_t_ready, 1)

            for n in range(ATT_STEPS):
                if n < N_HEADS:
                    exp_scores(n)
                if 0 <= n - 2 < N_HEADS:
                    exp_att(n - 2)
                if (n - OUT_T_LAG) % HEADS == 0 and n >= HEADS:
                    out_t((n - OUT_T_LAG) // HEADS - 1)

            act.wait_ge(var_ready, 3)
            nc.scalar.sqrt(tok_rstd[:], tok_rstd[:]).then_inc(std_ready, 1)
            act_norm_transposes(act, 2)
            act.wait_ge(L1.gap_ready, 1)
            nc.scalar.activation(gap_e[:], gap[:], ACT.Exp).then_inc(L1.gap_exp, 1)
            for s in range(2 * L1.IC):
                act_shared(act, L1, s)
            act_blocks(act, L1)

        @block.vector
        def _(dve):
            v = nc.vector
            step, join, go = chained(dve, dve_c)

            dve.wait_ge(s_x, 16)
            for k in range(NCH):
                for img in range(IMAGES):
                    step(v.bn_stats(chan_stats[:, k * IMAGES + img, :],
                                    x_t[:, k, img * TOKENS_IMG:(img + 1) * TOKENS_IMG]))
            join()
            for n in range(NCH * IMAGES):
                v.bn_aggr(chan_mv[:, n, :], chan_stats[:, n, :]).then_inc(chan_ready, 1)
            dve.wait_ge(gmean_ps, 1)
            go(v.tensor_copy(grp_mean[:], bank[0:CH, 0, 0:NCH * IMAGES]))
            go(v.tensor_tensor(chan_dev[:], chan_mv[:, :, 0], grp_mean[:], ALU.subtract))
            go(v.tensor_tensor(chan_dev[:], chan_dev[:], chan_dev[:], ALU.mult))
            v.tensor_tensor(chan_dev[:], chan_dev[:], chan_mv[:, :, 1], ALU.add).then_inc(dev_ready, 1)
            dve.wait_ge(gvar_ps, 1)
            v.tensor_scalar(grp_rstd[:], bank[0:CH, 0, 64:64 + NCH * IMAGES], 1e-5, None, ALU.add
                            ).then_inc(var_ready, 1)
            dve.wait_ge(std_ready, 1)
            go(v.reciprocal(grp_rstd[:], grp_rstd[:]))
            for img in range(IMAGES):
                for k in range(NCH):
                    n = k * IMAGES + img
                    span = slice(img * TOKENS_IMG, (img + 1) * TOKENS_IMG)
                    v.tensor_scalar(xn_t[0:CH, k, span], x_t[:, k, span], grp_mean[:, n:n + 1],
                                    grp_rstd[:, n:n + 1], ALU.subtract, ALU.mult).then_inc(xn_t_ready, 1)

            def route(L, stage):
                E, NBP = L.E, L.NB + 1
                if stage == "top2":
                    dve.wait_ge(L.logits_ps, 1)
                    lg = logit[:, :, 0:E]
                    go(v.tensor_copy(lg, bank[:, 3, 0:NT * E].rearrange("p (j e) -> p j e", e=E)))
                    for j in range(NT):
                        step(v.max(top8[:, j, :], logit[:, j, 0:E]))
                    join()
                    for j in range(NT):
                        step(v.max_index(top8i[:, j, :], top8[:, j, :], logit[:, j, 0:E]))
                    v.tensor_tensor(gap[:], top8[:, :, 1], top8[:, :, 0], ALU.subtract).then_inc(L.gap_ready, 1)
                    join()
                    go(v.tensor_copy(choice[:], top8i[:, :, 0:TOPK]))
                    iota_e = bc(iota[:, 0:E], 1, [P, NT, E])
                    for k in range(TOPK):
                        step(v.tensor_tensor(picked[:, k, :, 0:E], iota_e,
                                             bc(choice[:, :, k], 2, [P, NT, E]), ALU.is_equal))
                    join()
                    go(v.tensor_tensor(at_pick[:, :, 0:E], picked[:, 0, :, 0:E], picked[:, 1, :, 0:E], ALU.add))
                    dve.wait_ge(filled, 1)
                    for j in range(NT):
                        ins = v.tensor_tensor(before[:, j + 1, 0:E], before[:, j, 0:E], at_pick[:, j, 0:E], ALU.add)
                        if j < NT - 1:
                            go(ins)
                    ins.then_inc(L.prefix_ready, 1)
                    dve.wait_ge(L.gap_exp, 1)
                    go(v.tensor_scalar(gap_1[:], gap_e[:], 1.0, None, ALU.add))
                    go(v.reciprocal(weight[:, 0, :], gap_1[:]))
                    go(v.tensor_tensor(weight[:, 1, :], gap_e[:], weight[:, 0, :], ALU.mult))
                    if L.l == 0:
                        w = [bc(weight[:, k, :], 2, [P, NT, E]) for k in range(TOPK)]
                        go(v.tensor_tensor(comb_a[:], picked[:, 0, :, 0:E], w[0], ALU.mult))
                        go(v.tensor_tensor(comb[:, :, 0:E], picked[:, 1, :, 0:E], w[1], ALU.mult))
                        v.tensor_tensor(comb[:, :, 0:E], comb[:, :, 0:E], comb_a[:], ALU.add
                                        ).then_inc(L.comb_ready, 1)
                elif stage == "pads":
                    dve.wait_ge(L.count_ps, 1)
                    go(v.tensor_scalar(count_i[0:E], bank[0:E, 3, 256:257], float(P - 1), None, ALU.add))
                    go(v.tensor_scalar(count_i2[0:E], count_i[0:E], 7, 7, ALU.arith_shift_right,
                                       ALU.arith_shift_left))
                    go(v.tensor_copy(padded[0:E], count_i2[0:E]))
                    v.tensor_scalar(padded_b[0:E], ones[0:E, :], padded[0:E, 0:1], None, ALU.mult
                                    ).then_inc(L.pads_ready, 1)
                elif stage == "ended":
                    dve.wait_ge(L.rank_ps, 1)
                    go(v.tensor_copy(padded[0:E], bank[0:E, 3, 260:261]))
                    v.tensor_scalar(ended[0:E, 0:NBP], blk_start[0:E, 0:NBP], padded[0:E, 0:1], None,
                                    ALU.is_ge).then_inc(L.ended_ready, 1)
                    rank = bank[:, 7, 0:NT * E].rearrange("p (j e) -> p j e", e=E)
                    for k in range(TOPK):
                        go(v.tensor_tensor(at_pick[:, :, 0:E], picked[:, k, :, 0:E], rank, ALU.mult))
                        go(v.tensor_reduce(slot[:, k, :], at_pick[:, :, 0:E], AXX, ALU.add))
                    go(v.tensor_copy(slot_i[:], slot[:].rearrange("p k j -> p (k j)")))
                    step(v.tensor_scalar(slot_j[:, 0, :], slot_i[:], P - 1, None, ALU.bitwise_and))
                    step(v.tensor_scalar(slot_j[:, 1, :], slot_i[:], 7, None, ALU.arith_shift_right))
                    join()
                    go(v.tensor_copy(slot_f[:], slot_j[:]))
                elif stage == "expert":
                    dve.wait_ge(L.expert_ps, 1)
                    v.tensor_scalar(blk_expert[:, 0:NBP], bank[0:1, 3, 264:264 + NBP], float(E - 1), None,
                                    ALU.min).then_inc(L.expert_ready, 1)
                elif stage == "place":
                    n = TOPK * NT
                    go(v.tensor_tensor(eq_blk[:, :, 0:NBP], bc(iota[:, 0:NBP], 1, [P, n, NBP]),
                                       bc(slot_f[:, 1, :], 2, [P, n, NBP]), ALU.is_equal))
                    for k in range(TOPK):
                        s = slice(k * NT, (k + 1) * NT)
                        v.tensor_tensor(in_blk[:, s, 0, 0:NBP], eq_blk[:, s, 0:NBP],
                                        bc(tok1, 2, [P, NT, NBP]), ALU.mult).then_inc(L.in_blk_ready, 1)
                        v.tensor_tensor(in_blk[:, s, 1, 0:NBP], eq_blk[:, s, 0:NBP],
                                        bc(weight[:, k, :], 2, [P, NT, NBP]), ALU.mult
                                        ).then_inc(L.in_blk_ready, 1)
                    for m in range(n):
                        v.tensor_scalar(at_place[:, m, :], iota, slot_f[:, 0, m:m + 1], None, ALU.is_equal
                                        ).then_inc(L.at_place_ready, 1)
                elif stage == "slots":
                    dve.wait_ge(L.slots_ps, 1)
                    sm = bank[:, 6, 0:2 * NBP].rearrange("p (w b) -> p w b", w=2)
                    go(v.tensor_scalar(empty[:, 0:NBP], sm[:, 0], 0.0, float(OUT_OF_BOUNDS), ALU.is_equal, ALU.mult))
                    step(v.tensor_copy(slot_w[:, 0:NBP], sm[:, 1]))
                    step(v.scalar_tensor_tensor(slot_tok[:, 0:NBP], sm[:, 0], -1.0, empty[:, 0:NBP],
                                                ALU.add, ALU.add))
                    join()
                    dve.sem_inc(L.slots_ready, 1)

            def shared(L, s):
                half, ic = s // L.IC, s % L.IC
                dve.wait_ge(L.sh_c_ps, s + 1)
                dve.wait_ge(L.sh_g_ready, s + 1)
                dst = L.hid[:, ic, half * HALF:(half + 1) * HALF]
                if L.l == 0:
                    ins = v.scalar_tensor_tensor(dst, bank[:, 1 + s % 2, :], b13[:, 1, ic:ic + 1],
                                                 g_sh[s % 2][:], ALU.add, ALU.mult)
                else:
                    ins = v.tensor_tensor(dst, bank[:, 1 + s % 2, :], g_sh[s % 2][:], ALU.mult)
                ins.then_inc(L.sh_h_ready, 1)

            def shared_out(L):
                if L.l == 0:
                    for half in range(2):
                        dve.wait_ge(L.comb_ps, half + 1)
                        v.tensor_copy(comb_t[:, half * HALF:(half + 1) * HALF], bank[0:E0 + 1, 1 + half, :]
                                      ).then_inc(L.comb_out, 1)
                    dve.wait_ge(x_tok_in, 16)
                for j in range(NT):
                    dve.wait_ge(L.sh_y_ps, j + 1)
                    if j >= 2:
                        dve.wait_ge(L.sh_stored[j % 2], 16 * (j // 2))
                    v.tensor_tensor(y_sh[j % 2][:], bank[:, 4 + j % 2, 0:C], x_tok[:, j, :], ALU.add
                                    ).then_inc(L.sh_y_ready, 1)

            def hid_copy(L, b):
                dve.wait_ge(L.hid_t_ps, b + 1)
                v.tensor_copy(hid_t[:, 0:L.I], bank[:, 7, 0:L.I]).then_inc(L.hid_t_ready, 1)

            def product(L, b):
                dve.wait_ge(L.up_ps, b + 1)
                dve.wait_ge(L.gate_act, b + 1)
                v.tensor_tensor(act_h[:, 0:I1], bank[:, 6, 0:I1], act_g[:], ALU.mult).then_inc(L.hid_ready, 1)

            def result(L, b, u, first=False):
                dve.wait_ge(L.y_ps, b + 1)
                if not first:
                    dve.wait_ge(L.added, (b - 1) * 16)
                v.tensor_scalar(y[u][:], bank[:, 1, 0:C], slot_w[:, bass.ds(b, 1)], None, ALU.mult
                                ).then_inc(L.y_ready, 1)

            def blocks(L):
                if L.l:
                    product(L, 0)
                hid_copy(L, 0)
                if L.l:
                    product(L, 1)
                result(L, 0, 0, True)
                hid_copy(L, 1)
                if L.l:
                    product(L, 2)
                result(L, 1, 1, True)
                with dve.Fori(0, (L.NB - 3) // 2) as i:
                    for u in range(2):
                        b = i * 2 + (u + 3)
                        hid_copy(L, b - 1)
                        if L.l:
                            product(L, b)
                        result(L, b - 1, u)
                hid_copy(L, L.NB - 1)
                result(L, L.NB - 1, (L.NB - 1) % 2)

            def layernorm(which):
                for j in range(NT):
                    step(v.bn_stats(tok_stats[:, j, :], x_tok[:, j, :]))
                join()
                for j in range(NT):
                    step(v.bn_aggr(tok_mv[:, j, :], tok_stats[:, j, :]))
                join()
                v.tensor_scalar(tok_rstd[:], tok_mv[:, :, 1], 1e-5, None, ALU.add).then_inc(var_ready, 1)
                dve.wait_ge(std_ready, which + 1)
                go(v.reciprocal(tok_rstd[:], tok_rstd[:]))
                for j in range(NT):
                    v.tensor_scalar(xn_tok[:, j, :], x_tok[:, j, :], tok_mv[:, j, 0:1], tok_rstd[:, j:j + 1],
                                    ALU.subtract, ALU.mult).then_inc(xn_tok_ready, 1)

            for s in plan[0][1]:
                shared(L0, s) if isinstance(s, int) else route(L0, s)
            shared_out(L0)
            blocks(L0)

            dve.wait_ge(sum_ready, 16)
            layernorm(1)
            for n in range(1, 2 * QKC, 2):
                c = n // 2
                dve.wait_ge(qk_ps, n + 1)
                v.tensor_scalar(qk_t[:, c, HALF:T], bank[:, n % 6, :], D ** -0.5 if c < QKC // 2 else 1.0,
                                None, ALU.mult).then_inc(qk_out_v, 1)
            dve.wait_ge(filled, 1)
            for n in range(NT // 2):
                dve.wait_ge(v_ps, n + 1)
                v.tensor_copy(v_tok[:, 2 * n:2 * n + 2, :, 0:D].rearrange("p j h d -> p (j h) d"),
                              bank[:, 6 + n % 2, 0:2 * C].rearrange("p (m d) -> p m d", d=D)
                              ).then_inc(v_out, 1)

            def neg_maximum(n):
                dve.wait_ge(sc_ps, n + 1)
                v.tensor_reduce(neg_max[:, n % 4, :], bank[:, n % 3, :].rearrange("p (a b) -> p a b", a=2),
                                AXX, ALU.max, negate=True).then_inc(nmax_ready, 1)

            def attention(n):
                dve.wait_ge(e1_ready, 2 * n + 2)
                if n >= 2:
                    dve.wait_ge(att_t_ps, n - 1)
                go(v.reciprocal(exp_inv[:, n % 2, :], exp_sum[:, n % 4, :]))
                for qt in range(2):
                    ins = v.scalar_tensor_tensor(att[n % 2][:, qt, :], e1[n % 3][:, qt, :], exp_inv[:, n % 2, qt:qt + 1],
                                                 mask, ALU.mult, ALU.mult)
                    if qt == 0:
                        step(ins)
                ins.then_inc(att_ready, 1)

            def out_norm(img):
                dve.wait_ge(av_ps, HEADS * (img + 1))
                src = bank[:, 5 + img % 2, 0:2 * HEADS * DV].rearrange("p (m d) -> p m d", d=DV)
                go(v.reciprocal(o_inv[:].rearrange("p a h -> p (a h)"), src[:, :, D]))
                if img:
                    dve.wait_ge(o_t_ps, img)
                v.tensor_tensor(o_tok[:].rearrange("p a (h d) -> p (a h) d", d=D), src[:, :, 0:D],
                                bc(o_inv[:].rearrange("p a h -> p (a h)"), 2, [P, 2 * HEADS, D]), ALU.mult
                                ).then_inc(o_ready, 1)

            def residual(img):
                dve.wait_ge(proj_ps, img + 1)
                go(v.tensor_tensor(x_tok[:, 2 * img:2 * img + 2, :], x_tok[:, 2 * img:2 * img + 2, :],
                                   bank[:, 5 + img % 2, 0:2 * C].rearrange("p (j c) -> p j c", c=C), ALU.add))
                dve.sem_inc(x_new, 1)

            for n in range(ATT_STEPS):
                if n < N_HEADS:
                    neg_maximum(n)
                if 0 <= n - 1 < N_HEADS:
                    attention(n - 1)
                if n >= HEADS and (n - 4) % HEADS == 0:
                    out_norm((n - 4) // HEADS - 1)
                if n >= HEADS and (n - 7) % HEADS == 0:
                    residual((n - 7) // HEADS - 1)

            layernorm(2)
            for s in plan[1][1]:
                shared(L1, s) if isinstance(s, int) else route(L1, s)
            shared_out(L1)
            blocks(L1)

        @block.tensor
        def _(pe):
            def tile(j):
                return slice(j * P, (j + 1) * P)

            def route(L, stage):
                E, NBP = L.E, L.NB + 1
                if stage == "logits":
                    pe.wait_ge(s_gate0 if L.l == 0 else s_gate1, 16 if L.l == 0 else 32)
                    rows_k = CH + 1 if L.l else CH
                    for j in range(NT):
                        for k in range(NCH):
                            kr = rows_k if k == 1 else CH
                            ins = pe.matmul(bank[:, 3, j * E:(j + 1) * E], xn_t[0:kr, k, tile(j)],
                                            gate_w[L.l][0:kr, k, :], start=(k == 0), stop=(k == NCH - 1))
                    ins.then_inc(L.logits_ps, 1)
                elif stage == "count":
                    pe.wait_ge(L.prefix_ready, 1)
                    pe.matmul(bank[0:E, 3, 256:257], before[:, NT, 0:E], ones[:, 0:1],
                              start=True, stop=True).then_inc(L.count_ps, 1)
                elif stage == "rank":
                    pe.wait_ge(L.pads_ready, 1)
                    dst = bank[:, 7, 0:NT * E].rearrange("p (j e) -> p j e", e=E)
                    subt = const[0:E, C_SUBT:C_SUBT + NT * E1].rearrange("p (j e) -> p j e", e=E1)[:, :, 0:E]
                    pe.matmul(dst, tri, at_pick[:, :, 0:E], start=True, stop=False)
                    pe.matmul(dst, ones[:], before[:, 0:NT, 0:E], start=False, stop=False)
                    pe.matmul(dst, padded_b[0:E, :], subt, start=False, stop=True)
                    pe.matmul(bank[0:E, 3, 260:261], subt[:, 0, :], padded[0:E, :], start=True, stop=False)
                    pe.matmul(bank[0:E, 3, 260:261], ident[0:E, 0:E], padded[0:E, :], start=False, stop=True
                              ).then_inc(L.rank_ps, 1)
                elif stage == "expert":
                    pe.wait_ge(L.ended_ready, 1)
                    pe.matmul(bank[0:1, 3, 264:264 + NBP], ones[0:E, 0:1], ended[0:E, 0:NBP],
                              start=True, stop=True).then_inc(L.expert_ps, 1)
                elif stage == "slots":
                    n = TOPK * NT
                    pe.wait_ge(L.in_blk_ready, 2 * TOPK)
                    pe.wait_ge(L.at_place_ready, n)
                    dst = bank[:, 6, 0:2 * NBP].rearrange("p (w b) -> p w b", w=2)
                    for m in range(n):
                        ins = pe.matmul(dst, at_place[:, m, :], in_blk[:, m, :, 0:NBP],
                                        start=(m == 0), stop=(m == n - 1))
                    ins.then_inc(L.slots_ps, 1)

            def shared(L, s):
                half, ic = s // L.IC, s % L.IC
                w = w13 if L.l == 0 else sh1
                for g, (bk, done) in enumerate(((4, L.sh_a_ps), (1, L.sh_c_ps))):
                    if s >= 2:
                        pe.wait_ge(L.sh_g_ready if g == 0 else L.sh_h_ready, s - 1)
                    for k in range(NCH):
                        ins = pe.matmul(bank[:, bk + s % 2, :], w[:, k, g, ic * P:(ic + 1) * P],
                                        xn_t[0:CH, k, half * HALF:(half + 1) * HALF],
                                        start=(k == 0), stop=(k == NCH - 1))
                    ins.then_inc(done, 1)

            def shared_out(L):
                steps = 2 * L.IC
                if L.l == 0:
                    pe.wait_ge(L.comb_ready, 1)
                    pe.wait_ge(L.sh_h_ready, steps)
                    for half in range(2):
                        for j in range(NT // 2):
                            ins = pe.transpose(bank[0:E0 + 1, 1 + half, tile(j)],
                                               comb[:, half * NT // 2 + j, :], ident)
                        ins.then_inc(L.comb_ps, 1)
                pe.wait_ge(L.sh_h_ready, steps)
                w = w2 if L.l == 0 else sh1d[:]
                for j in range(NT):
                    if j >= 2:
                        pe.wait_ge(L.sh_y_ready, j - 1)
                    dst = bank[:, 4 + j % 2, 0:C]
                    for ic in range(L.IC):
                        ins = pe.matmul(dst, L.hid[:, ic, tile(j)], w[:, ic, :], start=(ic == 0),
                                        stop=(L.l == 1 and ic == L.IC - 1))
                    if L.l == 0:
                        pe.wait_ge(L.comb_out, 1 if j < NT // 2 else 2)
                        ins = pe.matmul(dst, comb_t[:, tile(j)], b2[:], start=False, stop=True)
                    ins.then_inc(L.sh_y_ps, 1)

            def rows_transpose(L, b, u, n):
                pe.wait_ge(L.rows_in[u], (n + 1) * 16)
                for k in range(NCH):
                    ins = pe.transpose(bank[0:CH, 0, tile(k)], rows[u][:, k * CH:(k + 1) * CH], ident)
                ins.then_inc(L.rows_t_ps, 1)

            def expert_of(L, b):
                return pe.value_load(blk_expert[0:1, bass.ds(b, 1)], min_val=0, max_val=L.E - 1)

            def first(L, b):
                e = expert_of(L, b)
                pe.wait_ge(L.rows_t_ready, b + 1)
                if L.l == 0:
                    for k in range(NCH):
                        kr = CH + k
                        ins = pe.matmul(bank[:, 5, :], rows_t[0:kr, k, :],
                                        w_first[0:kr, bass.ds(e * (NCH * I0) + k * I0, I0)],
                                        start=(k == 0), stop=(k == NCH - 1))
                    ins.then_inc(L.first_ps, 1)
                else:
                    for g, done in enumerate((L.first_ps, L.up_ps)):
                        for k in range(NCH):
                            ins = pe.matmul(bank[:, 5 + g, 0:I1], rows_t[0:CH, k, :],
                                            w_first[0:CH, bass.ds(e * (NCH * 2 * I1) + (k * 2 + g) * I1, I1)],
                                            start=(k == 0), stop=(k == NCH - 1))
                        ins.then_inc(done, 1)

            def hid_transpose(L, b):
                pe.wait_ge(L.hid_ready, b + 1)
                for ic in range(L.IC):
                    ins = pe.transpose(bank[:, 7, tile(ic)], act_h[:, tile(ic)], ident)
                ins.then_inc(L.hid_t_ps, 1)

            def second(L, b, first_block=False):
                e = expert_of(L, b)
                pe.wait_ge(L.hid_t_ready, b + 1)
                if not first_block:
                    pe.wait_ge(L.y_ready, b)
                for ic in range(L.IC):
                    ins = pe.matmul(bank[:, 1, 0:C], hid_t[:, tile(ic)],
                                    w_second[:, bass.ds(e * (L.IC * C) + ic * C, C)],
                                    start=(ic == 0), stop=(ic == L.IC - 1))
                ins.then_inc(L.y_ps, 1)

            def blocks(L):
                pe.wait_ge(L.expert_ready, 1)
                pe.wait_ge(L.sh_y_ready, NT)
                rows_transpose(L, 0, 0, 0)
                if L.l == 0:
                    pe.wait_ge(s_fc1, 32)
                    pe.wait_ge(s_fc2, 16)
                else:
                    pe.wait_ge(s_w1a, 16 * E1)
                    pe.wait_ge(s_w1b, 16)
                first(L, 0)
                rows_transpose(L, 1, 1, 0)
                hid_transpose(L, 0)
                first(L, 1)
                rows_transpose(L, 2, 0, 1)
                second(L, 0, True)
                hid_transpose(L, 1)
                first(L, 2)
                rows_transpose(L, 3, 1, 1)
                second(L, 1)
                with pe.Fori(0, (L.NB - 3) // 2) as i:
                    for u in range(2):
                        b = i * 2 + (u + 3)
                        hid_transpose(L, b - 1)
                        first(L, b)
                        rows_transpose(L, b + 1, u, i + 2)
                        second(L, b - 1)
                hid_transpose(L, L.NB - 1)
                second(L, L.NB - 1)

            pe.wait_ge(s_const, 16)
            pe.wait_ge(chan_ready, NCH * IMAGES)
            pe.matmul(bank[0:CH, 0, 0:NCH * IMAGES], gavg, chan_mv[:, :, 0], start=True, stop=True
                      ).then_inc(gmean_ps, 1)
            pe.wait_ge(dev_ready, 1)
            pe.matmul(bank[0:CH, 0, 64:64 + NCH * IMAGES], gavg, chan_dev[:], start=True, stop=True
                      ).then_inc(gvar_ps, 1)
            for n in range(NT // 2):
                pe.wait_ge(xn_t_ready, 2 * (n + 1))
                if n >= 2:
                    pe.wait_ge(tp_out, n - 1)
                for m in range(2):
                    for k in range(NCH):
                        ins = pe.transpose(bank[:, 1 + n % 2, (m * NCH + k) * CH:(m * NCH + k + 1) * CH],
                                           xn_t[0:CH, k, tile(2 * n + m)], ident[0:CH, 0:CH])
                ins.then_inc(tp_ps, 1)
            pe.wait_ge(filled, 1)

            def moe_before(L):
                for s in plan[L.l][0]:
                    if s == 0:
                        pe.wait_ge(s_sh0 if L.l == 0 else s_sh1, 80 if L.l == 0 else 32)
                        pe.wait_ge(tp_out, NT // 2 * (1 if L.l == 0 else 3))
                    shared(L, s) if isinstance(s, int) else route(L, s)
                shared_out(L)
                blocks(L)

            moe_before(L0)

            def norm_transposes(which):
                for n in range(NT // 2):
                    pe.wait_ge(xn_tok_ready, (which - 1) * NT + 2 * (n + 1))
                    if n >= 2:
                        pe.wait_ge(tp_out, which * (NT // 2) + n - 1)
                    for k in range(NCH):
                        for m in range(2):
                            ins = pe.transpose(bank[0:CH, 1 + n % 2, (k * 2 + m) * P:(k * 2 + m + 1) * P],
                                               xn_tok[:, 2 * n + m, k * CH:(k + 1) * CH], ident)
                    ins.then_inc(tp_ps, 1)
                pe.wait_ge(tp_out, (which + 1) * (NT // 2))

            norm_transposes(1)
            pe.wait_ge(s_attw, 64)
            for n in range(2 * QKC):
                c, half = n // 2, n % 2
                if n >= 6:
                    pe.wait_ge(qk_out if n % 2 == 0 else qk_out_v, (n - 6) // 2 + 1)
                for k in range(NCH):
                    ins = pe.matmul(bank[:, n % 6, :], wqk[:, k, c, :], xn_t[0:CH, k, half * HALF:(half + 1) * HALF],
                                    start=(k == 0), stop=(k == NCH - 1))
                ins.then_inc(qk_ps, 1)
            for n in range(NT // 2):
                if n >= 2:
                    pe.wait_ge(v_out, n - 1)
                for m in range(2):
                    for k in range(NCH):
                        ins = pe.matmul(bank[:, 6 + n % 2, m * C:(m + 1) * C], xn_t[0:CH, k, tile(2 * n + m)],
                                        wv[:, k, :], start=(k == 0), stop=(k == NCH - 1))
                ins.then_inc(v_ps, 1)
            pe.wait_ge(qk_out, QKC)
            pe.wait_ge(qk_out_v, QKC)
            pe.wait_ge(v_out, NT // 2)

            def scores(n):
                img, h = n // HEADS, n % HEADS
                r = slice(ROWG * (h % 4), ROWG * (h % 4 + 1))
                if n >= 3:
                    pe.wait_ge(e1_ready, 2 * (n - 2))
                for qt in range(2):
                    q0 = img * TOKENS_IMG + qt * P
                    ins = pe.matmul(bank[:, n % 3, qt * 256:(qt + 1) * 256], qk_t[r, h // 4, q0:q0 + P],
                                    qk_t[r, QKC // 2 + h // 4, img * TOKENS_IMG:(img + 1) * TOKENS_IMG],
                                    start=True, stop=True)
                ins.then_inc(sc_ps, 1)

            def att_transpose(n):
                pe.wait_ge(att_ready, n + 1)
                if n >= 2:
                    pe.wait_ge(p2_ready, n - 1)
                for kt in range(2):
                    for qt in range(2):
                        ins = pe.transpose(bank[:, 3 + n % 2, (kt * 2 + qt) * P:(kt * 2 + qt + 1) * P],
                                           att[n % 2][:, qt, tile(kt)], ident)
                ins.then_inc(att_t_ps, 1)

            def weigh_values(n):
                img, h = n // HEADS, n % HEADS
                pe.wait_ge(p2_ready, n + 1)
                if h == 0 and img >= 2:
                    pe.wait_ge(x_new, img - 1)
                for qt in range(2):
                    for kt in range(2):
                        o = (qt * HEADS + h) * DV
                        ins = pe.matmul(bank[:, 5 + img % 2, o:o + DV], p2_t[n % 3][:, kt, tile(qt)],
                                        v_tok[:, 2 * img + kt, h, :], start=(kt == 0), stop=(kt == 1))
                ins.then_inc(av_ps, 1)

            def out_transpose(img):
                pe.wait_ge(o_ready, img + 1)
                for k in range(NCH):
                    for qt in range(2):
                        ins = pe.transpose(bank[0:CH, 7, (k * 2 + qt) * P:(k * 2 + qt + 1) * P],
                                           o_tok[:, qt, k * CH:(k + 1) * CH], ident)
                ins.then_inc(o_t_ps, 1)

            def project(img):
                pe.wait_ge(o_t_ready, img + 1)
                for qt in range(2):
                    for k in range(NCH):
                        ins = pe.matmul(bank[:, 5 + img % 2, qt * C:(qt + 1) * C], o_t[0:CH + k, k, tile(qt)],
                                        wo[0:CH + k, k, :], start=(k == 0), stop=(k == NCH - 1))
                ins.then_inc(proj_ps, 1)

            for n in range(ATT_STEPS):
                if n < N_HEADS:
                    scores(n)
                if 0 <= n - 2 < N_HEADS:
                    att_transpose(n - 2)
                if 0 <= n - 3 < N_HEADS:
                    weigh_values(n - 3)
                if n >= HEADS and (n - 5) % HEADS == 0:
                    out_transpose((n - 5) // HEADS - 1)
                if n >= HEADS and (n - 6) % HEADS == 0:
                    project((n - 6) // HEADS - 1)

            norm_transposes(2)
            moe_before(L1)


_OUT = ((4, 16, 16, C), "float32")


def kernel(**inputs):
    import concourse.bacc as bacc
    from concourse.bass_utils import run_bass_kernel_spmd

    a = {k: np.asarray(v) for k, v in inputs.items()}

    def chunks(w):
        return w.reshape(NCH, CH, -1).transpose(1, 0, 2)

    x = a["x"].reshape(T, C)
    qkv = a["L1_attn_w_qkv"].reshape(3, HEADS, D, C)
    qk = np.zeros((2, HEADS, ROWG, C), np.float32)
    qk[:, :, 0:D] = qkv[0:2]
    arrays = {
        "x": x,
        "x_t": chunks(x.T),
        "const": constants(),
        "gate0": chunks(a["L0_conv_gate_w"].T),
        "w13": np.stack([chunks(a["L0_conv_w1_w"].T), chunks(a["L0_conv_w3_w"].T)], 2),
        "b13": np.stack([a["L0_conv_w1_b"].reshape(-1, P).T, a["L0_conv_w3_b"].reshape(-1, P).T], 1),
        "w2": a["L0_conv_w2_w"].T.reshape(I0 // P, P, C).transpose(1, 0, 2),
        "fc2_b": a["L0_conv_fc2_b"],
        "w2_b": a["L0_conv_w2_b"].reshape(1, C),
        "fc1": a["L0_conv_fc1_w"].transpose(2, 0, 1).reshape(NCH, CH, E0, I0).transpose(1, 2, 0, 3),
        "fc1_b": a["L0_conv_fc1_b"].reshape(1, E0, I0),
        "fc2": a["L0_conv_fc2_w"].transpose(2, 0, 1).reshape(I0 // P, P, E0, C).transpose(1, 2, 0, 3)
        .reshape(P, -1),
        "wqk": chunks(qk.reshape(-1, C).T).reshape(CH, NCH, QKC, P),
        "wv": chunks(a["L1_attn_w_qkv"][2 * C:].T),
        "wo": chunks(a["L1_attn_w_out"].T),
        "b_out": a["L1_attn_b_out"].reshape(1, C),
        "gate1": chunks(a["L1_ffn_w_gate"]),
        "bias1": a["L1_ffn_expert_bias"].reshape(1, E1),
        "gate_up": np.stack([a["L1_ffn_wg"], a["L1_ffn_wu"]], 0).reshape(2, E1, NCH, CH, I1)
        .transpose(3, 1, 2, 0, 4),
        "down": a["L1_ffn_wd"].reshape(E1, I1 // P, P, C).transpose(2, 0, 1, 3).reshape(P, -1),
        "sh1": np.stack([chunks(a["L1_ffn_swg"]), chunks(a["L1_ffn_swu"])], 2),
        "sh1d": a["L1_ffn_swd"].reshape(I1 // P, P, C).transpose(1, 0, 2),
    }
    arrays = {k: np.ascontiguousarray(v) for k, v in arrays.items()}
    nc = bacc.Bacc("TRN2", target_bir_lowering=False, num_devices=1)
    d = {k: nc.dram_tensor(f"in_{k}", v.shape, mybir.dt.from_np(v.dtype), kind="ExternalInput").ap()
         for k, v in arrays.items()}
    out = nc.dram_tensor("out_0", (T, C), F32, kind="ExternalOutput").ap()
    build(nc, d, out)
    r = run_bass_kernel_spmd(nc, [{f"in_{k}": v for k, v in arrays.items()}], core_ids=[0])
    return r.results[0]["out_0"].reshape(_OUT[0])
```

```python
from contextlib import ExitStack

import numpy as np

import concourse.bass as bass
from concourse import mybir

ALU = mybir.AluOpType
ACT = mybir.ActivationFunctionType
AXX = mybir.AxisListType.X
F32 = mybir.dt.float32
F32R = mybir.dt.float32r
I32 = mybir.dt.int32
U32 = mybir.dt.uint32

P = 128
IMAGES, TOKENS_IMG = 4, 256
T = IMAGES * TOKENS_IMG
NT = T // P
C = 192
CH = 96
NCH = C // CH
GROUP = C // 32
HEADS, D = 12, 16
HG = 32
HPC = P // HG
HC = HEADS // HPC
QKC = 2 * HC
TOPK = 2
E0, I0 = 8, 512
E1, I1 = 16, 384
NB0 = TOPK * T // P + E0 - 1
NB1 = TOPK * T // P + E1 - 1
OUT_OF_BOUNDS = 4096

C_IDENT = 0
C_TRI = C_IDENT + P
C_IOTA = C_TRI + P
C_GAVG = C_IOTA + P
C_MASK = C_GAVG + CH
C_TOK1 = C_MASK + TOKENS_IMG
C_BLK = C_TOK1 + NT
C_SUBT = C_BLK + NB1 + 1
C_SUM = C_SUBT + NT * E1
C_LOW = C_SUM + P
C_ALL = C_LOW + 1


def constants():
    c = np.zeros((P, C_ALL), np.float32)
    n = np.arange(P)
    c[:, C_IDENT:C_IDENT + P] = np.eye(P)
    c[:, C_TRI:C_TRI + P] = n[:, None] < n[None, :]
    c[:, C_IOTA:C_IOTA + P] = n[None, :]
    g = np.arange(CH) // GROUP
    c[:CH, C_GAVG:C_GAVG + CH] = (g[:, None] == g[None, :]) / GROUP
    k = np.arange(TOKENS_IMG)
    c[:, C_MASK:C_MASK + TOKENS_IMG] = np.where(n[:, None] % 64 == k[None, :] % 64, 0.5, 1.0)
    c[:, C_TOK1:C_TOK1 + NT] = P * np.arange(NT)[None, :] + n[:, None] + 1
    c[:, C_BLK:C_BLK + NB1 + 1] = P * np.arange(NB1 + 1)[None, :]
    e = np.arange(E1)
    c[:E1, C_SUBT:C_SUBT + NT * E1] = np.tile(e[:, None] < e[None, :], (1, NT))
    c[:, C_SUM:C_SUM + P] = n[:, None] == n[None, :] // HG * HG + D
    c[:, C_LOW] = -1.0 * (n % HG >= D)
    return c


class Layer:

    def __init__(self, n, experts, blocks, inner, hid, sem):
        self.l, self.E, self.NB, self.I, self.IC, self.hid = n, experts, blocks, inner, inner // P, hid
        self.sh_stored = [sem(f"L{n}_sh_stored{i}") for i in range(2)]
        self.rows_in = [sem(f"L{n}_rows_in{i}") for i in range(2)]
        self.logits_ps = sem(f"L{n}_logits_ps")
        self.gap_ready = sem(f"L{n}_gap_ready")
        self.gap_exp = sem(f"L{n}_gap_exp")
        self.prefix_ready = sem(f"L{n}_prefix_ready")
        self.count_ps = sem(f"L{n}_count_ps")
        self.pads_ready = sem(f"L{n}_pads_ready")
        self.rank_ps = sem(f"L{n}_rank_ps")
        self.ended_ready = sem(f"L{n}_ended_ready")
        self.expert_ps = sem(f"L{n}_expert_ps")
        self.expert_ready = sem(f"L{n}_expert_ready")
        self.in_blk_ready = sem(f"L{n}_in_blk_ready")
        self.at_place_ready = sem(f"L{n}_at_place_ready")
        self.slots_ps = sem(f"L{n}_slots_ps")
        self.slots_ready = sem(f"L{n}_slots_ready")
        self.comb_ready = sem(f"L{n}_comb_ready")
        self.comb_ps = sem(f"L{n}_comb_ps")
        self.comb_out = sem(f"L{n}_comb_out")
        self.sh_a_ps = sem(f"L{n}_sh_a_ps")
        self.sh_c_ps = sem(f"L{n}_sh_c_ps")
        self.sh_g_ready = sem(f"L{n}_sh_g_ready")
        self.sh_h_ready = sem(f"L{n}_sh_h_ready")
        self.sh_y_ps = sem(f"L{n}_sh_y_ps")
        self.sh_y_ready = sem(f"L{n}_sh_y_ready")
        self.rows_t_ps = sem(f"L{n}_rows_t_ps")
        self.rows_t_ready = sem(f"L{n}_rows_t_ready")
        self.first_ps = sem(f"L{n}_first_ps")
        self.up_ps = sem(f"L{n}_up_ps")
        self.gate_act = sem(f"L{n}_gate_act")
        self.hid_ready = sem(f"L{n}_hid_ready")
        self.hid_t_ps = sem(f"L{n}_hid_t_ps")
        self.hid_t_ready = sem(f"L{n}_hid_t_ready")
        self.y_ps = sem(f"L{n}_y_ps")
        self.y_ready = sem(f"L{n}_y_ready")
        self.added = sem(f"L{n}_added")


def build(nc, d, out):
    with ExitStack() as ctx:
        def sb(name, shape, dt=F32):
            return ctx.enter_context(nc.sbuf_tensor(name, shape, dt))

        def sem(name):
            return ctx.enter_context(nc.semaphore(name))

        bank = ctx.enter_context(nc.psum_tensor("bank", [P, 8, 512], F32))

        xn_rows = [nc.dram_tensor(f"xn_rows{l}", [T, C], F32).ap() for l in range(2)]
        sum0 = nc.dram_tensor("sum0", [T, C], F32).ap()

        def by_tile(ap):
            return ap.rearrange("(j p) c -> p j c", p=P)

        const = sb("const", [P, C_ALL])
        ident = const[:, C_IDENT:C_IDENT + P]
        tri = const[:, C_TRI:C_TRI + P]
        iota = const[:, C_IOTA:C_IOTA + P]
        gavg = const[0:CH, C_GAVG:C_GAVG + CH]
        mask = const[:, C_MASK:C_MASK + TOKENS_IMG]
        tok1 = const[:, C_TOK1:C_TOK1 + NT]
        blk_start = const[:, C_BLK:C_BLK + NB1 + 1]
        sum_row = const[:, C_SUM:C_SUM + P]
        minus_low = const[:, C_LOW:C_LOW + 1]

        ones = sb("ones", [P, P])
        with nc.sbuf_tensor("w_first", [P, E1 * NCH * 2 * I1], F32) as w_first:
            pass
        wg_up = w_first[0:CH, :].rearrange("p (e k g i) -> p e k g i", e=E1, k=NCH, g=2)
        fc1 = w_first[0:CH + 1, 0:E0 * NCH * I0].rearrange("p (e k i) -> p e k i", e=E0, k=NCH)
        o = E0 * NCH * I0
        w13 = w_first[0:CH, o:o + NCH * 2 * I0].rearrange("p (k g i) -> p k g i", k=NCH, g=2)
        o += NCH * 2 * I0
        w2 = w_first[:, o:o + (I0 // P) * C].rearrange("p (i c) -> p i c", c=C)
        o += (I0 // P) * C
        hid0 = w_first[:, o:o + (I0 // P) * T].rearrange("p (i t) -> p i t", t=T)
        o += (I0 // P) * T
        x_t = w_first[0:CH, o:o + NCH * T].rearrange("p (k t) -> p k t", t=T)
        o += NCH * T
        a_end = E1 * NCH * 2 * I1
        a = a_end - (NCH * QKC * P + NCH * C)
        wqk = w_first[0:CH, a:a + NCH * QKC * P].rearrange("p (k c m) -> p k c m", k=NCH, c=QKC)
        wv = w_first[0:CH, a + NCH * QKC * P:a_end].rearrange("p (k c) -> p k c", k=NCH)
        a -= HC * C
        wo = w_first[:, a:a + HC * C].rearrange("p (k c) -> p k c", k=HC)
        a -= NT * HEADS * HG
        v_tok = w_first[:, a:a + NT * HEADS * HG].rearrange("p (j h d) -> p j h d", j=NT, h=HEADS)
        assert o <= a
        a -= HC * TOKENS_IMG
        o_t = w_first[:, a:a + HC * TOKENS_IMG].rearrange("p (k t) -> p k t", k=HC)
        a -= 2 * TOKENS_IMG
        o_raw = w_first[:, a:a + 2 * TOKENS_IMG].rearrange("p (k t) -> p k t", k=2)
        behind = a_end - a
        a -= 3 * HC * T
        sb("before_attention", [P, a])
        q_parts = sb("q_parts", [P, HC, T], F32R)
        k_high = sb("k_high", [P, HC, T], F32R)
        k_low = sb("k_low", [P, HC, T], F32R)
        sb("behind_scores", [P, behind])
        w_second = sb("w_second", [P, E1 * (I1 // P) * C])
        fc2 = w_second[:, 0:E0 * (I0 // P) * C]
        per_expert = NCH * 2 * I1
        EARLY = a // per_expert
        LATE = E1 - 2
        hid1 = w_first[:, LATE * per_expert:].rearrange("p (i t) -> p i t", t=T)
        comb_t = w_second[0:E0 + 1, E0 * (I0 // P) * C:E0 * (I0 // P) * C + T]
        scratch = sb("scratch", [P, 4096])

        def scratch_at(o, *dims):
            n = int(np.prod(dims))
            ap = scratch[:, o:o + n]
            return ap.rearrange("p (a b) -> p a b", a=dims[0]) if len(dims) == 2 else ap.rearrange(
                "p (a b c) -> p a b c", a=dims[0], b=dims[1])

        x_tok = sb("x_tok", [P, NT, C])
        xn_tok = sb("xn_tok", [P, NT, C])
        xn_t = sb("xn_t", [CH + 1, NCH, T])
        chan_stats = sb("chan_stats", [CH, NCH * IMAGES, 6])
        chan_mv = sb("chan_mv", [CH, NCH * IMAGES, 2])
        grp_mean = sb("grp_mean", [CH, NCH * IMAGES])
        chan_dev = sb("chan_dev", [CH, NCH * IMAGES])
        grp_rstd = sb("grp_rstd", [CH, NCH * IMAGES])
        tok_stats = sb("tok_stats", [P, NT, 6])
        tok_mv = sb("tok_mv", [P, NT, 2])
        tok_rstd = sb("tok_rstd", [P, NT])

        gate_w = [sb("gate0", [CH, NCH, E0]), sb("gate1", [CH + 1, NCH, E1])]
        b13 = sb("b13", [P, 2, I0 // P])
        b2 = sb("b2", [E0 + 1, C])
        sh1 = sb("sh1", [CH, NCH, 2, I1])
        sh1d = sb("sh1d", [P, I1 // P, C])

        logit = sb("logit", [P, NT, E1])
        top8 = sb("top8", [P, NT, 8])
        top8i = sb("top8i", [P, NT, 8], U32)
        choice = sb("choice", [P, NT, TOPK])
        gap = sb("gap", [P, NT])
        gap_e = sb("gap_e", [P, NT])
        gap_1 = sb("gap_1", [P, NT])
        weight = sb("weight", [P, TOPK, NT])
        picked = sb("picked", [P, TOPK, NT, E1])
        comb = sb("comb", [P, NT, E0 + 1])
        comb_a = sb("comb_a", [P, NT, E0])
        before = sb("before", [P, NT + 1, E1])
        count_i = sb("count_i", [E1, 1], I32)
        count_i2 = sb("count_i2", [E1, 1], I32)
        padded = sb("padded", [E1, 1])
        padded_b = sb("padded_b", [E1, P])
        ended = sb("ended", [E1, NB1 + 1])
        blk_expert = sb("blk_expert", [1, NB1 + 1], I32)
        at_pick = sb("at_pick", [P, NT, E1])
        slot = sb("slot", [P, TOPK, NT])
        slot_i = sb("slot_i", [P, TOPK * NT], I32)
        slot_j = sb("slot_j", [P, 2, TOPK * NT], I32)
        slot_f = sb("slot_f", [P, 2, TOPK * NT])
        at_place = scratch_at(0, TOPK * NT, P)
        in_blk = scratch_at(TOPK * NT * P, TOPK * NT, 2, NB1 + 1)
        eq_blk = scratch_at(TOPK * NT * (P + 2 * NB1 + 2), TOPK * NT, NB1 + 1)
        empty = sb("empty", [P, NB1 + 1])
        slot_tok = sb("slot_tok", [P, NB1 + 1], I32)
        slot_w = sb("slot_w", [P, NB1 + 1])

        rows = [sb(f"rows{i}", [P, C]) for i in range(2)]
        rows_t = sb("rows_t", [CH + 1, NCH, P])
        act_h = sb("act_h", [P, I0])
        act_g = sb("act_g", [P, I1])
        hid_t = sb("hid_t", [P, I0])
        y = [sb(f"y{i}", [P, C]) for i in range(2)]
        g_sh = [sb(f"g_sh{i}", [P, 512]) for i in range(2)]
        y_sh = [sb(f"y_sh{i}", [P, C]) for i in range(2)]

        neg_max = sb("neg_max", [P, 4, 2])
        exp_sum = sb("exp_sum", [P, 4, 2])
        exp_inv = sb("exp_inv", [P, 2, 2])
        q_high = scratch[:, 0:2 * 512].bitcast(F32R).rearrange("p (a t) -> p a t", a=2)
        e1 = [scratch_at(512 * i, 2, TOKENS_IMG) for i in range(3)]
        att = [scratch_at(512 * (3 + i), 2, TOKENS_IMG) for i in range(2)]
        p2_t = [scratch_at(512 * (5 + i), 2, TOKENS_IMG) for i in range(3)]

        s_const, s_x, s_gate0, s_sh0, s_fc1, s_fc2 = (sem(n) for n in (
            "const_loaded", "x_loaded", "gate0_loaded", "shared0_loaded", "fc1_loaded", "fc2_loaded"))
        s_attw, s_gate1, s_sh1, s_w1a, s_w1b = (sem(n) for n in (
            "attn_w_loaded", "gate1_loaded", "shared1_loaded", "gate_up_loaded", "down_loaded"))
        filled = sem("fills_done")
        x_tok_in = sem("x_tok_loaded")
        act_c, dve_c, pool_c = sem("act_own"), sem("dve_own"), sem("pool_own")
        chan_ready, dev_ready = sem("chan_stats_ready"), sem("chan_dev_ready")
        gmean_ps, gvar_ps = sem("group_mean_in_psum"), sem("group_var_in_psum")
        var_ready, std_ready = sem("var_ready"), sem("std_ready")
        xn_t_ready = sem("xn_t_ready")
        tp_ps = sem("norm_transposed_in_psum")
        tp_out = sem("norm_transposes_copied")
        xn_stored = sem("xn_rows_stored")
        xn_tok_ready = sem("xn_tok_ready")
        sum_ready = sem("sum0_loaded")

        layers = []
        for l, (E, NB, I) in enumerate(((E0, NB0, I0), (E1, NB1, I1))):
            layers.append(Layer(l, E, NB, I, (hid0, hid1)[l], sem))
        L0, L1 = layers

        qk_ps, v_ps, v_out = sem("qk_in_psum"), sem("v_in_psum"), sem("v_copied")
        high_ready, parts_ready = sem("qk_high_part_ready"), sem("qk_parts_ready")
        sc_ps, nmax_ready, e1_ready, att_ready = (
            sem("scores_in_psum"), sem("neg_max_ready"), sem("exp_ready"), sem("att_ready"))
        att_t_ps, p2_ready, av_ps = sem("att_t_in_psum"), sem("p2_ready"), sem("av_in_psum")
        o_raw_ready, sums_ps, o_ready, proj_ps, x_new = (
            sem("o_raw_ready"), sem("sums_in_psum"), sem("o_ready"), sem("proj_in_psum"), sem("x_updated"))
        out_done = sem("out_stored")

        def chained(eng, s):
            n = [0]

            def step(ins):
                n[0] += 1
                ins.then_inc(s, 1)

            def join():
                eng.wait_ge(s, n[0])

            def go(ins):
                step(ins)
                join()
            return step, join, go

        N_HEADS = IMAGES * HEADS
        ATT_STEPS = N_HEADS + 8

        def chunk_at(n, lag):
            c = (n - lag + 1) // HPC - 1
            return c if (n - lag + 1) % HPC == 0 and 0 <= c < N_HEADS // HPC else None

        HALF = T // 2
        plan = {
            0: (["logits", 0, 1, "count", 2, "rank", 3, "expert", 4, 5, "slots", 6, 7],
                ["top2", 0, 1, "pads", 2, "ended", 3, "expert", "place", 4, 5, "slots", 6, 7]),
            1: (["logits", 0, 1, "count", 2, "rank", 3, "expert", 4, "slots", 5],
                ["top2", 0, 1, "pads", 2, "ended", 3, "expert", "place", 4, "slots", 5]),
        }

        def bc(ap, axis, shape):
            return ap.unsqueeze(axis).to_broadcast(shape)

        block = ctx.enter_context(nc.Block())

        @block.sync
        def _(sp):
            sp.dma_start(x_t, d["x_t"]).then_inc(s_x, 16)
            sp.dma_start(const[:], d["const"]).then_inc(s_const, 16)
            sp.dma_start(gate_w[0][:], d["gate0"]).then_inc(s_gate0, 16)
            sp.dma_start(w13, d["w13"]).then_inc(s_sh0, 16)
            sp.dma_start(b13[:], d["b13"]).then_inc(s_sh0, 16)
            sp.dma_start(w2, d["w2"]).then_inc(s_sh0, 16)
            sp.dma_start(b2[0:E0, :], d["fc2_b"]).then_inc(s_sh0, 16)
            sp.dma_start(b2[E0:E0 + 1, :], d["w2_b"]).then_inc(s_sh0, 16)
            sp.dma_start(x_tok[:], by_tile(d["x"])).then_inc(x_tok_in, 16)
            sp.dma_start(fc1[0:CH], d["fc1"]).then_inc(s_fc1, 16)
            sp.dma_start(fc1[CH:CH + 1, :, 1, :], d["fc1_b"]).then_inc(s_fc1, 16)
            sp.dma_start(fc2, d["fc2"]).then_inc(s_fc2, 16)
            sp.wait_ge(tp_out, NT // 2)
            sp.dma_start(by_tile(xn_rows[0]), xn_tok[:]).then_inc(xn_stored, 16)
            sp.dma_start(wqk, d["wqk"]).then_inc(s_attw, 16)
            sp.dma_start(wv, d["wv"]).then_inc(s_attw, 16)
            sp.dma_start(wo, d["wo"]).then_inc(s_attw, 16)
            sp.dma_start(gate_w[1][0:CH], d["gate1"]).then_inc(s_gate1, 16)
            sp.dma_start(gate_w[1][CH:CH + 1, 1, :], d["bias1"]).then_inc(s_gate1, 16)
            sp.dma_start(sh1[:], d["sh1"]).then_inc(s_sh1, 16)
            sp.dma_start(sh1d[:], d["sh1d"]).then_inc(s_sh1, 16)
            for j in range(NT):
                sp.wait_ge(L0.sh_y_ready, j + 1)
                sp.dma_start(sum0[j * P:(j + 1) * P], y_sh[j % 2][:]).then_inc(L0.sh_stored[j % 2], 16)
            sp.wait_ge(L0.added, 16 * NB0)
            sp.dma_start(x_tok[:], by_tile(sum0)).then_inc(sum_ready, 16)
            sp.wait_ge(L0.y_ps, NB0)
            for e in range(EARLY):
                sp.dma_start(wg_up[:, e], d["gate_up"][:, e]).then_inc(s_w1a, 16)
            sp.dma_start(w_second[:], d["down"]).then_inc(s_w1b, 16)
            sp.wait_ge(xn_tok_ready, 2 * NT)
            sp.dma_start(by_tile(xn_rows[1]), xn_tok[:]).then_inc(xn_stored, 16)
            for e in range(EARLY, LATE):
                sp.dma_start(wg_up[:, e], d["gate_up"][:, e]).then_inc(s_w1a, 16)
            for j in range(NT):
                sp.wait_ge(L1.sh_y_ready, j + 1)
                sp.dma_start(out[j * P:(j + 1) * P], y_sh[j % 2][:]).then_inc(L1.sh_stored[j % 2], 16)
            for e in range(LATE, E1):
                sp.dma_start(wg_up[:, e], d["gate_up"][:, e]).then_inc(s_w1a, 16)
            sp.wait_ge(L1.added, 16 * NB1)

        def pool_blocks(pool, L, target):
            pool.wait_ge(L.slots_ready, 1)
            pool.wait_ge(xn_stored, 16 * (L.l + 1))

            def gather(b):
                pool.indirect_dma_start(
                    rows[b % 2][:], None, xn_rows[L.l],
                    bass.IndirectOffsetOnAxis(slot_tok[:, b:b + 1].bitcast(U32), 0),
                    bounds_check=T - 1, oob_is_err=False).then_inc(L.rows_in[b % 2], 16)

            def add(b):
                pool.wait_ge(L.y_ready, b + 1)
                if b:
                    pool.wait_ge(L.added, b * 16)
                pool.indirect_dma_start(
                    target, bass.IndirectOffsetOnAxis(slot_tok[:, b:b + 1].bitcast(U32), 0), y[b % 2][:], None,
                    bounds_check=T - 1, oob_is_err=False, compute_op=ALU.add).then_inc(L.added, 16)

            AHEAD = 4
            for b in range(AHEAD):
                if b >= 2:
                    pool.wait_ge(L.rows_t_ps, b - 1)
                gather(b)
            for s in L.sh_stored:
                pool.wait_ge(s, 16 * NT // 2)
            for b in range(L.NB):
                add(b)
                if b + AHEAD <= L.NB:
                    pool.wait_ge(L.rows_t_ps, b + AHEAD - 1)
                    gather(b + AHEAD)

        @block.gpsimd
        def _(pool):
            fills = [(ones[:], 1.0), (rows[0][:], 0.0), (rows[1][:], 0.0), (comb[:, :, E0:E0 + 1], 1.0),
                     (xn_t[CH:CH + 1, 1, :], 1.0), (rows_t[CH:CH + 1, 1, :], 1.0),
                     (v_tok[:, :, :, D:HG], 0.0), (v_tok[:, :, :, D:D + 1], 1.0),
                     (before[:, 0, :], 0.0)]
            for n, (ap, v) in enumerate(fills):
                nc.gpsimd.memset(ap, v).then_inc(pool_c, 1)
                pool.wait_ge(pool_c, n + 1)
            pool.sem_inc(filled, 1)
            pool_blocks(pool, L0, sum0)
            pool_blocks(pool, L1, out)

        def act_norm_transposes(act, which):
            for n in range(NT // 2):
                act.wait_ge(tp_ps, which * (NT // 2) + n + 1)
                src = bank[:, 1 + n % 2, :]
                if which == 0:
                    ins = nc.scalar.copy(xn_tok[:, 2 * n:2 * n + 2, :],
                                         src[:, 0:2 * C].rearrange("p (j c) -> p j c", c=C))
                else:
                    ins = nc.scalar.copy(xn_t[0:CH, :, 2 * n * P:(2 * n + 2) * P],
                                         src[0:CH].rearrange("p (k t) -> p k t", k=NCH))
                ins.then_inc(tp_out, 1)

        def act_shared(act, L, s):
            ic = s % L.IC
            act.wait_ge(L.sh_a_ps, s + 1)
            if s >= 2:
                act.wait_ge(L.sh_h_ready, s - 1)
            if L.l == 0:
                ins = nc.scalar.activation(g_sh[s % 2][:], bank[:, 4 + s % 2, :], ACT.Gelu,
                                           bias=b13[:, 0, ic:ic + 1])
            else:
                ins = nc.scalar.activation(g_sh[s % 2][:], bank[:, 4 + s % 2, :], ACT.Silu)
            ins.then_inc(L.sh_g_ready, 1)

        def act_rows(act, L, b):
            act.wait_ge(L.rows_t_ps, b + 1)
            nc.scalar.copy(rows_t[0:CH], bank[0:CH, 0, 0:NCH * P].rearrange("p (k t) -> p k t", k=NCH)
                           ).then_inc(L.rows_t_ready, 1)

        def act_block(act, L, b):
            act.wait_ge(L.first_ps, b + 1)
            if L.l == 0:
                nc.scalar.activation(act_h[:], bank[:, 5, :], ACT.Gelu).then_inc(L.hid_ready, 1)
            else:
                if not isinstance(b, int) or b > 0:
                    act.wait_ge(L.hid_ready, b)
                nc.scalar.activation(act_g[:], bank[:, 5, 0:I1], ACT.Silu).then_inc(L.gate_act, 1)

        def act_blocks(act, L):
            act_rows(act, L, 0)
            act_block(act, L, 0)
            act_rows(act, L, 1)
            with act.Fori(0, (L.NB - 1) // 2) as i:
                for u in range(2):
                    b = i * 2 + (u + 1)
                    act_block(act, L, b)
                    act_rows(act, L, b + 1)

        @block.scalar
        def _(act):
            act.wait_ge(var_ready, 1)
            nc.scalar.sqrt(grp_rstd[:], grp_rstd[:]).then_inc(std_ready, 1)
            act_norm_transposes(act, 0)
            act.wait_ge(L0.gap_ready, 1)
            nc.scalar.activation(gap_e[:], gap[:], ACT.Exp).then_inc(L0.gap_exp, 1)
            for s in range(2 * L0.IC):
                act_shared(act, L0, s)
            act_blocks(act, L0)

            act.wait_ge(var_ready, 2)
            nc.scalar.sqrt(tok_rstd[:], tok_rstd[:]).then_inc(std_ready, 1)
            act_norm_transposes(act, 1)
            for n in range(2 * QKC):
                c, half = n // 2, n % 2
                act.wait_ge(qk_ps, n + 1)
                if c < HC:
                    if n >= 2:
                        act.wait_ge(parts_ready, n - 1)
                    ins = nc.scalar.copy(q_high[:, n % 2, :], bank[:, n % 6, :])
                else:
                    ins = nc.scalar.mul(k_high[:, c - HC, half * HALF:(half + 1) * HALF], bank[:, n % 6, :],
                                        D ** -0.5)
                ins.then_inc(high_ready, 1)

            def exp_scores(n):
                act.wait_ge(nmax_ready, n + 1)
                if n >= 3:
                    act.wait_ge(att_ready, n - 2)
                for qt in range(2):
                    nc.scalar.activation(e1[n % 3][:, qt, :], bank[:, n % 3, qt * 256:(qt + 1) * 256], ACT.Exp,
                                         bias=neg_max[:, n % 4, qt:qt + 1],
                                         accum_out=exp_sum[:, n % 4, qt:qt + 1]).then_inc(e1_ready, 1)

            def exp_att(n):
                act.wait_ge(att_t_ps, n + 1)
                if n >= 3:
                    act.wait_ge(av_ps, n - 2)
                nc.scalar.activation(p2_t[n % 3][:].rearrange("p a b -> p (a b)"), bank[:, 3 + n % 2, :],
                                     ACT.Exp).then_inc(p2_ready, 1)

            for n in range(N_HEADS + 2):
                if n < N_HEADS:
                    exp_scores(n)
                if n >= 2:
                    exp_att(n - 2)

            act.wait_ge(var_ready, 3)
            nc.scalar.sqrt(tok_rstd[:], tok_rstd[:]).then_inc(std_ready, 1)
            act_norm_transposes(act, 2)
            act.wait_ge(L1.gap_ready, 1)
            nc.scalar.activation(gap_e[:], gap[:], ACT.Exp).then_inc(L1.gap_exp, 1)
            for s in range(2 * L1.IC):
                act_shared(act, L1, s)
            act_blocks(act, L1)

        @block.vector
        def _(dve):
            v = nc.vector
            step, join, go = chained(dve, dve_c)

            dve.wait_ge(s_x, 16)
            for k in range(NCH):
                for img in range(IMAGES):
                    step(v.bn_stats(chan_stats[:, k * IMAGES + img, :],
                                    x_t[:, k, img * TOKENS_IMG:(img + 1) * TOKENS_IMG]))
            join()
            for n in range(NCH * IMAGES):
                v.bn_aggr(chan_mv[:, n, :], chan_stats[:, n, :]).then_inc(chan_ready, 1)
            dve.wait_ge(gmean_ps, 1)
            go(v.tensor_copy(grp_mean[:], bank[0:CH, 0, 0:NCH * IMAGES]))
            go(v.tensor_tensor(chan_dev[:], chan_mv[:, :, 0], grp_mean[:], ALU.subtract))
            go(v.tensor_tensor(chan_dev[:], chan_dev[:], chan_dev[:], ALU.mult))
            v.tensor_tensor(chan_dev[:], chan_dev[:], chan_mv[:, :, 1], ALU.add).then_inc(dev_ready, 1)
            dve.wait_ge(gvar_ps, 1)
            v.tensor_scalar(grp_rstd[:], bank[0:CH, 0, 64:64 + NCH * IMAGES], 1e-5, None, ALU.add
                            ).then_inc(var_ready, 1)
            dve.wait_ge(std_ready, 1)
            go(v.reciprocal(grp_rstd[:], grp_rstd[:]))
            for img in range(IMAGES):
                for k in range(NCH):
                    n = k * IMAGES + img
                    span = slice(img * TOKENS_IMG, (img + 1) * TOKENS_IMG)
                    v.tensor_scalar(xn_t[0:CH, k, span], x_t[:, k, span], grp_mean[:, n:n + 1],
                                    grp_rstd[:, n:n + 1], ALU.subtract, ALU.mult).then_inc(xn_t_ready, 1)

            def route(L, stage):
                E, NBP = L.E, L.NB + 1
                if stage == "top2":
                    dve.wait_ge(L.logits_ps, 1)
                    lg = logit[:, :, 0:E]
                    go(v.tensor_copy(lg, bank[:, 3, 0:NT * E].rearrange("p (j e) -> p j e", e=E)))
                    for j in range(NT):
                        step(v.max(top8[:, j, :], logit[:, j, 0:E]))
                    join()
                    for j in range(NT):
                        step(v.max_index(top8i[:, j, :], top8[:, j, :], logit[:, j, 0:E]))
                    v.tensor_tensor(gap[:], top8[:, :, 1], top8[:, :, 0], ALU.subtract).then_inc(L.gap_ready, 1)
                    join()
                    go(v.tensor_copy(choice[:], top8i[:, :, 0:TOPK]))
                    iota_e = bc(iota[:, 0:E], 1, [P, NT, E])
                    for k in range(TOPK):
                        step(v.tensor_tensor(picked[:, k, :, 0:E], iota_e,
                                             bc(choice[:, :, k], 2, [P, NT, E]), ALU.is_equal))
                    join()
                    go(v.tensor_tensor(at_pick[:, :, 0:E], picked[:, 0, :, 0:E], picked[:, 1, :, 0:E], ALU.add))
                    dve.wait_ge(filled, 1)
                    for j in range(NT):
                        ins = v.tensor_tensor(before[:, j + 1, 0:E], before[:, j, 0:E], at_pick[:, j, 0:E], ALU.add)
                        if j < NT - 1:
                            go(ins)
                    ins.then_inc(L.prefix_ready, 1)
                    dve.wait_ge(L.gap_exp, 1)
                    go(v.tensor_scalar(gap_1[:], gap_e[:], 1.0, None, ALU.add))
                    go(v.reciprocal(weight[:, 0, :], gap_1[:]))
                    go(v.tensor_tensor(weight[:, 1, :], gap_e[:], weight[:, 0, :], ALU.mult))
                    if L.l == 0:
                        w = [bc(weight[:, k, :], 2, [P, NT, E]) for k in range(TOPK)]
                        go(v.tensor_tensor(comb_a[:], picked[:, 0, :, 0:E], w[0], ALU.mult))
                        go(v.tensor_tensor(comb[:, :, 0:E], picked[:, 1, :, 0:E], w[1], ALU.mult))
                        v.tensor_tensor(comb[:, :, 0:E], comb[:, :, 0:E], comb_a[:], ALU.add
                                        ).then_inc(L.comb_ready, 1)
                elif stage == "pads":
                    dve.wait_ge(L.count_ps, 1)
                    go(v.tensor_scalar(count_i[0:E], bank[0:E, 3, 256:257], float(P - 1), None, ALU.add))
                    go(v.tensor_scalar(count_i2[0:E], count_i[0:E], 7, 7, ALU.arith_shift_right,
                                       ALU.arith_shift_left))
                    go(v.tensor_copy(padded[0:E], count_i2[0:E]))
                    v.tensor_scalar(padded_b[0:E], ones[0:E, :], padded[0:E, 0:1], None, ALU.mult
                                    ).then_inc(L.pads_ready, 1)
                elif stage == "ended":
                    dve.wait_ge(L.rank_ps, 1)
                    go(v.tensor_copy(padded[0:E], bank[0:E, 3, 260:261]))
                    v.tensor_scalar(ended[0:E, 0:NBP], blk_start[0:E, 0:NBP], padded[0:E, 0:1], None,
                                    ALU.is_ge).then_inc(L.ended_ready, 1)
                    rank = bank[:, 7, 0:NT * E].rearrange("p (j e) -> p j e", e=E)
                    for k in range(TOPK):
                        go(v.tensor_tensor(at_pick[:, :, 0:E], picked[:, k, :, 0:E], rank, ALU.mult))
                        go(v.tensor_reduce(slot[:, k, :], at_pick[:, :, 0:E], AXX, ALU.add))
                    go(v.tensor_copy(slot_i[:], slot[:].rearrange("p k j -> p (k j)")))
                    step(v.tensor_scalar(slot_j[:, 0, :], slot_i[:], P - 1, None, ALU.bitwise_and))
                    step(v.tensor_scalar(slot_j[:, 1, :], slot_i[:], 7, None, ALU.arith_shift_right))
                    join()
                    go(v.tensor_copy(slot_f[:], slot_j[:]))
                elif stage == "expert":
                    dve.wait_ge(L.expert_ps, 1)
                    v.tensor_scalar(blk_expert[:, 0:NBP], bank[0:1, 3, 264:264 + NBP], float(E - 1), None,
                                    ALU.min).then_inc(L.expert_ready, 1)
                elif stage == "place":
                    n = TOPK * NT
                    go(v.tensor_tensor(eq_blk[:, :, 0:NBP], bc(iota[:, 0:NBP], 1, [P, n, NBP]),
                                       bc(slot_f[:, 1, :], 2, [P, n, NBP]), ALU.is_equal))
                    for k in range(TOPK):
                        s = slice(k * NT, (k + 1) * NT)
                        v.tensor_tensor(in_blk[:, s, 0, 0:NBP], eq_blk[:, s, 0:NBP],
                                        bc(tok1, 2, [P, NT, NBP]), ALU.mult).then_inc(L.in_blk_ready, 1)
                        v.tensor_tensor(in_blk[:, s, 1, 0:NBP], eq_blk[:, s, 0:NBP],
                                        bc(weight[:, k, :], 2, [P, NT, NBP]), ALU.mult
                                        ).then_inc(L.in_blk_ready, 1)
                    for m in range(n):
                        v.tensor_scalar(at_place[:, m, :], iota, slot_f[:, 0, m:m + 1], None, ALU.is_equal
                                        ).then_inc(L.at_place_ready, 1)
                elif stage == "slots":
                    dve.wait_ge(L.slots_ps, 1)
                    sm = bank[:, 6, 0:2 * NBP].rearrange("p (w b) -> p w b", w=2)
                    go(v.tensor_scalar(empty[:, 0:NBP], sm[:, 0], 0.0, float(OUT_OF_BOUNDS), ALU.is_equal, ALU.mult))
                    step(v.tensor_copy(slot_w[:, 0:NBP], sm[:, 1]))
                    step(v.scalar_tensor_tensor(slot_tok[:, 0:NBP], sm[:, 0], -1.0, empty[:, 0:NBP],
                                                ALU.add, ALU.add))
                    join()
                    dve.sem_inc(L.slots_ready, 1)

            def shared(L, s):
                half, ic = s // L.IC, s % L.IC
                dve.wait_ge(L.sh_c_ps, s + 1)
                dve.wait_ge(L.sh_g_ready, s + 1)
                dst = L.hid[:, ic, half * HALF:(half + 1) * HALF]
                if L.l == 0:
                    ins = v.scalar_tensor_tensor(dst, bank[:, 1 + s % 2, :], b13[:, 1, ic:ic + 1],
                                                 g_sh[s % 2][:], ALU.add, ALU.mult)
                else:
                    ins = v.tensor_tensor(dst, bank[:, 1 + s % 2, :], g_sh[s % 2][:], ALU.mult)
                ins.then_inc(L.sh_h_ready, 1)

            def shared_out(L):
                if L.l == 0:
                    for half in range(2):
                        dve.wait_ge(L.comb_ps, half + 1)
                        v.tensor_copy(comb_t[:, half * HALF:(half + 1) * HALF], bank[0:E0 + 1, 1 + half, :]
                                      ).then_inc(L.comb_out, 1)
                    dve.wait_ge(x_tok_in, 16)
                for j in range(NT):
                    dve.wait_ge(L.sh_y_ps, j + 1)
                    if j >= 2:
                        dve.wait_ge(L.sh_stored[j % 2], 16 * (j // 2))
                    v.tensor_tensor(y_sh[j % 2][:], bank[:, 4 + j % 2, 0:C], x_tok[:, j, :], ALU.add
                                    ).then_inc(L.sh_y_ready, 1)

            def hid_copy(L, b):
                dve.wait_ge(L.hid_t_ps, b + 1)
                v.tensor_copy(hid_t[:, 0:L.I], bank[:, 7, 0:L.I]).then_inc(L.hid_t_ready, 1)

            def product(L, b):
                dve.wait_ge(L.up_ps, b + 1)
                dve.wait_ge(L.gate_act, b + 1)
                v.tensor_tensor(act_h[:, 0:I1], bank[:, 6, 0:I1], act_g[:], ALU.mult).then_inc(L.hid_ready, 1)

            def result(L, b, u, first=False):
                dve.wait_ge(L.y_ps, b + 1)
                if not first:
                    dve.wait_ge(L.added, (b - 1) * 16)
                v.tensor_scalar(y[u][:], bank[:, 1, 0:C], slot_w[:, bass.ds(b, 1)], None, ALU.mult
                                ).then_inc(L.y_ready, 1)

            def blocks(L):
                if L.l:
                    product(L, 0)
                hid_copy(L, 0)
                if L.l:
                    product(L, 1)
                result(L, 0, 0, True)
                hid_copy(L, 1)
                if L.l:
                    product(L, 2)
                result(L, 1, 1, True)
                with dve.Fori(0, (L.NB - 3) // 2) as i:
                    for u in range(2):
                        b = i * 2 + (u + 3)
                        hid_copy(L, b - 1)
                        if L.l:
                            product(L, b)
                        result(L, b - 1, u)
                hid_copy(L, L.NB - 1)
                result(L, L.NB - 1, (L.NB - 1) % 2)

            def layernorm(which):
                for j in range(NT):
                    step(v.bn_stats(tok_stats[:, j, :], x_tok[:, j, :]))
                join()
                for j in range(NT):
                    step(v.bn_aggr(tok_mv[:, j, :], tok_stats[:, j, :]))
                join()
                v.tensor_scalar(tok_rstd[:], tok_mv[:, :, 1], 1e-5, None, ALU.add).then_inc(var_ready, 1)
                dve.wait_ge(std_ready, which + 1)
                go(v.reciprocal(tok_rstd[:], tok_rstd[:]))
                for j in range(NT):
                    v.tensor_scalar(xn_tok[:, j, :], x_tok[:, j, :], tok_mv[:, j, 0:1], tok_rstd[:, j:j + 1],
                                    ALU.subtract, ALU.mult).then_inc(xn_tok_ready, 1)

            for s in plan[0][1]:
                shared(L0, s) if isinstance(s, int) else route(L0, s)
            shared_out(L0)
            blocks(L0)

            dve.wait_ge(sum_ready, 16)
            layernorm(1)
            for n in range(2 * QKC):
                c, half = n // 2, n % 2
                span = slice(half * HALF, (half + 1) * HALF)
                dve.wait_ge(high_ready, n + 1)
                if c < HC:
                    ins = v.scalar_tensor_tensor(q_parts[:, c, span], q_high[:, n % 2, :].bitcast(F32), minus_low,
                                                 bank[:, n % 6, :], ALU.mult, ALU.add)
                else:
                    ins = v.scalar_tensor_tensor(k_low[:, c - HC, span], bank[:, n % 6, :], D ** -0.5,
                                                 k_high[:, c - HC, span].bitcast(F32), ALU.mult, ALU.subtract)
                ins.then_inc(parts_ready, 1)
            dve.wait_ge(filled, 1)
            for n in range(NT // 2):
                dve.wait_ge(v_ps, n + 1)
                v.tensor_copy(v_tok[:, 2 * n:2 * n + 2, :, 0:D].rearrange("p j h d -> p (j h) d"),
                              bank[:, 6 + n % 2, 0:2 * C].rearrange("p (m d) -> p m d", d=D)
                              ).then_inc(v_out, 1)

            def neg_maximum(n):
                dve.wait_ge(sc_ps, n + 1)
                v.tensor_reduce(neg_max[:, n % 4, :], bank[:, n % 3, :].rearrange("p (a b) -> p a b", a=2),
                                AXX, ALU.max, negate=True).then_inc(nmax_ready, 1)

            def attention(n):
                dve.wait_ge(e1_ready, 2 * n + 2)
                if n >= 2:
                    dve.wait_ge(att_t_ps, n - 1)
                go(v.reciprocal(exp_inv[:, n % 2, :], exp_sum[:, n % 4, :]))
                for qt in range(2):
                    ins = v.scalar_tensor_tensor(att[n % 2][:, qt, :], e1[n % 3][:, qt, :], exp_inv[:, n % 2, qt:qt + 1],
                                                 mask, ALU.mult, ALU.mult)
                    if qt == 0:
                        step(ins)
                ins.then_inc(att_ready, 1)

            def out_copy(c):
                dve.wait_ge(av_ps, HPC * (c + 1))
                if c >= 2:
                    dve.wait_ge(sums_ps, c - 1)
                v.tensor_copy(o_raw[:, c % 2, :], bank[:, 5 + c % 2, 0:TOKENS_IMG]).then_inc(o_raw_ready, 1)

            def out_norm(c):
                dve.wait_ge(sums_ps, c + 1)
                if c >= HC:
                    dve.wait_ge(proj_ps, c // HC)
                go(v.reciprocal(o_t[:, c % HC, :], bank[:, 7, 0:TOKENS_IMG]))
                v.tensor_tensor(o_t[:, c % HC, :], o_raw[:, c % 2, :], o_t[:, c % HC, :], ALU.mult
                                ).then_inc(o_ready, 1)

            def residual(img):
                dve.wait_ge(proj_ps, img + 1)
                go(v.tensor_tensor(x_tok[:, 2 * img:2 * img + 2, :], x_tok[:, 2 * img:2 * img + 2, :],
                                   bank[:, 7, 0:2 * C].rearrange("p (j c) -> p j c", c=C), ALU.add))
                dve.sem_inc(x_new, 1)

            for n in range(ATT_STEPS):
                if n < N_HEADS:
                    neg_maximum(n)
                if 0 <= n - 1 < N_HEADS:
                    attention(n - 1)
                if chunk_at(n, 4) is not None:
                    out_copy(chunk_at(n, 4))
                if chunk_at(n, 6) is not None:
                    out_norm(chunk_at(n, 6))
                if (chunk_at(n, 8) or 0) % HC == HC - 1:
                    residual(chunk_at(n, 8) // HC)

            layernorm(2)
            for s in plan[1][1]:
                shared(L1, s) if isinstance(s, int) else route(L1, s)
            shared_out(L1)
            blocks(L1)

        @block.tensor
        def _(pe):
            def tile(j):
                return slice(j * P, (j + 1) * P)

            def route(L, stage):
                E, NBP = L.E, L.NB + 1
                if stage == "logits":
                    pe.wait_ge(s_gate0 if L.l == 0 else s_gate1, 16 if L.l == 0 else 32)
                    rows_k = CH + 1 if L.l else CH
                    for j in range(NT):
                        for k in range(NCH):
                            kr = rows_k if k == 1 else CH
                            ins = pe.matmul(bank[:, 3, j * E:(j + 1) * E], xn_t[0:kr, k, tile(j)],
                                            gate_w[L.l][0:kr, k, :], start=(k == 0), stop=(k == NCH - 1))
                    ins.then_inc(L.logits_ps, 1)
                elif stage == "count":
                    pe.wait_ge(L.prefix_ready, 1)
                    pe.matmul(bank[0:E, 3, 256:257], before[:, NT, 0:E], ones[:, 0:1],
                              start=True, stop=True).then_inc(L.count_ps, 1)
                elif stage == "rank":
                    pe.wait_ge(L.pads_ready, 1)
                    dst = bank[:, 7, 0:NT * E].rearrange("p (j e) -> p j e", e=E)
                    subt = const[0:E, C_SUBT:C_SUBT + NT * E1].rearrange("p (j e) -> p j e", e=E1)[:, :, 0:E]
                    pe.matmul(dst, tri, at_pick[:, :, 0:E], start=True, stop=False)
                    pe.matmul(dst, ones[:], before[:, 0:NT, 0:E], start=False, stop=False)
                    pe.matmul(dst, padded_b[0:E, :], subt, start=False, stop=True)
                    pe.matmul(bank[0:E, 3, 260:261], subt[:, 0, :], padded[0:E, :], start=True, stop=False)
                    pe.matmul(bank[0:E, 3, 260:261], ident[0:E, 0:E], padded[0:E, :], start=False, stop=True
                              ).then_inc(L.rank_ps, 1)
                elif stage == "expert":
                    pe.wait_ge(L.ended_ready, 1)
                    pe.matmul(bank[0:1, 3, 264:264 + NBP], ones[0:E, 0:1], ended[0:E, 0:NBP],
                              start=True, stop=True).then_inc(L.expert_ps, 1)
                elif stage == "slots":
                    n = TOPK * NT
                    pe.wait_ge(L.in_blk_ready, 2 * TOPK)
                    pe.wait_ge(L.at_place_ready, n)
                    dst = bank[:, 6, 0:2 * NBP].rearrange("p (w b) -> p w b", w=2)
                    for m in range(n):
                        ins = pe.matmul(dst, at_place[:, m, :], in_blk[:, m, :, 0:NBP],
                                        start=(m == 0), stop=(m == n - 1))
                    ins.then_inc(L.slots_ps, 1)

            def shared(L, s):
                half, ic = s // L.IC, s % L.IC
                w = w13 if L.l == 0 else sh1
                for g, (bk, done) in enumerate(((4, L.sh_a_ps), (1, L.sh_c_ps))):
                    if s >= 2:
                        pe.wait_ge(L.sh_g_ready if g == 0 else L.sh_h_ready, s - 1)
                    for k in range(NCH):
                        ins = pe.matmul(bank[:, bk + s % 2, :], w[:, k, g, ic * P:(ic + 1) * P],
                                        xn_t[0:CH, k, half * HALF:(half + 1) * HALF],
                                        start=(k == 0), stop=(k == NCH - 1))
                    ins.then_inc(done, 1)

            def shared_out(L):
                steps = 2 * L.IC
                if L.l == 0:
                    pe.wait_ge(L.comb_ready, 1)
                    pe.wait_ge(L.sh_h_ready, steps)
                    for half in range(2):
                        for j in range(NT // 2):
                            ins = pe.transpose(bank[0:E0 + 1, 1 + half, tile(j)],
                                               comb[:, half * NT // 2 + j, :], ident)
                        ins.then_inc(L.comb_ps, 1)
                pe.wait_ge(L.sh_h_ready, steps)
                w = w2 if L.l == 0 else sh1d[:]
                for j in range(NT):
                    if j >= 2:
                        pe.wait_ge(L.sh_y_ready, j - 1)
                    dst = bank[:, 4 + j % 2, 0:C]
                    for ic in range(L.IC):
                        ins = pe.matmul(dst, L.hid[:, ic, tile(j)], w[:, ic, :], start=(ic == 0),
                                        stop=(L.l == 1 and ic == L.IC - 1))
                    if L.l == 0:
                        pe.wait_ge(L.comb_out, 1 if j < NT // 2 else 2)
                        ins = pe.matmul(dst, comb_t[:, tile(j)], b2[:], start=False, stop=True)
                    ins.then_inc(L.sh_y_ps, 1)

            def rows_transpose(L, b, u, n):
                pe.wait_ge(L.rows_in[u], (n + 1) * 16)
                for k in range(NCH):
                    ins = pe.transpose(bank[0:CH, 0, tile(k)], rows[u][:, k * CH:(k + 1) * CH], ident)
                ins.then_inc(L.rows_t_ps, 1)

            def expert_of(L, b):
                return pe.value_load(blk_expert[0:1, bass.ds(b, 1)], min_val=0, max_val=L.E - 1)

            def first(L, b):
                e = expert_of(L, b)
                pe.wait_ge(L.rows_t_ready, b + 1)
                if L.l == 0:
                    for k in range(NCH):
                        kr = CH + k
                        ins = pe.matmul(bank[:, 5, :], rows_t[0:kr, k, :],
                                        w_first[0:kr, bass.ds(e * (NCH * I0) + k * I0, I0)],
                                        start=(k == 0), stop=(k == NCH - 1))
                    ins.then_inc(L.first_ps, 1)
                else:
                    for g, done in enumerate((L.first_ps, L.up_ps)):
                        for k in range(NCH):
                            ins = pe.matmul(bank[:, 5 + g, 0:I1], rows_t[0:CH, k, :],
                                            w_first[0:CH, bass.ds(e * (NCH * 2 * I1) + (k * 2 + g) * I1, I1)],
                                            start=(k == 0), stop=(k == NCH - 1))
                        ins.then_inc(done, 1)

            def hid_transpose(L, b):
                pe.wait_ge(L.hid_ready, b + 1)
                for ic in range(L.IC):
                    ins = pe.transpose(bank[:, 7, tile(ic)], act_h[:, tile(ic)], ident)
                ins.then_inc(L.hid_t_ps, 1)

            def second(L, b, first_block=False):
                e = expert_of(L, b)
                pe.wait_ge(L.hid_t_ready, b + 1)
                if not first_block:
                    pe.wait_ge(L.y_ready, b)
                for ic in range(L.IC):
                    ins = pe.matmul(bank[:, 1, 0:C], hid_t[:, tile(ic)],
                                    w_second[:, bass.ds(e * (L.IC * C) + ic * C, C)],
                                    start=(ic == 0), stop=(ic == L.IC - 1))
                ins.then_inc(L.y_ps, 1)

            def blocks(L):
                pe.wait_ge(L.expert_ready, 1)
                pe.wait_ge(L.sh_y_ready, NT)
                rows_transpose(L, 0, 0, 0)
                if L.l == 0:
                    pe.wait_ge(s_fc1, 32)
                    pe.wait_ge(s_fc2, 16)
                else:
                    pe.wait_ge(s_w1a, 16 * E1)
                    pe.wait_ge(s_w1b, 16)
                first(L, 0)
                rows_transpose(L, 1, 1, 0)
                hid_transpose(L, 0)
                first(L, 1)
                rows_transpose(L, 2, 0, 1)
                second(L, 0, True)
                hid_transpose(L, 1)
                first(L, 2)
                rows_transpose(L, 3, 1, 1)
                second(L, 1)
                with pe.Fori(0, (L.NB - 3) // 2) as i:
                    for u in range(2):
                        b = i * 2 + (u + 3)
                        hid_transpose(L, b - 1)
                        first(L, b)
                        rows_transpose(L, b + 1, u, i + 2)
                        second(L, b - 1)
                hid_transpose(L, L.NB - 1)
                second(L, L.NB - 1)

            pe.wait_ge(s_const, 16)
            pe.wait_ge(chan_ready, NCH * IMAGES)
            pe.matmul(bank[0:CH, 0, 0:NCH * IMAGES], gavg, chan_mv[:, :, 0], start=True, stop=True
                      ).then_inc(gmean_ps, 1)
            pe.wait_ge(dev_ready, 1)
            pe.matmul(bank[0:CH, 0, 64:64 + NCH * IMAGES], gavg, chan_dev[:], start=True, stop=True
                      ).then_inc(gvar_ps, 1)
            for n in range(NT // 2):
                pe.wait_ge(xn_t_ready, 2 * (n + 1))
                if n >= 2:
                    pe.wait_ge(tp_out, n - 1)
                for m in range(2):
                    for k in range(NCH):
                        ins = pe.transpose(bank[:, 1 + n % 2, (m * NCH + k) * CH:(m * NCH + k + 1) * CH],
                                           xn_t[0:CH, k, tile(2 * n + m)], ident[0:CH, 0:CH])
                ins.then_inc(tp_ps, 1)
            pe.wait_ge(filled, 1)

            def moe_before(L):
                for s in plan[L.l][0]:
                    if s == 0:
                        pe.wait_ge(s_sh0 if L.l == 0 else s_sh1, 80 if L.l == 0 else 32)
                        pe.wait_ge(tp_out, NT // 2 * (1 if L.l == 0 else 3))
                    shared(L, s) if isinstance(s, int) else route(L, s)
                shared_out(L)
                blocks(L)

            moe_before(L0)

            def norm_transposes(which):
                for n in range(NT // 2):
                    pe.wait_ge(xn_tok_ready, (which - 1) * NT + 2 * (n + 1))
                    if n >= 2:
                        pe.wait_ge(tp_out, which * (NT // 2) + n - 1)
                    for k in range(NCH):
                        for m in range(2):
                            ins = pe.transpose(bank[0:CH, 1 + n % 2, (k * 2 + m) * P:(k * 2 + m + 1) * P],
                                               xn_tok[:, 2 * n + m, k * CH:(k + 1) * CH], ident)
                    ins.then_inc(tp_ps, 1)
                pe.wait_ge(tp_out, (which + 1) * (NT // 2))

            norm_transposes(1)
            pe.wait_ge(s_attw, 48)
            for n in range(2 * QKC):
                c, half = n // 2, n % 2
                if n >= 6:
                    pe.wait_ge(parts_ready, n - 5)
                for k in range(NCH):
                    ins = pe.matmul(bank[:, n % 6, :], wqk[:, k, c, :], xn_t[0:CH, k, half * HALF:(half + 1) * HALF],
                                    start=(k == 0), stop=(k == NCH - 1))
                ins.then_inc(qk_ps, 1)
            for n in range(NT // 2):
                if n >= 2:
                    pe.wait_ge(v_out, n - 1)
                for m in range(2):
                    for k in range(NCH):
                        ins = pe.matmul(bank[:, 6 + n % 2, m * C:(m + 1) * C], xn_t[0:CH, k, tile(2 * n + m)],
                                        wv[:, k, :], start=(k == 0), stop=(k == NCH - 1))
                ins.then_inc(v_ps, 1)
            pe.wait_ge(parts_ready, 2 * QKC)
            pe.wait_ge(v_out, NT // 2)

            def scores(n):
                img, h = n // HEADS, n % HEADS
                r = slice(HG * (h % HPC), HG * (h % HPC + 1))
                if n >= 3:
                    pe.wait_ge(e1_ready, 2 * (n - 2))
                for qt in range(2):
                    q0 = img * TOKENS_IMG + qt * P
                    for part in (k_high, k_low):
                        ins = pe.matmul(bank[:, n % 3, qt * 256:(qt + 1) * 256], q_parts[r, h // HPC, q0:q0 + P],
                                        part[r, h // HPC, img * TOKENS_IMG:(img + 1) * TOKENS_IMG],
                                        start=(part is k_high), stop=(part is k_low))
                ins.then_inc(sc_ps, 1)

            def att_transpose(n):
                pe.wait_ge(att_ready, n + 1)
                if n >= 2:
                    pe.wait_ge(p2_ready, n - 1)
                for kt in range(2):
                    for qt in range(2):
                        ins = pe.transpose(bank[:, 3 + n % 2, (kt * 2 + qt) * P:(kt * 2 + qt + 1) * P],
                                           att[n % 2][:, qt, tile(kt)], ident)
                ins.then_inc(att_t_ps, 1)

            def weigh_values(n):
                img, h = n // HEADS, n % HEADS
                g, c = n % HPC, n // HPC
                pe.wait_ge(p2_ready, n + 1)
                if g == 0 and c >= 2:
                    pe.wait_ge(o_raw_ready, c - 1)
                for kt in range(2):
                    ins = pe.matmul(bank[g * HG:(g + 1) * HG, 5 + c % 2, 0:TOKENS_IMG],
                                    v_tok[:, 2 * img + kt, h, :], p2_t[n % 3][:, kt, :],
                                    start=(kt == 0), stop=(kt == 1))
                ins.then_inc(av_ps, 1)

            def spread_sums(c):
                pe.wait_ge(o_raw_ready, c + 1)
                if c and c % HC == 0:
                    pe.wait_ge(x_new, c // HC)
                elif c:
                    pe.wait_ge(o_ready, c)
                pe.matmul(bank[:, 7, 0:TOKENS_IMG], sum_row, o_raw[:, c % 2, :],
                          start=True, stop=True).then_inc(sums_ps, 1)

            def project(img):
                pe.wait_ge(o_ready, HC * (img + 1))
                for qt in range(2):
                    for k in range(HC):
                        ins = pe.matmul(bank[:, 7, qt * C:(qt + 1) * C], o_t[:, k, tile(qt)], wo[:, k, :],
                                        start=(k == 0), stop=(k == HC - 1))
                ins.then_inc(proj_ps, 1)

            for n in range(ATT_STEPS):
                if n < N_HEADS:
                    scores(n)
                if 0 <= n - 2 < N_HEADS:
                    att_transpose(n - 2)
                if 0 <= n - 3 < N_HEADS:
                    weigh_values(n - 3)
                if chunk_at(n, 5) is not None:
                    spread_sums(chunk_at(n, 5))
                if (chunk_at(n, 7) or 0) % HC == HC - 1:
                    project(chunk_at(n, 7) // HC)

            norm_transposes(2)
            moe_before(L1)


_OUT = ((4, 16, 16, C), "float32")


def kernel(**inputs):
    import concourse.bacc as bacc
    from concourse.bass_utils import run_bass_kernel_spmd

    a = {k: np.asarray(v) for k, v in inputs.items()}

    def chunks(w):
        return w.reshape(NCH, CH, -1).transpose(1, 0, 2)

    x = a["x"].reshape(T, C)
    qkv = a["L1_attn_w_qkv"].reshape(3, HEADS, D, C)
    qk = np.stack([qkv[0:2], qkv[0:2]], 2)
    wo = np.zeros((HC, HPC, HG, C), np.float32)
    wo[:, :, 0:D] = a["L1_attn_w_out"].T.reshape(HC, HPC, D, C)
    wo[0, 0, D] = a["L1_attn_b_out"]
    arrays = {
        "x": x,
        "x_t": chunks(x.T),
        "const": constants(),
        "gate0": chunks(a["L0_conv_gate_w"].T),
        "w13": np.stack([chunks(a["L0_conv_w1_w"].T), chunks(a["L0_conv_w3_w"].T)], 2),
        "b13": np.stack([a["L0_conv_w1_b"].reshape(-1, P).T, a["L0_conv_w3_b"].reshape(-1, P).T], 1),
        "w2": a["L0_conv_w2_w"].T.reshape(I0 // P, P, C).transpose(1, 0, 2),
        "fc2_b": a["L0_conv_fc2_b"],
        "w2_b": a["L0_conv_w2_b"].reshape(1, C),
        "fc1": a["L0_conv_fc1_w"].transpose(2, 0, 1).reshape(NCH, CH, E0, I0).transpose(1, 2, 0, 3),
        "fc1_b": a["L0_conv_fc1_b"].reshape(1, E0, I0),
        "fc2": a["L0_conv_fc2_w"].transpose(2, 0, 1).reshape(I0 // P, P, E0, C).transpose(1, 2, 0, 3)
        .reshape(P, -1),
        "wqk": chunks(qk.reshape(-1, C).T).reshape(CH, NCH, QKC, P),
        "wv": chunks(a["L1_attn_w_qkv"][2 * C:].T),
        "wo": wo.reshape(HC, P, C).transpose(1, 0, 2),
        "gate1": chunks(a["L1_ffn_w_gate"]),
        "bias1": a["L1_ffn_expert_bias"].reshape(1, E1),
        "gate_up": np.stack([a["L1_ffn_wg"], a["L1_ffn_wu"]], 0).reshape(2, E1, NCH, CH, I1)
        .transpose(3, 1, 2, 0, 4),
        "down": a["L1_ffn_wd"].reshape(E1, I1 // P, P, C).transpose(2, 0, 1, 3).reshape(P, -1),
        "sh1": np.stack([chunks(a["L1_ffn_swg"]), chunks(a["L1_ffn_swu"])], 2),
        "sh1d": a["L1_ffn_swd"].reshape(I1 // P, P, C).transpose(1, 0, 2),
    }
    arrays = {k: np.ascontiguousarray(v) for k, v in arrays.items()}
    nc = bacc.Bacc("TRN2", target_bir_lowering=False, num_devices=1)
    d = {k: nc.dram_tensor(f"in_{k}", v.shape, mybir.dt.from_np(v.dtype), kind="ExternalInput").ap()
         for k, v in arrays.items()}
    out = nc.dram_tensor("out_0", (T, C), F32, kind="ExternalOutput").ap()
    build(nc, d, out)
    r = run_bass_kernel_spmd(nc, [{f"in_{k}": v for k, v in arrays.items()}], core_ids=[0])
    return r.results[0]["out_0"].reshape(_OUT[0])
```

```python
from contextlib import ExitStack

import numpy as np

import concourse.bass as bass
from concourse import mybir

ALU = mybir.AluOpType
ACT = mybir.ActivationFunctionType
AXX = mybir.AxisListType.X
F32 = mybir.dt.float32
F32R = mybir.dt.float32r
I32 = mybir.dt.int32
U32 = mybir.dt.uint32

P = 128
IMAGES, TOKENS_IMG = 4, 256
T = IMAGES * TOKENS_IMG
NT = T // P
C = 192
CH = 96
NCH = C // CH
GROUP = C // 32
HEADS, D = 12, 16
HG = 32
HPC = P // HG
HC = HEADS // HPC
QKC = 2 * HC
TOPK = 2
E0, I0 = 8, 512
E1, I1 = 16, 384
NB0 = TOPK * T // P + E0 - 1
NB1 = TOPK * T // P + E1 - 1
OUT_OF_BOUNDS = 4096

C_IDENT = 0
C_GAVG = C_IDENT + P
C_TRI = C_GAVG + CH
C_IOTA = C_TRI + P
C_MASK = C_IOTA + P
C_TOK1 = C_MASK + TOKENS_IMG
C_BLK = C_TOK1 + NT
C_SUBT = C_BLK + NB1 + 1
C_SUM = C_SUBT + NT * E1
C_LOW = C_SUM + HPC
C_ALL = C_LOW + 1


def constants():
    c = np.zeros((P, C_ALL), np.float32)
    n = np.arange(P)
    c[:, C_IDENT:C_IDENT + P] = np.eye(P)
    c[:, C_TRI:C_TRI + P] = n[:, None] < n[None, :]
    c[:, C_IOTA:C_IOTA + P] = n[None, :]
    g = np.arange(CH) // GROUP
    c[:CH, C_GAVG:C_GAVG + CH] = (g[:, None] == g[None, :]) / GROUP
    k = np.arange(TOKENS_IMG)
    c[:, C_MASK:C_MASK + TOKENS_IMG] = np.where(n[:, None] % 64 == k[None, :] % 64, 0.5, 1.0)
    c[:, C_TOK1:C_TOK1 + NT] = P * np.arange(NT)[None, :] + n[:, None] + 1
    c[:, C_BLK:C_BLK + NB1 + 1] = P * np.arange(NB1 + 1)[None, :]
    e = np.arange(E1)
    c[:E1, C_SUBT:C_SUBT + NT * E1] = np.tile(e[:, None] < e[None, :], (1, NT))
    c[:, C_SUM:C_SUM + HPC] = n[:, None] == n[None, 0:HPC] * HG + D
    c[:, C_LOW] = -1.0 * (n % HG >= D)
    return c


class Layer:

    def __init__(self, n, experts, blocks, inner, hid, sem):
        self.l, self.E, self.NB, self.I, self.IC, self.hid = n, experts, blocks, inner, inner // P, hid
        self.sizes = (NCH * (n + 1) * inner, self.IC * C)
        self.sh_stored = [sem(f"L{n}_sh_stored{i}") for i in range(2)]
        self.rows_in = [sem(f"L{n}_rows_in{i}") for i in range(2)]
        self.logits_ps = sem(f"L{n}_logits_ps")
        self.gap_ready = sem(f"L{n}_gap_ready")
        self.gap_exp = sem(f"L{n}_gap_exp")
        self.prefix_ready = sem(f"L{n}_prefix_ready")
        self.count_ps = sem(f"L{n}_count_ps")
        self.pads_ready = sem(f"L{n}_pads_ready")
        self.rank_ps = sem(f"L{n}_rank_ps")
        self.ended_ready = sem(f"L{n}_ended_ready")
        self.expert_ps = sem(f"L{n}_expert_ps")
        self.expert_ready = sem(f"L{n}_expert_ready")
        self.in_blk_ready = sem(f"L{n}_in_blk_ready")
        self.at_place_ready = sem(f"L{n}_at_place_ready")
        self.slots_ps = sem(f"L{n}_slots_ps")
        self.slots_ready = sem(f"L{n}_slots_ready")
        self.comb_ready = sem(f"L{n}_comb_ready")
        self.comb_ps = sem(f"L{n}_comb_ps")
        self.comb_out = sem(f"L{n}_comb_out")
        self.sh_a_ps = sem(f"L{n}_sh_a_ps")
        self.sh_c_ps = sem(f"L{n}_sh_c_ps")
        self.sh_g_ready = sem(f"L{n}_sh_g_ready")
        self.sh_h_ready = sem(f"L{n}_sh_h_ready")
        self.sh_y_ps = sem(f"L{n}_sh_y_ps")
        self.sh_y_ready = sem(f"L{n}_sh_y_ready")
        self.rows_t_ps = sem(f"L{n}_rows_t_ps")
        self.rows_t_ready = sem(f"L{n}_rows_t_ready")
        self.first_ps = sem(f"L{n}_first_ps")
        self.up_ps = sem(f"L{n}_up_ps")
        self.gate_act = sem(f"L{n}_gate_act")
        self.hid_ready = sem(f"L{n}_hid_ready")
        self.hid_t_ps = sem(f"L{n}_hid_t_ps")
        self.hid_t_ready = sem(f"L{n}_hid_t_ready")
        self.y_ps = sem(f"L{n}_y_ps")
        self.y_ready = sem(f"L{n}_y_ready")
        self.added = sem(f"L{n}_added")


def build(nc, d, out):
    with ExitStack() as ctx:
        def sb(name, shape, dt=F32):
            return ctx.enter_context(nc.sbuf_tensor(name, shape, dt))

        def sem(name):
            return ctx.enter_context(nc.semaphore(name))

        bank = ctx.enter_context(nc.psum_tensor("bank", [P, 8, 512], F32))

        xn_rows = [nc.dram_tensor(f"xn_rows{l}", [T, C], F32).ap() for l in range(2)]
        sum0 = nc.dram_tensor("sum0", [T, C], F32).ap()

        def by_tile(ap):
            return ap.rearrange("(j p) c -> p j c", p=P)

        const = sb("const", [P, C_ALL])
        ident = const[:, C_IDENT:C_IDENT + P]
        tri = const[:, C_TRI:C_TRI + P]
        iota = const[:, C_IOTA:C_IOTA + P]
        gavg = const[0:CH, C_GAVG:C_GAVG + CH]
        mask = const[:, C_MASK:C_MASK + TOKENS_IMG]
        tok1 = const[:, C_TOK1:C_TOK1 + NT]
        blk_start = const[:, C_BLK:C_BLK + NB1 + 1]
        sum_row = const[:, C_SUM:C_SUM + HPC]
        minus_low = const[:, C_LOW:C_LOW + 1]

        ones = sb("ones", [P, P])
        with nc.sbuf_tensor("w_first", [P, E1 * NCH * 2 * I1], F32) as w_first:
            pass
        wg_up = w_first[0:CH, :].rearrange("p (e k g i) -> p e k g i", e=E1, k=NCH, g=2)
        fc1 = w_first[0:CH + 1, 0:E0 * NCH * I0].rearrange("p (e k i) -> p e k i", e=E0, k=NCH)
        o = E0 * NCH * I0
        w13 = w_first[0:CH, o:o + NCH * 2 * I0].rearrange("p (k g i) -> p k g i", k=NCH, g=2)
        o += NCH * 2 * I0
        w2 = w_first[:, o:o + (I0 // P) * C].rearrange("p (i c) -> p i c", c=C)
        o += (I0 // P) * C
        hid0 = w_first[:, o:o + (I0 // P) * T].rearrange("p (i t) -> p i t", t=T)
        o += (I0 // P) * T
        x_t = w_first[0:CH, o:o + NCH * T].rearrange("p (k t) -> p k t", t=T)
        o += NCH * T
        a_end = E1 * NCH * 2 * I1
        a = a_end - (NCH * QKC * P + NCH * C)
        qkv_size = a_end - a
        wqkv = w_first[0:CH, a:a_end]
        a -= NT * HEADS * HG
        v_tok = w_first[:, a:a + NT * HEADS * HG].rearrange("p (j h d) -> p j h d", j=NT, h=HEADS)
        a -= qkv_size
        qkv_high = a
        assert o <= a
        a -= HC * C
        wo = w_first[:, a:a + HC * C].rearrange("p (k c) -> p k c", k=HC)
        a -= HC * TOKENS_IMG
        o_t = w_first[:, a:a + HC * TOKENS_IMG].rearrange("p (k t) -> p k t", k=HC)
        a -= 2 * TOKENS_IMG
        o_raw = w_first[:, a:a + 2 * TOKENS_IMG].rearrange("p (k t) -> p k t", k=2)
        behind = a_end - a
        a -= 3 * HC * T
        sb("before_attention", [P, a])
        q_parts = sb("q_parts", [P, HC, T], F32R)
        k_high = sb("k_high", [P, HC, T], F32R)
        k_low = sb("k_low", [P, HC, T], F32R)
        sb("behind_scores", [P, qkv_high - (a_end - behind)])
        w_high = sb("w_high", [P, qkv_size], F32R)[0:CH]
        sb("v_room", [P, a_end - qkv_high - 2 * qkv_size])
        w_low = sb("w_low", [P, qkv_size], F32R)[0:CH]

        def w_parts(k, c, m):
            o = NCH * QKC * P + k * C if c is None else (k * QKC + c) * P
            return w_high[:, o:o + m], w_low[:, o:o + m]
        w_second = sb("w_second", [P, E1 * (I1 // P) * C])
        fc2 = w_second[:, 0:E0 * (I0 // P) * C]
        per_expert = NCH * 2 * I1
        EARLY = a // per_expert
        MIDDLE = (a + 3 * HC * T) // per_expert
        comb_t = w_second[0:E0 + 1, E0 * (I0 // P) * C:E0 * (I0 // P) * C + T]
        with nc.sbuf_tensor("scratch", [P, 4096], F32) as scratch:
            pass
        with nc.sbuf_tensor("xn_high", [P, NCH, T], F32R) as xn_high:
            with nc.sbuf_tensor("xn_low", [P, NCH, T], F32R) as xn_low:
                pass
        at_place = sb("at_place", [P, TOPK * NT, P], F32R)
        in_blk = sb("in_blk", [P, TOPK * NT, 3, NB1 + 1], F32R)
        eq_blk = sb("eq_blk", [P, TOPK * NT, NB1 + 1])

        def scratch_at(o, *dims):
            n = int(np.prod(dims))
            ap = scratch[:, o:o + n]
            return ap.rearrange("p (a b) -> p a b", a=dims[0]) if len(dims) == 2 else ap.rearrange(
                "p (a b c) -> p a b c", a=dims[0], b=dims[1])

        x_tok = sb("x_tok", [P, NT, C])
        xn_tok = sb("xn_tok", [P, NT, C])
        hid1 = [w_first[:, (E1 - 1) * per_expert:], xn_tok[:].rearrange("p j c -> p (j c)")]
        hid1 = [h.rearrange("p (i t) -> p i t", t=T // 2) for h in hid1]
        hid0 = [hid0[:, :, 0:T // 2], hid0[:, :, T // 2:T]]
        xn_t = sb("xn_t", [CH + 1, NCH, T])
        chan_stats = sb("chan_stats", [CH, NCH * IMAGES, 6])
        chan_mv = sb("chan_mv", [CH, NCH * IMAGES, 2])
        grp_mean = sb("grp_mean", [CH, NCH * IMAGES])
        chan_dev = sb("chan_dev", [CH, NCH * IMAGES])
        grp_rstd = sb("grp_rstd", [CH, NCH * IMAGES])
        tok_stats = sb("tok_stats", [P, NT, 6])
        tok_mv = sb("tok_mv", [P, NT, 2])
        tok_rstd = sb("tok_rstd", [P, NT])

        gate_w = [sb("gate0", [CH, NCH, E0]), sb("gate1", [CH + 1, NCH, E1])]
        b13 = sb("b13", [P, 2, I0 // P])
        b2 = sb("b2", [E0 + 1, C])
        sh1 = sb("sh1", [CH, NCH, 2, I1])
        sh1d = sb("sh1d", [P, I1 // P, C])

        logit = sb("logit", [P, NT, E1])
        top8 = sb("top8", [P, NT, 8])
        top8i = sb("top8i", [P, NT, 8], U32)
        choice = sb("choice", [P, NT, TOPK])
        gap = sb("gap", [P, NT])
        gap_e = sb("gap_e", [P, NT])
        gap_1 = sb("gap_1", [P, NT])
        weight = sb("weight", [P, TOPK, NT])
        picked = sb("picked", [P, TOPK, NT, E1])
        comb = sb("comb", [P, NT, E0 + 1])
        comb_a = sb("comb_a", [P, NT, E0])
        before = sb("before", [P, NT + 1, E1])
        count_i = sb("count_i", [E1, 1], I32)
        count_i2 = sb("count_i2", [E1, 1], I32)
        padded = sb("padded", [E1, 1])
        padded_b = sb("padded_b", [E1, P])
        ended = sb("ended", [E1, NB1 + 1])
        blk_weights = sb("blk_weights", [1, 2, NB1 + 1], I32)
        at_pick = sb("at_pick", [P, NT, E1])
        slot = sb("slot", [P, TOPK, NT])
        slot_i = sb("slot_i", [P, TOPK * NT], I32)
        slot_j = sb("slot_j", [P, 2, TOPK * NT], I32)
        slot_f = sb("slot_f", [P, 2, TOPK * NT])
        weight_high = sb("weight_high", [P, TOPK, NT])
        weight_low = sb("weight_low", [P, TOPK, NT])
        empty = sb("empty", [P, NB1 + 1])
        slot_tok = sb("slot_tok", [P, NB1 + 1], I32)
        slot_w = sb("slot_w", [P, NB1 + 1])

        rows = [sb(f"rows{i}", [P, C]) for i in range(2)]
        rows_t = sb("rows_t", [CH + 1, NCH, P])
        act_h = sb("act_h", [P, I0])
        act_g = sb("act_g", [P, I1])
        hid_t = sb("hid_t", [P, I0])
        y = [sb(f"y{i}", [P, C]) for i in range(2)]
        g_sh = [sb(f"g_sh{i}", [P, 512]) for i in range(2)]
        y_sh = [sb(f"y_sh{i}", [P, C]) for i in range(2)]

        neg_max = sb("neg_max", [P, 4, 2])
        exp_sum = sb("exp_sum", [P, 4, 2])
        exp_inv = sb("exp_inv", [P, 2, 2])
        o_inv = sb("o_inv", [P, 2, HPC])
        o_inv_wide = act_h[:, 0:2 * P].rearrange("p (a g d) -> p a g d", a=2, g=HPC)
        q_high = [act_h, hid_t]
        e1 = [scratch_at(512 * i, 2, TOKENS_IMG) for i in range(3)]
        att = [scratch_at(512 * (3 + i), 2, TOKENS_IMG) for i in range(2)]
        p2_t = [scratch_at(512 * (5 + i), 2, TOKENS_IMG) for i in range(3)]

        s_const, s_gate0, s_sh0, s_fc1, s_fc2 = (sem(n) for n in (
            "const_loaded", "gate0_loaded", "shared0_loaded", "fc1_loaded", "fc2_loaded"))
        s_attw, s_gate1, s_sh1, s_w1a, s_w1b = (sem(n) for n in (
            "out_w_loaded", "gate1_loaded", "shared1_loaded", "gate_up_loaded", "down_loaded"))
        s_x = [sem(f"x_loaded_chunk{k}") for k in range(NCH)]
        s_qkvw, w_high_ready, w_low_ready, xn_low_ready = (
            sem("qkv_w_loaded"), sem("qkv_w_high_ready"), sem("qkv_w_low_ready"), sem("xn_low_ready"))
        s_w13, s_tables = sem("w13_loaded"), sem("tables_loaded")
        filled = sem("fills_done")
        x_tok_in = sem("x_tok_loaded")
        act_c, dve_c, pool_c = sem("act_own"), sem("dve_own"), sem("pool_own")
        chan_ready, dev_ready = sem("chan_stats_ready"), sem("chan_dev_ready")
        gmean_ps, gvar_ps = sem("group_mean_in_psum"), sem("group_var_in_psum")
        var_ready, std_ready = sem("var_ready"), sem("std_ready")
        xn_t_ready = sem("xn_t_ready")
        tp_ps = sem("norm_transposed_in_psum")
        tp_out = sem("norm_transposes_copied")
        xn_stored = sem("xn_rows_stored")
        xn_tok_ready = sem("xn_tok_ready")
        sum_ready = [sem(f"sum0_loaded_half{h}") for h in range(2)]

        layers = []
        for l, (E, NB, I) in enumerate(((E0, NB0, I0), (E1, NB1, I1))):
            layers.append(Layer(l, E, NB, I, (hid0, hid1)[l], sem))
        L0, L1 = layers

        qk_ps, v_ps, v_out = sem("qk_in_psum"), sem("v_in_psum"), sem("v_copied")
        high_ready, parts_ready = sem("qk_high_part_ready"), sem("qk_parts_ready")
        sc_ps, nmax_ready, e1_ready, att_ready = (
            sem("scores_in_psum"), sem("neg_max_ready"), sem("exp_ready"), sem("att_ready"))
        att_t_ps, p2_ready, av_ps = sem("att_t_in_psum"), sem("p2_ready"), sem("av_in_psum")
        o_raw_ready, sums_ps, inv_ready, wide_ready, spread_ps = (
            sem("o_raw_ready"), sem("sums_in_psum"), sem("inverse_sums_ready"), sem("inverse_sums_repeated"),
            sem("inverse_sums_in_psum"))
        o_ready, proj_ps, x_new = sem("o_ready"), sem("proj_in_psum"), sem("x_updated")
        out_done = sem("out_stored")

        def chained(eng, s):
            n = [0]

            def step(ins):
                n[0] += 1
                ins.then_inc(s, 1)

            def join():
                eng.wait_ge(s, n[0])

            def go(ins):
                step(ins)
                join()
            return step, join, go

        N_HEADS = IMAGES * HEADS
        SUMS = 7
        TAIL = 3
        ATT_STEPS = N_HEADS + SUMS + 3 - TAIL

        def chunk_at(n, lag):
            last = N_HEADS // HPC - 1
            if lag >= SUMS and n == N_HEADS - 1 + lag - TAIL:
                return last
            c = (n - lag + 1) // HPC - 1
            return c if (n - lag + 1) % HPC == 0 and 0 <= c < last + (lag < SUMS) else None

        def sums_bank(c):
            return 0 if c == N_HEADS // HPC - 1 else 7

        HALF = T // 2
        PASSES = ((0, 0), (1, 0), (0, 1))
        later = [("y", j) for j in range(NT // 2, NT)]
        plan = {
            0: ([0, ("shared", 1, 0), ("shared", 2, 1), "rows", 3, "count", 4, "rank", 5, "expert", 6, 7, "slots",
                 "comb"],
                [0, 1, "top2", 2, "pads", 3, "ended", 4, "blocks", 5, "places", "expert", 6, "slots", "comb", 7]),
            1: ([2, 3, "count", ("y", 0), "rank", ("y", 1), 4, ("y", 2), 5, "expert", ("y", 3), "slots"] + later,
                ["top2", 2, "pads", 3, "ended", ("y", 0), ("y", 1), "blocks", 4, "places", "expert", 5, ("y", 2),
                 ("y", 3), "slots"] + later),
        }

        def out_bank(L, j):
            return (0, 6)[j % 2] if L.l and j < NT // 2 else 5 - j % 2

        SECOND_HALF = 3

        def bc(ap, axis, shape):
            return ap.unsqueeze(axis).to_broadcast(shape)

        block = ctx.enter_context(nc.Block())

        @block.sync
        def _(sp):
            for k in range(NCH):
                sp.dma_start(x_t[:, k], d["x_t"][:, k]).then_inc(s_x[k], 16)
            sp.dma_start(const[:, 0:C_TRI], d["const"][:, 0:C_TRI]).then_inc(s_const, 16)
            sp.dma_start(gate_w[0][:], d["gate0"]).then_inc(s_gate0, 16)
            sp.dma_start(w13, d["w13"]).then_inc(s_w13, 16)
            sp.dma_start(b13[:], d["b13"]).then_inc(s_w13, 16)
            sp.dma_start(const[:, C_TRI:], d["const"][:, C_TRI:]).then_inc(s_tables, 16)
            sp.dma_start(w2, d["w2"]).then_inc(s_sh0, 16)
            sp.dma_start(b2[0:E0, :], d["fc2_b"]).then_inc(s_sh0, 16)
            sp.dma_start(b2[E0:E0 + 1, :], d["w2_b"]).then_inc(s_sh0, 16)
            sp.dma_start(x_tok[:], by_tile(d["x"])).then_inc(x_tok_in, 16)
            sp.dma_start(fc1[0:CH], d["fc1"]).then_inc(s_fc1, 16)
            sp.dma_start(fc1[CH:CH + 1, :, 1, :], d["fc1_b"]).then_inc(s_fc1, 16)
            sp.dma_start(fc2, d["fc2"]).then_inc(s_fc2, 16)
            sp.wait_ge(tp_out, NT // 2)
            sp.dma_start(by_tile(xn_rows[0]), xn_tok[:]).then_inc(xn_stored, 16)
            sp.dma_start(wqkv[:, 0:NCH * QKC * P], d["wqk"].rearrange("p k c m -> p (k c m)")).then_inc(s_qkvw, 16)
            sp.dma_start(wqkv[:, NCH * QKC * P:], d["wv"].rearrange("p k c -> p (k c)")).then_inc(s_qkvw, 16)
            sp.dma_start(gate_w[1][0:CH], d["gate1"]).then_inc(s_gate1, 16)
            sp.dma_start(gate_w[1][CH:CH + 1, 1, :], d["bias1"]).then_inc(s_gate1, 16)
            sp.dma_start(sh1[:], d["sh1"]).then_inc(s_sh1, 16)
            sp.dma_start(sh1d[:], d["sh1d"]).then_inc(s_sh1, 16)
            for j in range(NT):
                sp.wait_ge(L0.sh_y_ready, j + 1)
                sp.dma_start(sum0[j * P:(j + 1) * P], y_sh[j % 2][:]).then_inc(L0.sh_stored[j % 2], 16)
            sp.wait_ge(L0.added, 16 * NB0)
            for half in range(2):
                t = slice(half * NT // 2, (half + 1) * NT // 2)
                sp.dma_start(x_tok[:, t], by_tile(sum0)[:, t]).then_inc(sum_ready[half], 16)
            sp.wait_ge(L0.y_ps, NB0)
            sp.dma_start(wo, d["wo"]).then_inc(s_attw, 16)
            for e in range(EARLY):
                sp.dma_start(wg_up[:, e], d["gate_up"][:, e]).then_inc(s_w1a, 16)
            sp.dma_start(w_second[:], d["down"]).then_inc(s_w1b, 16)
            sp.wait_ge(sc_ps, N_HEADS)
            for e in range(EARLY, MIDDLE):
                sp.dma_start(wg_up[:, e], d["gate_up"][:, e]).then_inc(s_w1a, 16)
            sp.wait_ge(xn_tok_ready, 2 * NT)
            sp.dma_start(by_tile(xn_rows[1]), xn_tok[:]).then_inc(xn_stored, 16)
            for e in range(MIDDLE, E1 - 1):
                sp.dma_start(wg_up[:, e], d["gate_up"][:, e]).then_inc(s_w1a, 16)
            for j in range(NT):
                if j == NT // 2:
                    sp.dma_start(wg_up[:, E1 - 1], d["gate_up"][:, E1 - 1]).then_inc(s_w1a, 16)
                sp.wait_ge(L1.sh_y_ready, j + 1)
                sp.dma_start(out[j * P:(j + 1) * P], y_sh[j % 2][:]).then_inc(L1.sh_stored[j % 2], 16)
            sp.wait_ge(L1.added, 16 * NB1)

        def pool_blocks(pool, L, target):
            pool.wait_ge(L.slots_ready, 1)
            pool.wait_ge(xn_stored, 16 * (L.l + 1))

            def gather(b):
                pool.indirect_dma_start(
                    rows[b % 2][:], None, xn_rows[L.l],
                    bass.IndirectOffsetOnAxis(slot_tok[:, b:b + 1].bitcast(U32), 0),
                    bounds_check=T - 1, oob_is_err=False).then_inc(L.rows_in[b % 2], 16)

            def add(b):
                pool.wait_ge(L.y_ready, b + 1)
                if b:
                    pool.wait_ge(L.added, b * 16)
                pool.indirect_dma_start(
                    target, bass.IndirectOffsetOnAxis(slot_tok[:, b:b + 1].bitcast(U32), 0), y[b % 2][:], None,
                    bounds_check=T - 1, oob_is_err=False, compute_op=ALU.add).then_inc(L.added, 16)

            AHEAD = 4
            for b in range(AHEAD):
                if b >= 2:
                    pool.wait_ge(L.rows_t_ps, b - 1)
                gather(b)
            for s in L.sh_stored:
                pool.wait_ge(s, 16 * NT // 2)
            for b in range(L.NB):
                add(b)
                if b + AHEAD <= L.NB:
                    pool.wait_ge(L.rows_t_ps, b + AHEAD - 1)
                    gather(b + AHEAD)

        @block.gpsimd
        def _(pool):
            fills = [(ones[:], 1.0), (rows[0][:], 0.0), (rows[1][:], 0.0), (comb[:, :, E0:E0 + 1], 1.0),
                     (xn_t[CH:CH + 1, 1, :], 1.0), (rows_t[CH:CH + 1, 1, :], 1.0),
                     (v_tok[:, :, :, D:HG], 0.0), (v_tok[:, :, :, D:D + 1], 1.0),
                     (before[:, 0, :], 0.0)]
            for n, (ap, v) in enumerate(fills):
                nc.gpsimd.memset(ap, v).then_inc(pool_c, 1)
                pool.wait_ge(pool_c, n + 1)
            pool.sem_inc(filled, 1)
            pool_blocks(pool, L0, sum0)
            for c in range(N_HEADS // HPC):
                pool.wait_ge(inv_ready, c + 1)
                if c:
                    pool.wait_ge(spread_ps, c)
                nc.gpsimd.tensor_copy(o_inv_wide.rearrange("p a g d -> p (a g) d"),
                                      bc(o_inv[:].rearrange("p a g -> p (a g)"), 2, [P, 2 * HPC, HG])
                                      ).then_inc(wide_ready, 1)
            pool_blocks(pool, L1, out)

        def tp_bank(which, n):
            return 6 + n % 2 if which == 0 else (1, 2, 6, 7)[n] if which == 1 else (1, 2, 0, 7)[n]

        def act_norm_transposes(act, which, pairs):
            for n in pairs:
                act.wait_ge(tp_ps, which * (NT // 2) + n + 1)
                src = bank[:, tp_bank(which, n), :]
                if which == 0:
                    ins = nc.scalar.copy(xn_tok[:, 2 * n:2 * n + 2, :],
                                         src[:, 0:2 * C].rearrange("p (j c) -> p j c", c=C))
                else:
                    ins = nc.scalar.copy((xn_high if which == 1 else xn_t)[0:CH, :, 2 * n * P:(2 * n + 2) * P],
                                         src[0:CH].rearrange("p (k t) -> p k t", k=NCH))
                ins.then_inc(tp_out, 1)

        def act_std(act, which, half):
            act.wait_ge(var_ready, 2 * which + half)
            tiles = tok_rstd[:, half * NT // 2:(half + 1) * NT // 2]
            nc.scalar.sqrt(tiles, tiles).then_inc(std_ready, 1)

        def act_shared(act, L, s):
            ic = s % L.IC
            act.wait_ge(L.sh_a_ps, s + 1)
            if s >= 2:
                act.wait_ge(L.sh_h_ready, s - 1)
            if L.l == 0:
                ins = nc.scalar.activation(g_sh[s % 2][:], bank[:, 4 + s % 2, :], ACT.Gelu,
                                           bias=b13[:, 0, ic:ic + 1])
            else:
                ins = nc.scalar.activation(g_sh[s % 2][:], bank[:, 4 + s % 2, :], ACT.Silu)
            ins.then_inc(L.sh_g_ready, 1)

        def act_rows(act, L, b):
            act.wait_ge(L.rows_t_ps, b + 1)
            nc.scalar.copy(rows_t[0:CH], bank[0:CH, 0, 0:NCH * P].rearrange("p (k t) -> p k t", k=NCH)
                           ).then_inc(L.rows_t_ready, 1)

        def act_block(act, L, b):
            act.wait_ge(L.first_ps, b + 1)
            if L.l == 0:
                nc.scalar.activation(act_h[:], bank[:, 5, :], ACT.Gelu).then_inc(L.hid_ready, 1)
            else:
                if not isinstance(b, int) or b > 0:
                    act.wait_ge(L.hid_ready, b)
                nc.scalar.activation(act_g[:], bank[:, 5, 0:I1], ACT.Silu).then_inc(L.gate_act, 1)

        def act_blocks(act, L):
            act_rows(act, L, 0)
            act_block(act, L, 0)
            act_rows(act, L, 1)
            with act.Fori(0, (L.NB - 1) // 2) as i:
                for u in range(2):
                    b = i * 2 + (u + 1)
                    act_block(act, L, b)
                    act_rows(act, L, b + 1)

        @block.scalar
        def _(act):
            act.wait_ge(var_ready, 1)
            nc.scalar.sqrt(grp_rstd[:], grp_rstd[:]).then_inc(std_ready, 1)
            for s in range(2 * L0.IC):
                act_shared(act, L0, s)
                if s == 2:
                    act_norm_transposes(act, 0, range(NT // 2))
                    act.wait_ge(L0.gap_ready, 1)
                    nc.scalar.activation(gap_e[:], gap[:], ACT.Exp).then_inc(L0.gap_exp, 1)
            act.wait_ge(s_qkvw, 32)
            nc.scalar.copy(w_high, wqkv).then_inc(w_high_ready, 1)
            act_blocks(act, L0)

            act_std(act, 1, 0)
            act_std(act, 1, 1)
            act_norm_transposes(act, 1, (0, 1))
            for n in range(2 * QKC):
                c, half = n % QKC, n // QKC
                if n == SECOND_HALF:
                    act_norm_transposes(act, 1, (2, 3))
                act.wait_ge(qk_ps, n + 1)
                if c < HC:
                    if n >= 2:
                        act.wait_ge(parts_ready, n - 1)
                    ins = nc.scalar.copy(q_high[n % 2][:].bitcast(F32R), bank[:, n % 6, :])
                else:
                    ins = nc.scalar.mul(k_high[:, c - HC, half * HALF:(half + 1) * HALF], bank[:, n % 6, :],
                                        D ** -0.5)
                ins.then_inc(high_ready, 1)

            def exp_scores(n):
                act.wait_ge(nmax_ready, n + 1)
                if n >= 3:
                    act.wait_ge(att_ready, n - 2)
                for qt in range(2):
                    nc.scalar.activation(e1[n % 3][:, qt, :], bank[:, n % 4, qt * 256:(qt + 1) * 256], ACT.Exp,
                                         bias=neg_max[:, n % 4, qt:qt + 1],
                                         accum_out=exp_sum[:, n % 4, qt:qt + 1]).then_inc(e1_ready, 1)

            def exp_att(n):
                act.wait_ge(att_t_ps, n + 1)
                if n >= 3:
                    act.wait_ge(av_ps, n - 2)
                nc.scalar.activation(p2_t[n % 3][:].rearrange("p a b -> p (a b)"), bank[:, 4 + n % 2, :],
                                     ACT.Exp).then_inc(p2_ready, 1)

            def out_copy(c):
                act.wait_ge(av_ps, HPC * (c + 1))
                if c >= 2:
                    act.wait_ge(o_ready, c - 1)
                nc.scalar.copy(o_raw[:, c % 2, :], bank[:, 6, 0:TOKENS_IMG]).then_inc(o_raw_ready, 1)

            act.wait_ge(v_ps, NT // 2)
            for n in range(N_HEADS + 3):
                if n < N_HEADS:
                    exp_scores(n)
                if 0 <= n - 2 < N_HEADS:
                    exp_att(n - 2)
                if chunk_at(n, 3) is not None:
                    out_copy(chunk_at(n, 3))

            act_std(act, 2, 0)
            act_norm_transposes(act, 2, (0, 1))
            act_std(act, 2, 1)
            act_shared(act, L1, 0)
            act_norm_transposes(act, 2, (2, 3))
            for s in range(1, 2 * L1.IC):
                act_shared(act, L1, s)
                if s == 1:
                    act.wait_ge(L1.gap_ready, 1)
                    nc.scalar.activation(gap_e[:], gap[:], ACT.Exp).then_inc(L1.gap_exp, 1)
            act_blocks(act, L1)

        @block.vector
        def _(dve):
            v = nc.vector
            step, join, go = chained(dve, dve_c)

            for k in range(NCH):
                dve.wait_ge(s_x[k], 16)
                for img in range(IMAGES):
                    step(v.bn_stats(chan_stats[:, k * IMAGES + img, :],
                                    x_t[:, k, img * TOKENS_IMG:(img + 1) * TOKENS_IMG]))
            join()
            for n in range(NCH * IMAGES):
                v.bn_aggr(chan_mv[:, n, :], chan_stats[:, n, :]).then_inc(chan_ready, 1)
            dve.wait_ge(gmean_ps, 1)
            go(v.tensor_copy(grp_mean[:], bank[0:CH, 0, 0:NCH * IMAGES]))
            go(v.tensor_tensor(chan_dev[:], chan_mv[:, :, 0], grp_mean[:], ALU.subtract))
            go(v.tensor_tensor(chan_dev[:], chan_dev[:], chan_dev[:], ALU.mult))
            v.tensor_tensor(chan_dev[:], chan_dev[:], chan_mv[:, :, 1], ALU.add).then_inc(dev_ready, 1)
            dve.wait_ge(gvar_ps, 1)
            v.tensor_scalar(grp_rstd[:], bank[0:CH, 0, 64:64 + NCH * IMAGES], 1e-5, None, ALU.add
                            ).then_inc(var_ready, 1)
            dve.wait_ge(std_ready, 1)
            go(v.reciprocal(grp_rstd[:], grp_rstd[:]))
            for img in range(IMAGES):
                for k in range(NCH):
                    n = k * IMAGES + img
                    span = slice(img * TOKENS_IMG, (img + 1) * TOKENS_IMG)
                    v.tensor_scalar(xn_t[0:CH, k, span], x_t[:, k, span], grp_mean[:, n:n + 1],
                                    grp_rstd[:, n:n + 1], ALU.subtract, ALU.mult).then_inc(xn_t_ready, 1)

            def route(L, stage):
                E, NBP = L.E, L.NB + 1
                if stage == "top2":
                    dve.wait_ge(L.logits_ps, 2)
                    lg = logit[:, :, 0:E]
                    go(v.tensor_copy(lg, bank[:, 3, 0:NT * E].rearrange("p (j e) -> p j e", e=E)))
                    for j in range(NT):
                        step(v.max(top8[:, j, :], logit[:, j, 0:E]))
                    join()
                    for j in range(NT):
                        step(v.max_index(top8i[:, j, :], top8[:, j, :], logit[:, j, 0:E]))
                    v.tensor_tensor(gap[:], top8[:, :, 1], top8[:, :, 0], ALU.subtract).then_inc(L.gap_ready, 1)
                    join()
                    go(v.tensor_copy(choice[:], top8i[:, :, 0:TOPK]))
                    dve.wait_ge(s_tables, 16)
                    iota_e = bc(iota[:, 0:E], 1, [P, NT, E])
                    for k in range(TOPK):
                        step(v.tensor_tensor(picked[:, k, :, 0:E], iota_e,
                                             bc(choice[:, :, k], 2, [P, NT, E]), ALU.is_equal))
                    join()
                    go(v.tensor_tensor(at_pick[:, :, 0:E], picked[:, 0, :, 0:E], picked[:, 1, :, 0:E], ALU.add))
                    dve.wait_ge(filled, 1)
                    for j in range(NT):
                        ins = v.tensor_tensor(before[:, j + 1, 0:E], before[:, j, 0:E], at_pick[:, j, 0:E], ALU.add)
                        if j < NT - 1:
                            go(ins)
                    ins.then_inc(L.prefix_ready, 1)
                    dve.wait_ge(L.gap_exp, 1)
                    go(v.tensor_scalar(gap_1[:], gap_e[:], 1.0, None, ALU.add))
                    go(v.reciprocal(weight[:, 0, :], gap_1[:]))
                    go(v.tensor_tensor(weight[:, 1, :], gap_e[:], weight[:, 0, :], ALU.mult))
                    if L.l == 0:
                        w = [bc(weight[:, k, :], 2, [P, NT, E]) for k in range(TOPK)]
                        go(v.tensor_tensor(comb_a[:], picked[:, 0, :, 0:E], w[0], ALU.mult))
                        go(v.tensor_tensor(comb[:, :, 0:E], picked[:, 1, :, 0:E], w[1], ALU.mult))
                        v.tensor_tensor(comb[:, :, 0:E], comb[:, :, 0:E], comb_a[:], ALU.add
                                        ).then_inc(L.comb_ready, 1)
                elif stage == "pads":
                    dve.wait_ge(L.count_ps, 1)
                    go(v.tensor_scalar(count_i[0:E], bank[0:E, 3, 256:257], float(P - 1), None, ALU.add))
                    go(v.tensor_scalar(count_i2[0:E], count_i[0:E], 7, 7, ALU.arith_shift_right,
                                       ALU.arith_shift_left))
                    go(v.tensor_copy(padded[0:E], count_i2[0:E]))
                    v.tensor_scalar(padded_b[0:E], ones[0:E, :], padded[0:E, 0:1], None, ALU.mult
                                    ).then_inc(L.pads_ready, 1)
                elif stage == "ended":
                    dve.wait_ge(L.rank_ps, 1)
                    go(v.tensor_copy(padded[0:E], bank[0:E, 3, 260:261]))
                    v.tensor_scalar(ended[0:E, 0:NBP], blk_start[0:E, 0:NBP], padded[0:E, 0:1], None,
                                    ALU.is_ge).then_inc(L.ended_ready, 1)
                    rank = bank[:, 7, 0:NT * E].rearrange("p (j e) -> p j e", e=E)
                    for k in range(TOPK):
                        go(v.tensor_tensor(at_pick[:, :, 0:E], picked[:, k, :, 0:E], rank, ALU.mult))
                        go(v.tensor_reduce(slot[:, k, :], at_pick[:, :, 0:E], AXX, ALU.add))
                    go(v.tensor_copy(slot_i[:], slot[:].rearrange("p k j -> p (k j)")))
                    step(v.tensor_scalar(slot_j[:, 0, :], slot_i[:], P - 1, None, ALU.bitwise_and))
                    step(v.tensor_scalar(slot_j[:, 1, :], slot_i[:], 7, None, ALU.arith_shift_right))
                    join()
                    go(v.tensor_copy(slot_f[:], slot_j[:]))
                elif stage == "expert":
                    dve.wait_ge(L.expert_ps, 1)
                    for g, size in enumerate(L.sizes):
                        v.tensor_scalar(blk_weights[:, g, 0:NBP], bank[0:1, 3, 264:264 + NBP], float(E - 1),
                                        float(size), ALU.min, ALU.mult).then_inc(L.expert_ready, 1)
                elif stage == "blocks":
                    n = TOPK * NT
                    go(v.tensor_tensor(eq_blk[:, :, 0:NBP], bc(iota[:, 0:NBP], 1, [P, n, NBP]),
                                       bc(slot_f[:, 1, :], 2, [P, n, NBP]), ALU.is_equal))
                    go(v.tensor_copy(weight_high[:].bitcast(F32R), weight[:]))
                    go(v.tensor_tensor(weight_low[:], weight[:], weight_high[:], ALU.subtract))
                    for k in range(TOPK):
                        s = slice(k * NT, (k + 1) * NT)
                        for part, value in enumerate((tok1, weight_high[:, k, :], weight_low[:, k, :])):
                            v.tensor_tensor(in_blk[:, s, part, 0:NBP], eq_blk[:, s, 0:NBP],
                                            bc(value, 2, [P, NT, NBP]), ALU.mult).then_inc(L.in_blk_ready, 1)
                elif stage == "places":
                    n = TOPK * NT
                    for m in range(n):
                        v.tensor_scalar(at_place[:, m, :], iota, slot_f[:, 0, m:m + 1], None, ALU.is_equal
                                        ).then_inc(L.at_place_ready, 1)
                elif stage == "slots":
                    dve.wait_ge(L.slots_ps, 1)
                    sm = bank[:, 6, 0:3 * NBP].rearrange("p (w b) -> p w b", w=3)
                    go(v.tensor_scalar(empty[:, 0:NBP], sm[:, 0], 0.0, float(OUT_OF_BOUNDS), ALU.is_equal, ALU.mult))
                    go(v.tensor_copy(slot_w[:, 0:NBP], sm[:, 1]))
                    step(v.tensor_tensor(slot_w[:, 0:NBP], slot_w[:, 0:NBP], sm[:, 2], ALU.add))
                    step(v.scalar_tensor_tensor(slot_tok[:, 0:NBP], sm[:, 0], -1.0, empty[:, 0:NBP],
                                                ALU.add, ALU.add))
                    join()
                    dve.sem_inc(L.slots_ready, 1)
                elif stage == "comb":
                    for half in range(2):
                        dve.wait_ge(L.comb_ps, half + 1)
                        v.tensor_copy(comb_t[:, half * HALF:(half + 1) * HALF], bank[0:E0 + 1, 7 * half, :]
                                      ).then_inc(L.comb_out, 1)

            def shared(L, s):
                half, ic = s // L.IC, s % L.IC
                dve.wait_ge(L.sh_c_ps, s + 1)
                dve.wait_ge(L.sh_g_ready, s + 1)
                if L.l and half:
                    dve.wait_ge(xn_stored, 32)
                    dve.wait_ge(tp_ps, NT // 2 * 3)
                dst = L.hid[half][:, ic, :]
                if L.l == 0:
                    ins = v.scalar_tensor_tensor(dst, bank[:, 1 + s % 2, :], b13[:, 1, ic:ic + 1],
                                                 g_sh[s % 2][:], ALU.add, ALU.mult)
                else:
                    ins = v.tensor_tensor(dst, bank[:, 1 + s % 2, :], g_sh[s % 2][:], ALU.mult)
                ins.then_inc(L.sh_h_ready, 1)

            def shared_out(L):
                if L.l == 0:
                    dve.wait_ge(x_tok_in, 16)
                for j in range(NT):
                    out_tile(L, j)
                    if L.l == 0 and 2 <= j < 6:
                        dve.wait_ge(w_high_ready, 1)
                        q = slice((j - 2) * qkv_size // 4, (j - 1) * qkv_size // 4)
                        v.tensor_tensor(w_low[:, q], wqkv[:, q], w_high[:, q].bitcast(F32), ALU.subtract
                                        ).then_inc(w_low_ready, 1)

            def out_tile(L, j):
                dve.wait_ge(L.sh_y_ps, j + 1)
                if j >= 2:
                    dve.wait_ge(L.sh_stored[j % 2], 16 * (j // 2))
                v.tensor_tensor(y_sh[j % 2][:], bank[:, out_bank(L, j), 0:C], x_tok[:, j, :], ALU.add
                                ).then_inc(L.sh_y_ready, 1)

            def hid_copy(L, b):
                dve.wait_ge(L.hid_t_ps, b + 1)
                v.tensor_copy(hid_t[:, 0:L.I], bank[:, 7, 0:L.I]).then_inc(L.hid_t_ready, 1)

            def product(L, b):
                dve.wait_ge(L.up_ps, b + 1)
                dve.wait_ge(L.gate_act, b + 1)
                v.tensor_tensor(act_h[:, 0:I1], bank[:, 6, 0:I1], act_g[:], ALU.mult).then_inc(L.hid_ready, 1)

            def result(L, b, u, first=False):
                dve.wait_ge(L.y_ps, b + 1)
                if not first:
                    dve.wait_ge(L.added, (b - 1) * 16)
                v.tensor_scalar(y[u][:], bank[:, 1, 0:C], slot_w[:, bass.ds(b, 1)], None, ALU.mult
                                ).then_inc(L.y_ready, 1)

            def blocks(L):
                if L.l:
                    product(L, 0)
                hid_copy(L, 0)
                if L.l:
                    product(L, 1)
                result(L, 0, 0, True)
                hid_copy(L, 1)
                if L.l:
                    product(L, 2)
                result(L, 1, 1, True)
                with dve.Fori(0, (L.NB - 3) // 2) as i:
                    for u in range(2):
                        b = i * 2 + (u + 3)
                        hid_copy(L, b - 1)
                        if L.l:
                            product(L, b)
                        result(L, b - 1, u)
                hid_copy(L, L.NB - 1)
                result(L, L.NB - 1, (L.NB - 1) % 2)

            def ln_stats(half):
                tiles = range(half * NT // 2, (half + 1) * NT // 2)
                for j in tiles:
                    step(v.bn_stats(tok_stats[:, j, :], x_tok[:, j, :]))
                join()
                for j in tiles:
                    step(v.bn_aggr(tok_mv[:, j, :], tok_stats[:, j, :]))
                join()
                t = slice(tiles[0], tiles[-1] + 1)
                v.tensor_scalar(tok_rstd[:, t], tok_mv[:, t, 1], 1e-5, None, ALU.add).then_inc(var_ready, 1)

            def ln_rows(which, half):
                tiles = range(half * NT // 2, (half + 1) * NT // 2)
                t = slice(tiles[0], tiles[-1] + 1)
                dve.wait_ge(std_ready, 2 * which + half)
                go(v.reciprocal(tok_rstd[:, t], tok_rstd[:, t]))
                for j in tiles:
                    v.tensor_scalar(xn_tok[:, j, :], x_tok[:, j, :], tok_mv[:, j, 0:1], tok_rstd[:, j:j + 1],
                                    ALU.subtract, ALU.mult).then_inc(xn_tok_ready, 1)

            def stage(L, s):
                if isinstance(s, int):
                    shared(L, s)
                elif s[0] == "y":
                    out_tile(L, s[1])
                else:
                    route(L, s)

            for s in plan[0][1]:
                stage(L0, s)
            shared_out(L0)
            blocks(L0)

            for half in range(2):
                dve.wait_ge(sum_ready[half], 16)
                ln_stats(half)
                ln_rows(1, half)
            def xn_low_parts(pairs):
                for n in pairs:
                    dve.wait_ge(tp_out, NT // 2 + n + 1)
                    t = slice(2 * n * P, (2 * n + 2) * P)
                    v.tensor_tensor(xn_low[0:CH, :, t], bank[0:CH, tp_bank(1, n), :].rearrange("p (k t) -> p k t", k=NCH),
                                    xn_high[0:CH, :, t].bitcast(F32), ALU.subtract).then_inc(xn_low_ready, 1)

            xn_low_parts((0, 1))
            for n in range(2 * QKC):
                c, half = n % QKC, n // QKC
                if n == SECOND_HALF:
                    xn_low_parts((2, 3))
                span = slice(half * HALF, (half + 1) * HALF)
                dve.wait_ge(high_ready, n + 1)
                if c < HC:
                    ins = v.scalar_tensor_tensor(q_parts[:, c, span], q_high[n % 2][:], minus_low,
                                                 bank[:, n % 6, :], ALU.mult, ALU.add)
                else:
                    ins = v.scalar_tensor_tensor(k_low[:, c - HC, span], bank[:, n % 6, :], D ** -0.5,
                                                 k_high[:, c - HC, span].bitcast(F32), ALU.mult, ALU.subtract)
                ins.then_inc(parts_ready, 1)
            def neg_maximum(n):
                dve.wait_ge(sc_ps, n + 1)
                v.tensor_reduce(neg_max[:, n % 4, :], bank[:, n % 4, :].rearrange("p (a b) -> p a b", a=2),
                                AXX, ALU.max, negate=True).then_inc(nmax_ready, 1)

            neg_maximum(0)
            neg_maximum(1)
            dve.wait_ge(filled, 1)
            for n in range(NT // 2):
                dve.wait_ge(v_ps, n + 1)
                v.tensor_copy(v_tok[:, 2 * n:2 * n + 2, :, 0:D].rearrange("p j h d -> p (j h) d"),
                              bank[:, 6 + n % 2, 0:2 * C].rearrange("p (m d) -> p m d", d=D)
                              ).then_inc(v_out, 1)

            def attention(n):
                dve.wait_ge(e1_ready, 2 * n + 2)
                if n >= 2:
                    dve.wait_ge(att_t_ps, n - 1)
                go(v.reciprocal(exp_inv[:, n % 2, :], exp_sum[:, n % 4, :]))
                for qt in range(2):
                    ins = v.scalar_tensor_tensor(att[n % 2][:, qt, :], e1[n % 3][:, qt, :], exp_inv[:, n % 2, qt:qt + 1],
                                                 mask, ALU.mult, ALU.mult)
                    if qt == 0:
                        step(ins)
                ins.then_inc(att_ready, 1)

            def invert_sums(c):
                dve.wait_ge(sums_ps, c + 1)
                if c:
                    dve.wait_ge(wide_ready, c)
                v.reciprocal(o_inv[:].rearrange("p a h -> p (a h)"), 
                             bank[:, sums_bank(c), 0:2 * HPC]).then_inc(inv_ready, 1)

            def out_norm(c):
                dve.wait_ge(spread_ps, c + 1)
                if c >= HC:
                    dve.wait_ge(proj_ps, c // HC)
                v.tensor_tensor(o_t[:, c % HC, :], o_raw[:, c % 2, :], bank[:, sums_bank(c), 0:TOKENS_IMG], ALU.mult
                                ).then_inc(o_ready, 1)

            def residual(img):
                dve.wait_ge(proj_ps, img + 1)
                go(v.tensor_tensor(x_tok[:, 2 * img:2 * img + 2, :], x_tok[:, 2 * img:2 * img + 2, :],
                                   bank[:, 7, 0:2 * C].rearrange("p (j c) -> p j c", c=C), ALU.add))
                dve.sem_inc(x_new, 1)

            for n in range(ATT_STEPS):
                if 2 <= n < N_HEADS:
                    neg_maximum(n)
                if 0 <= n - 1 < N_HEADS:
                    attention(n - 1)
                if n == N_HEADS:
                    ln_stats(0)
                if chunk_at(n, SUMS) is not None:
                    invert_sums(chunk_at(n, SUMS))
                if n == ATT_STEPS - 1:
                    ln_rows(2, 0)
                if chunk_at(n, SUMS + 2) is not None:
                    out_norm(chunk_at(n, SUMS + 2))
                if (chunk_at(n, SUMS + 3) or 0) % HC == HC - 1:
                    residual(chunk_at(n, SUMS + 3) // HC)
            ln_stats(1)
            ln_rows(2, 1)
            shared(L1, 0)
            shared(L1, 1)
            for s in plan[1][1]:
                stage(L1, s)
            blocks(L1)

        @block.tensor
        def _(pe):
            def tile(j):
                return slice(j * P, (j + 1) * P)

            def route(L, stage):
                E, NBP = L.E, L.NB + 1
                if stage == "count":
                    pe.wait_ge(L.prefix_ready, 1)
                    pe.matmul(bank[0:E, 3, 256:257], before[:, NT, 0:E], ones[:, 0:1],
                              start=True, stop=True).then_inc(L.count_ps, 1)
                elif stage == "rank":
                    pe.wait_ge(L.pads_ready, 1)
                    pe.wait_ge(s_tables, 16)
                    pe.wait_ge(tp_out, NT // 2)
                    dst = bank[:, 7, 0:NT * E].rearrange("p (j e) -> p j e", e=E)
                    subt = const[0:E, C_SUBT:C_SUBT + NT * E1].rearrange("p (j e) -> p j e", e=E1)[:, :, 0:E]
                    pe.matmul(dst, tri, at_pick[:, :, 0:E], start=True, stop=False)
                    pe.matmul(dst, ones[:], before[:, 0:NT, 0:E], start=False, stop=False)
                    pe.matmul(dst, padded_b[0:E, :], subt, start=False, stop=True)
                    pe.matmul(bank[0:E, 3, 260:261], subt[:, 0, :], padded[0:E, :], start=True, stop=False)
                    pe.matmul(bank[0:E, 3, 260:261], ident[0:E, 0:E], padded[0:E, :], start=False, stop=True
                              ).then_inc(L.rank_ps, 1)
                elif stage == "expert":
                    pe.wait_ge(L.ended_ready, 1)
                    pe.matmul(bank[0:1, 3, 264:264 + NBP], ones[0:E, 0:1], ended[0:E, 0:NBP],
                              start=True, stop=True).then_inc(L.expert_ps, 1)
                elif stage == "slots":
                    n = TOPK * NT
                    pe.wait_ge(L.in_blk_ready, 3 * TOPK)
                    pe.wait_ge(L.at_place_ready, n)
                    if L.l:
                        pe.wait_ge(L.sh_y_ready, NT // 2)
                    dst = bank[:, 6, 0:3 * NBP].rearrange("p (w b) -> p w b", w=3)
                    for m in range(n):
                        ins = pe.matmul(dst, at_place[:, m, :], in_blk[:, m, :, 0:NBP],
                                        start=(m == 0), stop=(m == n - 1))
                    ins.then_inc(L.slots_ps, 1)
                elif stage == "comb":
                    pe.wait_ge(L.comb_ready, 1)
                    for half in range(2):
                        for j in range(NT // 2):
                            ins = pe.transpose(bank[0:E0 + 1, 7 * half, tile(j)],
                                               comb[:, half * NT // 2 + j, :], ident)
                        ins.then_inc(L.comb_ps, 1)

            def logits(L, j):
                rows_k = CH + 1 if L.l else CH
                for k in range(NCH):
                    kr = rows_k if k == 1 else CH
                    ins = pe.matmul(bank[:, 3, j * L.E:(j + 1) * L.E], xn_t[0:kr, k, tile(j)],
                                    gate_w[L.l][0:kr, k, :], start=(k == 0), stop=(k == NCH - 1))
                if j % (NT // 2) == NT // 2 - 1:
                    ins.then_inc(L.logits_ps, 1)

            def shared(L, s, gate_half=None):
                if gate_half is not None:
                    pe.wait_ge(s_gate0 if L.l == 0 else s_gate1, 16 if L.l == 0 else 32)
                half, ic = s // L.IC, s % L.IC
                w = w13 if L.l == 0 else sh1
                for g, (bk, done) in enumerate(((4, L.sh_a_ps), (1, L.sh_c_ps))):
                    if s >= 2:
                        pe.wait_ge(L.sh_g_ready if g == 0 else L.sh_h_ready, s - 1)
                    for k in range(NCH):
                        ins = pe.matmul(bank[:, bk + s % 2, :], w[:, k, g, ic * P:(ic + 1) * P],
                                        xn_t[0:CH, k, half * HALF:(half + 1) * HALF],
                                        start=(k == 0), stop=(k == NCH - 1))
                    ins.then_inc(done, 1)
                    if gate_half is not None:
                        for j in range(2):
                            logits(L, gate_half * NT // 2 + g * 2 + j)

            def shared_out(L):
                for j in range(NT):
                    out_tile(L, j)

            def out_tile(L, j):
                w = w2 if L.l == 0 else sh1d[:]
                half = j // (NT // 2)
                if j == NT - 1:
                    rows_transpose(L, 0, 0, 0)
                if L.l == 0 and j == 0:
                    pe.wait_ge(L.sh_g_ready, 2 * L.IC)
                pe.wait_ge(L.sh_h_ready, (half + 1) * L.IC)
                if j >= 2:
                    pe.wait_ge(L.sh_y_ready, j - 1)
                dst = bank[:, out_bank(L, j), 0:C]
                if L.l == 0:
                    pe.wait_ge(L.comb_out, 2)
                    pe.matmul(dst, comb_t[:, tile(j)], b2[:], start=True, stop=False)
                for ic in range(L.IC):
                    ins = pe.matmul(dst, L.hid[half][:, ic, tile(j % (NT // 2))], w[:, ic, :],
                                    start=(L.l == 1 and ic == 0), stop=(ic == L.IC - 1))
                ins.then_inc(L.sh_y_ps, 1)

            def rows_transpose(L, b, u, n):
                pe.wait_ge(L.rows_in[u], (n + 1) * 16)
                for k in range(NCH):
                    ins = pe.transpose(bank[0:CH, 0, tile(k)], rows[u][:, k * CH:(k + 1) * CH], ident)
                ins.then_inc(L.rows_t_ps, 1)

            def weights(L, b, g):
                tensor, size = (w_first, w_second)[g], L.sizes[g]
                start = pe.value_load(blk_weights[0:1, g, bass.ds(b, 1)], min_val=0, max_val=(L.E - 1) * size)

                def part(rows, o, n):
                    return tensor[0:rows, o:o + (L.E - 1) * size + n][:, bass.ds(start, n)]
                return part

            def first(L, b, w):
                pe.wait_ge(L.rows_t_ready, b + 1)
                if L.l == 0:
                    for k in range(NCH):
                        kr = CH + k
                        ins = pe.matmul(bank[:, 5, :], rows_t[0:kr, k, :], w(kr, k * I0, I0),
                                        start=(k == 0), stop=(k == NCH - 1))
                    ins.then_inc(L.first_ps, 1)
                else:
                    for g, done in enumerate((L.first_ps, L.up_ps)):
                        for k in range(NCH):
                            ins = pe.matmul(bank[:, 5 + g, 0:I1], rows_t[0:CH, k, :], w(CH, (k * 2 + g) * I1, I1),
                                            start=(k == 0), stop=(k == NCH - 1))
                        ins.then_inc(done, 1)

            def hid_transpose(L, b):
                pe.wait_ge(L.hid_ready, b + 1)
                for ic in range(L.IC):
                    ins = pe.transpose(bank[:, 7, tile(ic)], act_h[:, tile(ic)], ident)
                ins.then_inc(L.hid_t_ps, 1)

            def second(L, b, w, first_block=False):
                pe.wait_ge(L.hid_t_ready, b + 1)
                if not first_block:
                    pe.wait_ge(L.y_ready, b)
                for ic in range(L.IC):
                    ins = pe.matmul(bank[:, 1, 0:C], hid_t[:, tile(ic)],
                                    w(P, ic * C, C),
                                    start=(ic == 0), stop=(ic == L.IC - 1))
                ins.then_inc(L.y_ps, 1)

            def blocks(L):
                pe.wait_ge(L.expert_ready, 2)
                pe.wait_ge(L.sh_y_ready, NT - 1)
                if L.l == 0:
                    pe.wait_ge(s_fc1, 32)
                    pe.wait_ge(s_fc2, 16)
                else:
                    pe.wait_ge(s_w1a, 16 * E1)
                    pe.wait_ge(s_w1b, 16)
                first(L, 0, weights(L, 0, 0))
                rows_transpose(L, 1, 1, 0)
                hid_transpose(L, 0)
                first(L, 1, weights(L, 1, 0))
                rows_transpose(L, 2, 0, 1)
                second(L, 0, weights(L, 0, 1), True)
                hid_transpose(L, 1)
                first(L, 2, weights(L, 2, 0))
                rows_transpose(L, 3, 1, 1)
                second(L, 1, weights(L, 1, 1))
                with pe.Fori(0, (L.NB - 3) // 2) as i:
                    w1 = weights(L, i * 2 + 3, 0)
                    for u in range(2):
                        b = i * 2 + (u + 3)
                        hid_transpose(L, b - 1)
                        first(L, b, w1)
                        w2 = weights(L, b - 1, 1)
                        rows_transpose(L, b + 1, u, i + 2)
                        if u == 0:
                            w1 = weights(L, b + 1, 0)
                        second(L, b - 1, w2)
                hid_transpose(L, L.NB - 1)
                second(L, L.NB - 1, weights(L, L.NB - 1, 1))

            pe.wait_ge(s_const, 16)
            pe.wait_ge(chan_ready, NCH * IMAGES)
            pe.matmul(bank[0:CH, 0, 0:NCH * IMAGES], gavg, chan_mv[:, :, 0], start=True, stop=True
                      ).then_inc(gmean_ps, 1)
            pe.wait_ge(dev_ready, 1)
            pe.matmul(bank[0:CH, 0, 64:64 + NCH * IMAGES], gavg, chan_dev[:], start=True, stop=True
                      ).then_inc(gvar_ps, 1)
            pe.wait_ge(filled, 1)

            def stage(L, s):
                if isinstance(s, int):
                    shared(L, s)
                elif s[0] == "y":
                    out_tile(L, s[1])
                elif s[0] == "shared":
                    shared(L, s[1], s[2])
                elif s == "rows":
                    for n in range(NT // 2):
                        if n >= 2:
                            pe.wait_ge(tp_out, n - 1)
                        for m in range(2):
                            for k in range(NCH):
                                ins = pe.transpose(bank[:, tp_bank(0, n), (m * NCH + k) * CH:(m * NCH + k + 1) * CH],
                                                   xn_t[0:CH, k, tile(2 * n + m)], ident[0:CH, 0:CH])
                        ins.then_inc(tp_ps, 1)
                else:
                    route(L, s)

            pe.wait_ge(xn_t_ready, NCH * IMAGES)
            for s in plan[0][0]:
                if s == 0:
                    pe.wait_ge(s_w13, 32)
                stage(L0, s)
            pe.wait_ge(s_sh0, 48)
            shared_out(L0)
            blocks(L0)

            def norm_transposes(which, half):
                for n in (2 * half, 2 * half + 1):
                    pe.wait_ge(xn_tok_ready, (which - 1) * NT + 2 * (n + 1))
                    for k in range(NCH):
                        for m in range(2):
                            ins = pe.transpose(bank[0:CH, tp_bank(which, n), (k * 2 + m) * P:(k * 2 + m + 1) * P],
                                               xn_tok[:, 2 * n + m, k * CH:(k + 1) * CH], ident)
                    ins.then_inc(tp_ps, 1)

            norm_transposes(1, 0)
            pe.wait_ge(xn_low_ready, 2)
            pe.wait_ge(w_low_ready, 4)
            for n in range(2 * QKC):
                c, half = n % QKC, n // QKC
                if n == SECOND_HALF:
                    norm_transposes(1, 1)
                    pe.wait_ge(xn_low_ready, 4)
                if n >= 6:
                    pe.wait_ge(parts_ready, n - 5)
                for k in range(NCH):
                    w, x = w_parts(k, c, P), [a[0:CH, k, half * HALF:(half + 1) * HALF] for a in (xn_high, xn_low)]
                    for g, h in PASSES:
                        ins = pe.matmul(bank[:, n % 6, :], w[g], x[h], start=(k == 0 and (g, h) == PASSES[0]),
                                        stop=(k == NCH - 1 and (g, h) == PASSES[-1]))
                ins.then_inc(qk_ps, 1)
            def scores(n):
                pair, img = (n, n + 1), n // HEADS
                if n >= 4:
                    pe.wait_ge(e1_ready, 2 * (n - 2))
                for qt in range(2):
                    q0 = img * TOKENS_IMG + qt * P
                    for part in (k_high, k_low):
                        for m in pair:
                            h = m % HEADS
                            r = slice(HG * (h % HPC), HG * (h % HPC + 1))
                            ins = pe.matmul(bank[:, m % 4, qt * 256:(qt + 1) * 256], q_parts[r, h // HPC, q0:q0 + P],
                                            part[r, h // HPC, img * TOKENS_IMG:(img + 1) * TOKENS_IMG],
                                            start=(part is k_high), stop=(part is k_low))
                            if qt == 1 and part is k_low:
                                ins.then_inc(sc_ps, 1)

            pe.wait_ge(parts_ready, 2 * QKC)
            scores(0)
            for n in range(NT // 2):
                if n >= 2:
                    pe.wait_ge(v_out, n - 1)
                for m in range(2):
                    for k in range(NCH):
                        w, x = w_parts(k, None, C), [a[0:CH, k, tile(2 * n + m)] for a in (xn_high, xn_low)]
                        for g, h in PASSES:
                            ins = pe.matmul(bank[:, 6 + n % 2, m * C:(m + 1) * C], x[h], w[g],
                                            start=(k == 0 and (g, h) == PASSES[0]),
                                            stop=(k == NCH - 1 and (g, h) == PASSES[-1]))
                ins.then_inc(v_ps, 1)
            pe.wait_ge(v_out, NT // 2)

            def att_transpose(n):
                pe.wait_ge(att_ready, n + 1)
                if n >= 2:
                    pe.wait_ge(p2_ready, n - 1)
                for kt in range(2):
                    for qt in range(2):
                        dst = bank[:, 4 + n % 2, (kt * 2 + qt) * P:(kt * 2 + qt + 1) * P]
                        src = att[n % 2][:, qt, tile(kt)]
                        if kt == qt:
                            ins = pe.matmul(dst, src, ident, start=True, stop=True)
                        else:
                            ins = pe.transpose(dst, src, ident)
                ins.then_inc(att_t_ps, 1)

            def weigh_values(n):
                img, h = n // HEADS, n % HEADS
                g, c = n % HPC, n // HPC
                pe.wait_ge(p2_ready, n + 1)
                if g == 0 and c:
                    pe.wait_ge(o_raw_ready, c)
                for kt in range(2):
                    ins = pe.matmul(bank[g * HG:(g + 1) * HG, 6, 0:TOKENS_IMG],
                                    v_tok[:, 2 * img + kt, h, :], p2_t[n % 3][:, kt, :],
                                    start=(kt == 0), stop=(kt == 1))
                ins.then_inc(av_ps, 1)

            def sums_by_token(c):
                pe.wait_ge(o_raw_ready, c + 1)
                if sums_bank(c) == 0:
                    pe.wait_ge(e1_ready, 2 * N_HEADS)
                elif c and c % HC == 0:
                    pe.wait_ge(x_new, c // HC)
                elif c:
                    pe.wait_ge(o_ready, c)
                for qt in range(2):
                    o = qt * HPC
                    ins = pe.matmul(bank[:, sums_bank(c), o:o + HPC], o_raw[:, c % 2, tile(qt)], sum_row,
                                    start=True, stop=True)
                ins.then_inc(sums_ps, 1)

            def spread_inverses(c):
                pe.wait_ge(wide_ready, c + 1)
                for qt in range(2):
                    ins = pe.transpose(bank[:, sums_bank(c), tile(qt)], o_inv_wide[:, qt].rearrange("p g d -> p (g d)"), ident)
                ins.then_inc(spread_ps, 1)

            def project(img):
                pe.wait_ge(o_ready, HC * (img + 1))
                if img == 0:
                    pe.wait_ge(s_attw, 16)
                for qt in range(2):
                    for k in range(HC):
                        ins = pe.matmul(bank[:, 7, qt * C:(qt + 1) * C], o_t[:, k, tile(qt)], wo[:, k, :],
                                        start=(k == 0), stop=(k == HC - 1))
                ins.then_inc(proj_ps, 1)

            for n in range(ATT_STEPS):
                if n % 2 and n + 1 < N_HEADS:
                    scores(n + 1)
                if 0 <= n - 2 < N_HEADS:
                    att_transpose(n - 2)
                if 0 <= n - 3 < N_HEADS:
                    weigh_values(n - 3)
                if chunk_at(n, SUMS) is not None:
                    sums_by_token(chunk_at(n, SUMS))
                if chunk_at(n, SUMS + 2) is not None:
                    spread_inverses(chunk_at(n, SUMS + 2))
                if (chunk_at(n, SUMS + 3) or 0) % HC == HC - 1:
                    project(chunk_at(n, SUMS + 3) // HC)

            pe.wait_ge(p2_ready, N_HEADS)
            norm_transposes(2, 0)
            pe.wait_ge(tp_out, NT + 2)
            pe.wait_ge(s_sh1, 32)
            shared(L1, 0, 0)
            pe.wait_ge(x_new, IMAGES)
            norm_transposes(2, 1)
            pe.wait_ge(tp_out, NT // 2 * 3)
            shared(L1, 1, 1)
            for s in plan[1][0]:
                stage(L1, s)
            blocks(L1)


_OUT = ((4, 16, 16, C), "float32")


def kernel(**inputs):
    import concourse.bacc as bacc
    from concourse.bass_utils import run_bass_kernel_spmd

    a = {k: np.asarray(v) for k, v in inputs.items()}

    def chunks(w):
        return w.reshape(NCH, CH, -1).transpose(1, 0, 2)

    x = a["x"].reshape(T, C)
    qkv = a["L1_attn_w_qkv"].reshape(3, HEADS, D, C)
    qk = np.stack([qkv[0:2], qkv[0:2]], 2)
    wo = np.zeros((HC, HPC, HG, C), np.float32)
    wo[:, :, 0:D] = a["L1_attn_w_out"].T.reshape(HC, HPC, D, C)
    wo[0, 0, D] = a["L1_attn_b_out"]
    arrays = {
        "x": x,
        "x_t": chunks(x.T),
        "const": constants(),
        "gate0": chunks(a["L0_conv_gate_w"].T),
        "w13": np.stack([chunks(a["L0_conv_w1_w"].T), chunks(a["L0_conv_w3_w"].T)], 2),
        "b13": np.stack([a["L0_conv_w1_b"].reshape(-1, P).T, a["L0_conv_w3_b"].reshape(-1, P).T], 1),
        "w2": a["L0_conv_w2_w"].T.reshape(I0 // P, P, C).transpose(1, 0, 2),
        "fc2_b": a["L0_conv_fc2_b"],
        "w2_b": a["L0_conv_w2_b"].reshape(1, C),
        "fc1": a["L0_conv_fc1_w"].transpose(2, 0, 1).reshape(NCH, CH, E0, I0).transpose(1, 2, 0, 3),
        "fc1_b": a["L0_conv_fc1_b"].reshape(1, E0, I0),
        "fc2": a["L0_conv_fc2_w"].transpose(2, 0, 1).reshape(I0 // P, P, E0, C).transpose(1, 2, 0, 3)
        .reshape(P, -1),
        "wqk": chunks(qk.reshape(-1, C).T).reshape(CH, NCH, QKC, P),
        "wv": chunks(a["L1_attn_w_qkv"][2 * C:].T),
        "wo": wo.reshape(HC, P, C).transpose(1, 0, 2),
        "gate1": chunks(a["L1_ffn_w_gate"]),
        "bias1": a["L1_ffn_expert_bias"].reshape(1, E1),
        "gate_up": np.stack([a["L1_ffn_wg"], a["L1_ffn_wu"]], 0).reshape(2, E1, NCH, CH, I1)
        .transpose(3, 1, 2, 0, 4),
        "down": a["L1_ffn_wd"].reshape(E1, I1 // P, P, C).transpose(2, 0, 1, 3).reshape(P, -1),
        "sh1": np.stack([chunks(a["L1_ffn_swg"]), chunks(a["L1_ffn_swu"])], 2),
        "sh1d": a["L1_ffn_swd"].reshape(I1 // P, P, C).transpose(1, 0, 2),
    }
    arrays = {k: np.ascontiguousarray(v) for k, v in arrays.items()}
    nc = bacc.Bacc("TRN2", target_bir_lowering=False, num_devices=1)
    d = {k: nc.dram_tensor(f"in_{k}", v.shape, mybir.dt.from_np(v.dtype), kind="ExternalInput").ap()
         for k, v in arrays.items()}
    out = nc.dram_tensor("out_0", (T, C), F32, kind="ExternalOutput").ap()
    build(nc, d, out)
    r = run_bass_kernel_spmd(nc, [{f"in_{k}": v for k, v in arrays.items()}], core_ids=[0])
    return r.results[0]["out_0"].reshape(_OUT[0])
```
